# Optimizing a Trainium2 kernel written in Bass

```python
import numpy as np
import jax
import jax.numpy as jnp

def _softmax(x, axis=-1):
    return jax.nn.softmax(x, axis=axis)

def _gelu(x):
    return jax.nn.gelu(x, approximate=True)

def _silu(x):
    return jax.nn.silu(x)

def _sigmoid(x):
    return jax.nn.sigmoid(x)

def _layernorm(x, axis=-1, eps=1e-05):
    m = jnp.mean(x, axis=axis, keepdims=True)
    v = jnp.var(x, axis=axis, keepdims=True)
    return (x - m) / jnp.sqrt(v + eps)

def _scatter_add(tgt, idx, src, axis=0):
    return tgt.at[idx].add(src)

def _segment_sum(src, seg, n):
    return jax.ops.segment_sum(src, seg, n)
kernel_name = 'mk_flamingo_gated_d2_seqx_r8_5713fe'

def setup_inputs(seed: int=0):
    np.random.seed(seed)
    _w = jnp.asarray

    def _rec_inputs():
        import jax
        import jax.numpy as jnp
        _rk = jax.random.key(seed)
        x = -0.0002928 + 1 * jax.random.normal(jax.random.fold_in(_rk, 1), (4, 512, 128), jnp.float32)
        _lenS = 512 - jax.random.randint(jax.random.fold_in(_rk, 7), (4,), 0, max(1, 512 // 4) + 1, jnp.int32)
        _lenS2 = 77 - jax.random.randint(jax.random.fold_in(_rk, 8), (4,), 0, max(1, 77 // 4) + 1, jnp.int32)
        _ctx_1024P = jax.random.normal(jax.random.fold_in(_rk, 11), (4, 16, 128), jnp.float32)
        _ctx_1024c = jax.random.dirichlet(jax.random.fold_in(_rk, 511), 0.3 * jnp.ones((16,), jnp.float32), (4, 77))
        _ctx_1024t = jnp.einsum('bsk,bkd->bsd', _ctx_1024c, _ctx_1024P)
        _ctx_1024t = _ctx_1024t * jax.lax.rsqrt(jnp.mean(jnp.square(_ctx_1024t)) + 1e-12) * 0.953939
        ctx_1024 = -1.39393e-06 + 0.999914 * (_ctx_1024t + 0.3 * jax.random.normal(jax.random.fold_in(_rk, 611), (4, 77, 128), jnp.float32))
        _validS = jnp.arange(512)[None, :] < _lenS[:, None]
        _validS2 = jnp.arange(77)[None, :] < _lenS2[:, None]
        _causal = jnp.tril(jnp.ones((512, 512), dtype=bool))
        mask_Bx1xSxS2_if1 = jnp.where(jnp.ones((4, 1, 512, 77), dtype=bool), 1, 0).astype(jnp.int32)
        mask_1x1xSxS2_if1 = jnp.where(jnp.ones((1, 1, 512, 77), dtype=bool), 1, 0).astype(jnp.int32)
        _g = jax.random.normal(jax.random.fold_in(_rk, 9001), (2, 2), jnp.float32)
        _g = jnp.sign(_g) * jnp.maximum(jnp.abs(_g), 1.0) + (_g == 0) * 1.0
        g_xattn = _g[0]
        g_ffn = _g[1]
        return (x, ctx_1024, mask_Bx1xSxS2_if1, mask_1x1xSxS2_if1, g_xattn, g_ffn)
    x, ctx_1024, mask_Bx1xSxS2_if1, mask_1x1xSxS2_if1, g_xattn, g_ffn = _rec_inputs()

    def _L0_xattn_setup():
        import jax, jax.numpy as jnp
        import numpy as np
        B, S, H, NH = (2, 256, 128, 16)
        DK = H // NH

        def _split_heads(x):
            b, s, _ = x.shape
            return x.reshape(b, s, NH, DK).transpose(0, 2, 1, 3)
        key = jax.random.key(seed)
        ks = jax.random.split(key, 10)
        init = lambda k, shape: jax.random.normal(k, shape, dtype=jnp.float32) * 0.02
        return {'query': jax.random.normal(ks[0], (B, S, H), dtype=jnp.float32), 'key': jax.random.normal(ks[1], (B, S, H), dtype=jnp.float32), 'attn_mask': jnp.ones((B, 1, S, S), dtype=jnp.int32), 'Wq': init(ks[2], (H, H)), 'bq': init(ks[3], (H,)), 'Wk': init(ks[4], (H, H)), 'bk': init(ks[5], (H,)), 'Wv': init(ks[6], (H, H)), 'bv': init(ks[7], (H,)), 'Wo': init(ks[8], (H, H)), 'bo': init(ks[9], (H,))}
    _L0_xattn_all = _L0_xattn_setup()
    _L0_xattn_in = {k: v for k, v in _L0_xattn_all.items() if k in ('Wq', 'bq', 'Wk', 'bk', 'Wv', 'bv', 'Wo', 'bo')}
    del _L0_xattn_all

    def _L0_ffn_setup():
        import jax, jax.numpy as jnp
        import numpy as np
        D_MODEL = 128
        HIDDEN = 128
        NUM_EXPERTS = 8
        TOP_K = 2
        key = jax.random.key(seed)
        ks = jax.random.split(key, 10)
        s = 0.02
        return {'x': jax.random.normal(ks[0], (2, 256, D_MODEL), dtype=jnp.float32), 'gate_w': jax.random.normal(ks[1], (NUM_EXPERTS, D_MODEL), dtype=jnp.float32) * s, 'up_w': jax.random.normal(ks[2], (NUM_EXPERTS, D_MODEL, HIDDEN), dtype=jnp.float32) * s, 'up_b': jnp.zeros((NUM_EXPERTS, HIDDEN), dtype=jnp.float32), 'down_w': jax.random.normal(ks[3], (NUM_EXPERTS, HIDDEN, D_MODEL), dtype=jnp.float32) * s, 'down_b': jnp.zeros((NUM_EXPERTS, D_MODEL), dtype=jnp.float32), 'sh_up_w': jax.random.normal(ks[4], (D_MODEL, HIDDEN), dtype=jnp.float32) * s, 'sh_up_b': jnp.zeros((HIDDEN,), dtype=jnp.float32), 'sh_down_w': jax.random.normal(ks[5], (HIDDEN, D_MODEL), dtype=jnp.float32) * s, 'sh_down_b': jnp.zeros((D_MODEL,), dtype=jnp.float32)}
    _L0_ffn_all = _L0_ffn_setup()
    _L0_ffn_in = {k: v for k, v in _L0_ffn_all.items() if k in ('gate_w', 'up_w', 'up_b', 'down_w', 'down_b', 'sh_up_w', 'sh_up_b', 'sh_down_w', 'sh_down_b')}
    del _L0_ffn_all

    def _L1_xattn_setup():
        import jax, jax.numpy as jnp
        import numpy as np
        D_MODEL = 128
        HEAD = 16
        D_K = D_MODEL // HEAD
        NEG = -1000000000.0
        key = jax.random.key(seed)
        ks = jax.random.split(key, 8)
        B, S = (2, 256)
        q = jax.random.normal(ks[0], (B, S, D_MODEL), dtype=jnp.float32)
        k = jax.random.normal(ks[1], (B, S, D_MODEL), dtype=jnp.float32)
        v = jax.random.normal(ks[2], (B, S, D_MODEL), dtype=jnp.float32)
        mask = jnp.ones((1, 1, S, S), dtype=jnp.int32)
        scale = 1.0 / np.sqrt(D_MODEL)
        w_q = jax.random.normal(ks[3], (D_MODEL, D_MODEL), dtype=jnp.float32) * scale
        w_k = jax.random.normal(ks[4], (D_MODEL, D_MODEL), dtype=jnp.float32) * scale
        w_v = jax.random.normal(ks[5], (D_MODEL, D_MODEL), dtype=jnp.float32) * scale
        w_o = jax.random.normal(ks[6], (D_MODEL, D_MODEL), dtype=jnp.float32) * scale
        return {'q': q, 'k': k, 'v': v, 'mask': mask, 'w_q': w_q, 'w_k': w_k, 'w_v': w_v, 'w_o': w_o}
    _L1_xattn_all = _L1_xattn_setup()
    _L1_xattn_in = {k: v for k, v in _L1_xattn_all.items() if k in ('w_q', 'w_k', 'w_v', 'w_o')}
    del _L1_xattn_all

    def _L1_ffn_setup():
        import jax, jax.numpy as jnp
        import numpy as np
        S_LEN, BATCH, HIDDEN = (256, 2, 128)
        N_HEADS, N_KV = (16, 8)
        N_EXP, TOP_K, CAP_F = (8, 2, 1.25)
        FFN = 512
        HEAD_DIM = HIDDEN // N_HEADS
        Q_PER_KV = N_HEADS // N_KV
        EPS = 1e-05
        NEG = -1000000000.0

        def _ln(x, w, b):
            mu = jnp.mean(x, -1, keepdims=True)
            var = jnp.var(x, -1, keepdims=True)
            return (x - mu) * jax.lax.rsqrt(var + EPS) * w + b

        def _forward(hidden_states, ln1_weight, ln1_bias, ln2_weight, ln2_bias, qkv_weight, proj_weight, router_weight, moe_w1, moe_w2):
            S, B, H = hidden_states.shape
            ln1 = _ln(hidden_states, ln1_weight, ln1_bias)
            qkv = (ln1 @ qkv_weight.T).reshape(S, B, N_KV, (Q_PER_KV + 2) * HEAD_DIM)
            q_dim = Q_PER_KV * HEAD_DIM
            q = qkv[..., :q_dim].reshape(S, B, N_HEADS, HEAD_DIM)
            k = jnp.repeat(qkv[..., q_dim:q_dim + HEAD_DIM], Q_PER_KV, axis=2)
            v = jnp.repeat(qkv[..., q_dim + HEAD_DIM:], Q_PER_KV, axis=2)
            scores = jnp.einsum('sbhd,tbhd->bhst', q, k) / jnp.sqrt(jnp.float32(HEAD_DIM))
            causal = jnp.tril(jnp.ones((S, S), bool))
            attn = jax.nn.softmax(jnp.where(causal[None, None], scores, NEG), axis=-1)
            attn_out = jnp.einsum('bhst,tbhd->sbhd', attn, v).reshape(S, B, H)
            hidden_after_attn = hidden_states + attn_out @ proj_weight.T
            x = _ln(hidden_after_attn, ln2_weight, ln2_bias).reshape(-1, H)
            N = S * B
            probs = jax.nn.softmax(x.astype(jnp.float32) @ router_weight, axis=-1)
            top_p, top_i = jax.lax.top_k(probs, TOP_K)
            top_p = top_p / jnp.sum(top_p, -1, keepdims=True)
            flat_exp = top_i.reshape(-1)
            order = jnp.argsort(flat_exp)
            sorted_exp = flat_exp[order]
            counts = jnp.bincount(sorted_exp, length=N_EXP)
            offsets = jnp.concatenate([jnp.zeros((1,), counts.dtype), jnp.cumsum(counts)])
            within = jnp.arange(N * TOP_K) - offsets[sorted_exp]
            cap = int(np.ceil(N * TOP_K / N_EXP * CAP_F))
            keep = within < cap
            slot = jnp.where(keep, sorted_exp * cap + within, N_EXP * cap)
            tok_id = order // TOP_K
            padded_tokens = jnp.zeros((N_EXP * cap + 1, H), x.dtype).at[slot].set(x[tok_id])[:-1]
            padded_probs = jnp.zeros((N_EXP * cap + 1,), jnp.float32).at[slot].set(top_p.reshape(-1)[order])[:-1]
            padded_ids = jnp.zeros((N_EXP * cap + 1,), jnp.int32).at[slot].set(tok_id.astype(jnp.int32))[:-1]
            exp_in = padded_tokens.reshape(N_EXP, cap, H)
            act = jax.nn.gelu(jnp.einsum('ech,ehf->ecf', exp_in, moe_w1), approximate=False)
            exp_out = jnp.einsum('ecf,efh->ech', act, moe_w2).reshape(N_EXP * cap, H)
            weighted = exp_out * padded_probs[:, None].astype(exp_out.dtype)
            moe = jnp.zeros((N, H), exp_out.dtype).at[padded_ids].add(weighted)
            return hidden_after_attn + moe.reshape(S, B, H)
        ks = jax.random.split(jax.random.key(seed), 6)
        qkv_out = N_KV * (Q_PER_KV + 2) * HEAD_DIM
        sc = 0.02
        return {'hidden_states': jax.random.normal(ks[0], (S_LEN, BATCH, HIDDEN), jnp.float32), 'ln1_weight': jnp.ones((HIDDEN,), jnp.float32), 'ln1_bias': jnp.zeros((HIDDEN,), jnp.float32), 'ln2_weight': jnp.ones((HIDDEN,), jnp.float32), 'ln2_bias': jnp.zeros((HIDDEN,), jnp.float32), 'qkv_weight': jax.random.normal(ks[1], (qkv_out, HIDDEN), jnp.float32) * sc, 'proj_weight': jax.random.normal(ks[2], (HIDDEN, HIDDEN), jnp.float32) * sc, 'router_weight': jax.random.normal(ks[3], (HIDDEN, N_EXP), jnp.float32) * sc, 'moe_w1': jax.random.normal(ks[4], (N_EXP, HIDDEN, FFN), jnp.float32) * sc, 'moe_w2': jax.random.normal(ks[5], (N_EXP, FFN, HIDDEN), jnp.float32) * sc}
    _L1_ffn_all = _L1_ffn_setup()
    _L1_ffn_in = {k: v for k, v in _L1_ffn_all.items() if k in ('ln1_weight', 'ln1_bias', 'ln2_weight', 'ln2_bias', 'qkv_weight', 'proj_weight', 'router_weight', 'moe_w1', 'moe_w2')}
    del _L1_ffn_all
    return {'x': x, 'ctx_1024': ctx_1024, 'mask_Bx1xSxS2_if1': mask_Bx1xSxS2_if1, 'mask_1x1xSxS2_if1': mask_1x1xSxS2_if1, 'g_xattn': g_xattn, 'g_ffn': g_ffn, 'L0_xattn_Wq': _L0_xattn_in['Wq'], 'L0_xattn_bq': _L0_xattn_in['bq'], 'L0_xattn_Wk': _L0_xattn_in['Wk'], 'L0_xattn_bk': _L0_xattn_in['bk'], 'L0_xattn_Wv': _L0_xattn_in['Wv'], 'L0_xattn_bv': _L0_xattn_in['bv'], 'L0_xattn_Wo': _L0_xattn_in['Wo'], 'L0_xattn_bo': _L0_xattn_in['bo'], 'L0_ffn_gate_w': _L0_ffn_in['gate_w'], 'L0_ffn_up_w': _L0_ffn_in['up_w'], 'L0_ffn_up_b': _L0_ffn_in['up_b'], 'L0_ffn_down_w': _L0_ffn_in['down_w'], 'L0_ffn_down_b': _L0_ffn_in['down_b'], 'L0_ffn_sh_up_w': _L0_ffn_in['sh_up_w'], 'L0_ffn_sh_up_b': _L0_ffn_in['sh_up_b'], 'L0_ffn_sh_down_w': _L0_ffn_in['sh_down_w'], 'L0_ffn_sh_down_b': _L0_ffn_in['sh_down_b'], 'L1_xattn_w_q': _L1_xattn_in['w_q'], 'L1_xattn_w_k': _L1_xattn_in['w_k'], 'L1_xattn_w_v': _L1_xattn_in['w_v'], 'L1_xattn_w_o': _L1_xattn_in['w_o'], 'L1_ffn_ln1_weight': _L1_ffn_in['ln1_weight'], 'L1_ffn_ln1_bias': _L1_ffn_in['ln1_bias'], 'L1_ffn_ln2_weight': _L1_ffn_in['ln2_weight'], 'L1_ffn_ln2_bias': _L1_ffn_in['ln2_bias'], 'L1_ffn_qkv_weight': _L1_ffn_in['qkv_weight'], 'L1_ffn_proj_weight': _L1_ffn_in['proj_weight'], 'L1_ffn_router_weight': _L1_ffn_in['router_weight'], 'L1_ffn_moe_w1': _L1_ffn_in['moe_w1'], 'L1_ffn_moe_w2': _L1_ffn_in['moe_w2']}

def reference(x, ctx_1024, mask_Bx1xSxS2_if1, mask_1x1xSxS2_if1, g_xattn, g_ffn, L0_xattn_Wq, L0_xattn_bq, L0_xattn_Wk, L0_xattn_bk, L0_xattn_Wv, L0_xattn_bv, L0_xattn_Wo, L0_xattn_bo, L0_ffn_gate_w, L0_ffn_up_w, L0_ffn_up_b, L0_ffn_down_w, L0_ffn_down_b, L0_ffn_sh_up_w, L0_ffn_sh_up_b, L0_ffn_sh_down_w, L0_ffn_sh_down_b, L1_xattn_w_q, L1_xattn_w_k, L1_xattn_w_v, L1_xattn_w_o, L1_ffn_ln1_weight, L1_ffn_ln1_bias, L1_ffn_ln2_weight, L1_ffn_ln2_bias, L1_ffn_qkv_weight, L1_ffn_proj_weight, L1_ffn_router_weight, L1_ffn_moe_w1, L1_ffn_moe_w2):
    import jax
    import jax.numpy as jnp

    def _L0_xattn_ref(query, key, attn_mask, Wq, bq, Wk, bk, Wv, bv, Wo, bo):
        import jax, jax.numpy as jnp
        import numpy as np
        B, S, H, NH = (2, 256, 128, 16)
        DK = H // NH

        def _split_heads(x):
            b, s, _ = x.shape
            return x.reshape(b, s, NH, DK).transpose(0, 2, 1, 3)
        q = _split_heads(query @ Wq.T + bq)
        k = _split_heads(key @ Wk.T + bk)
        v = _split_heads(key @ Wv.T + bv)
        scores = jnp.einsum('bhqd,bhkd->bhqk', q, k) / jnp.sqrt(jnp.float32(DK))
        scores = jnp.where(attn_mask == 0, jnp.float32(-60000.0), scores)
        weights = jax.nn.softmax(scores, axis=-1)
        out = jnp.einsum('bhqk,bhkd->bhqd', weights, v)
        out = out.transpose(0, 2, 1, 3).reshape(query.shape[0], -1, H)
        return out @ Wo.T + bo

    def _L0_ffn_ref(x, gate_w, up_w, up_b, down_w, down_b, sh_up_w, sh_up_b, sh_down_w, sh_down_b):
        import jax, jax.numpy as jnp
        import numpy as np
        D_MODEL = 128
        HIDDEN = 128
        NUM_EXPERTS = 8
        TOP_K = 2
        b, s, d = x.shape
        xf = x.reshape(-1, d)
        shared = jax.nn.silu(x @ sh_up_w + sh_up_b) @ sh_down_w + sh_down_b
        logits = xf @ gate_w.T
        scores = jax.nn.softmax(logits, axis=-1)
        topk_w, topk_i = jax.lax.top_k(scores, TOP_K)
        topk_w = topk_w / (topk_w.sum(axis=-1, keepdims=True) + 1e-20)
        comb = (jax.nn.one_hot(topk_i, NUM_EXPERTS, dtype=xf.dtype) * topk_w[..., None]).sum(axis=1)
        h = jnp.einsum('nd,edh->neh', xf, up_w) + up_b
        h = jax.nn.silu(h)
        ye = jnp.einsum('neh,ehd->ned', h, down_w) + down_b
        y = jnp.einsum('ned,ne->nd', ye, comb).reshape(b, s, d)
        return y + shared

    def _L1_xattn_ref(q, k, v, mask, w_q, w_k, w_v, w_o):
        import jax, jax.numpy as jnp
        import numpy as np
        D_MODEL = 128
        HEAD = 16
        D_K = D_MODEL // HEAD
        NEG = -1000000000.0
        B, S, _ = q.shape

        def proj(x, w):
            return (x @ w.T).reshape(B, -1, HEAD, D_K).transpose(0, 2, 1, 3)
        Q = proj(q, w_q)
        K = proj(k, w_k)
        V = proj(v, w_v)
        scores = jnp.einsum('bhqd,bhkd->bhqk', Q, K) / jnp.sqrt(jnp.float32(D_K))
        scores = jnp.where(mask == 0, NEG, scores)
        attn = jax.nn.softmax(scores, axis=-1)
        x = jnp.einsum('bhqk,bhkd->bhqd', attn, V)
        x = x.transpose(0, 2, 1, 3).reshape(B, S, HEAD * D_K)
        return x @ w_o.T

    def _L1_ffn_ref(hidden_states, ln1_weight, ln1_bias, ln2_weight, ln2_bias, qkv_weight, proj_weight, router_weight, moe_w1, moe_w2):
        import jax, jax.numpy as jnp
        import numpy as np
        S_LEN, BATCH, HIDDEN = (256, 2, 128)
        N_HEADS, N_KV = (16, 8)
        N_EXP, TOP_K, CAP_F = (8, 2, 1.25)
        FFN = 512
        HEAD_DIM = HIDDEN // N_HEADS
        Q_PER_KV = N_HEADS // N_KV
        EPS = 1e-05
        NEG = -1000000000.0

        def _ln(x, w, b):
            mu = jnp.mean(x, -1, keepdims=True)
            var = jnp.var(x, -1, keepdims=True)
            return (x - mu) * jax.lax.rsqrt(var + EPS) * w + b

        def _forward(hidden_states, ln1_weight, ln1_bias, ln2_weight, ln2_bias, qkv_weight, proj_weight, router_weight, moe_w1, moe_w2):
            S, B, H = hidden_states.shape
            ln1 = _ln(hidden_states, ln1_weight, ln1_bias)
            qkv = (ln1 @ qkv_weight.T).reshape(S, B, N_KV, (Q_PER_KV + 2) * HEAD_DIM)
            q_dim = Q_PER_KV * HEAD_DIM
            q = qkv[..., :q_dim].reshape(S, B, N_HEADS, HEAD_DIM)
            k = jnp.repeat(qkv[..., q_dim:q_dim + HEAD_DIM], Q_PER_KV, axis=2)
            v = jnp.repeat(qkv[..., q_dim + HEAD_DIM:], Q_PER_KV, axis=2)
            scores = jnp.einsum('sbhd,tbhd->bhst', q, k) / jnp.sqrt(jnp.float32(HEAD_DIM))
            causal = jnp.tril(jnp.ones((S, S), bool))
            attn = jax.nn.softmax(jnp.where(causal[None, None], scores, NEG), axis=-1)
            attn_out = jnp.einsum('bhst,tbhd->sbhd', attn, v).reshape(S, B, H)
            hidden_after_attn = hidden_states + attn_out @ proj_weight.T
            x = _ln(hidden_after_attn, ln2_weight, ln2_bias).reshape(-1, H)
            N = S * B
            probs = jax.nn.softmax(x.astype(jnp.float32) @ router_weight, axis=-1)
            top_p, top_i = jax.lax.top_k(probs, TOP_K)
            top_p = top_p / jnp.sum(top_p, -1, keepdims=True)
            flat_exp = top_i.reshape(-1)
            order = jnp.argsort(flat_exp)
            sorted_exp = flat_exp[order]
            counts = jnp.bincount(sorted_exp, length=N_EXP)
            offsets = jnp.concatenate([jnp.zeros((1,), counts.dtype), jnp.cumsum(counts)])
            within = jnp.arange(N * TOP_K) - offsets[sorted_exp]
            cap = int(np.ceil(N * TOP_K / N_EXP * CAP_F))
            keep = within < cap
            slot = jnp.where(keep, sorted_exp * cap + within, N_EXP * cap)
            tok_id = order // TOP_K
            padded_tokens = jnp.zeros((N_EXP * cap + 1, H), x.dtype).at[slot].set(x[tok_id])[:-1]
            padded_probs = jnp.zeros((N_EXP * cap + 1,), jnp.float32).at[slot].set(top_p.reshape(-1)[order])[:-1]
            padded_ids = jnp.zeros((N_EXP * cap + 1,), jnp.int32).at[slot].set(tok_id.astype(jnp.int32))[:-1]
            exp_in = padded_tokens.reshape(N_EXP, cap, H)
            act = jax.nn.gelu(jnp.einsum('ech,ehf->ecf', exp_in, moe_w1), approximate=False)
            exp_out = jnp.einsum('ecf,efh->ech', act, moe_w2).reshape(N_EXP * cap, H)
            weighted = exp_out * padded_probs[:, None].astype(exp_out.dtype)
            moe = jnp.zeros((N, H), exp_out.dtype).at[padded_ids].add(weighted)
            return hidden_after_attn + moe.reshape(S, B, H)
        return _forward(hidden_states, ln1_weight, ln1_bias, ln2_weight, ln2_bias, qkv_weight, proj_weight, router_weight, moe_w1, moe_w2)
    x = x + jnp.tanh(g_xattn[0]) * _L0_xattn_ref(_layernorm(x, axis=-1), ctx_1024, mask_Bx1xSxS2_if1, L0_xattn_Wq, L0_xattn_bq, L0_xattn_Wk, L0_xattn_bk, L0_xattn_Wv, L0_xattn_bv, L0_xattn_Wo, L0_xattn_bo)
    x = x + jnp.tanh(g_ffn[0]) * _L0_ffn_ref(_layernorm(x, axis=-1), L0_ffn_gate_w, L0_ffn_up_w, L0_ffn_up_b, L0_ffn_down_w, L0_ffn_down_b, L0_ffn_sh_up_w, L0_ffn_sh_up_b, L0_ffn_sh_down_w, L0_ffn_sh_down_b)
    x = x + jnp.tanh(g_xattn[1]) * _L1_xattn_ref(_layernorm(x, axis=-1), ctx_1024, ctx_1024, mask_1x1xSxS2_if1, L1_xattn_w_q, L1_xattn_w_k, L1_xattn_w_v, L1_xattn_w_o)
    x = x + jnp.tanh(g_ffn[1]) * _L1_ffn_ref(_layernorm(x, axis=-1), L1_ffn_ln1_weight, L1_ffn_ln1_bias, L1_ffn_ln2_weight, L1_ffn_ln2_bias, L1_ffn_qkv_weight, L1_ffn_proj_weight, L1_ffn_router_weight, L1_ffn_moe_w1, L1_ffn_moe_w2)
    return x

_drawn_inputs = setup_inputs


def setup_inputs(seed=0):
    import zlib

    import numpy as np

    out = dict(_drawn_inputs(seed))
    spreads = {'g_ffn': (-1.0, 0.2),
     'L0_ffn_up_b': (0.0, 0.8),
     'L0_ffn_down_b': (0.0, 0.1),
     'L0_ffn_sh_up_b': (0.0, 0.615),
     'L0_ffn_sh_down_b': (0.0, 0.1),
     'L1_ffn_ln1_weight': (1.0, 0.6),
     'L1_ffn_ln1_bias': (0.0, 0.443),
     'L1_ffn_ln2_weight': (1.0, 0.2),
     'L1_ffn_ln2_bias': (0.0, 0.1)}
    factors = {'L0_xattn_Wq': 8.0,
     'L0_xattn_bq': 33.18,
     'L0_xattn_Wk': 8.0,
     'L0_xattn_bk': 64.0,
     'L0_xattn_bv': 7.674,
     'L0_xattn_bo': 3.001,
     'L0_ffn_up_w': 3.508,
     'L0_ffn_down_w': 3.2}
    for name, (base, spread) in spreads.items():
        noise = np.random.default_rng([zlib.crc32(name.encode()), seed]).standard_normal(out[name].shape)
        drawn = base * np.exp(spread * noise) if base else spread * noise
        out[name] = jnp.asarray(drawn.astype(out[name].dtype))
    for name, factor in factors.items():
        out[name] = (out[name] * factor).astype(out[name].dtype)
    return out
```

```python
import concourse.bass as bass
from concourse import mybir
from contextlib import ExitStack

B, S, D, P = 4, 512, 128, 128
TPB = S // P
NT = B * TPB
H, DK, KEYS = 16, 8, 77
HK = H * KEYS
NCH = -(-HK // P)
NB = [min(P, HK - P * c) for c in range(NCH)]
CH0 = [min(P * c // KEYS, H - 3) for c in range(NCH)]
GROUPS = [(0, 6), (6, 6), (12, 4)]
E = 8
CAP = -(-(B * S * 2 * 5) // (E * 4))
XT_TILES = CAP // P
FC = 4
KV = 8
BANK = 512
SCALE = float(DK) ** -0.5


def shape_constants():
    import numpy as np
    p = np.arange(P)
    flat = P * np.arange(NCH)[None, :, None] + p[:, None, None]
    vmask = (flat // KEYS == np.array(CH0)[None, :, None] + np.arange(3)) & (flat < HK)
    sel = np.zeros((P, E, P), np.float32)
    for e in range(E):
        sel[[e, E + e, 2 * E + e], e, :] = 1.0
    parts = {
        "ident": np.eye(P),
        "hmask": (p[:, None] // DK == np.arange(H)) * SCALE,
        "vmask": vmask.reshape(P, NCH * 3),
        "iota": np.broadcast_to(np.arange(E), (P, E)),
        "before": p[:, None] < p,
        "ones": np.ones((P, P)),
        "sel": sel.reshape(P, E * P),
        "base": np.broadcast_to(np.arange(E) * CAP, (P, E)),
    }
    at, start = {}, 0
    for k, a in parts.items():
        at[k] = (start, start + a.shape[1])
        start += a.shape[1]
    return np.ascontiguousarray(np.concatenate(list(parts.values()), 1).astype(np.float32)), at


def gated_layers_kernel(nc, x, ctx_t, mask_b, mask_1, consts, at, sq, gate, up_w, down_w, cols, bo_rows,
                        down_rows, gates, qkv_t, router, moe_w1, moe_w2, out):
    f32, bf16, i32, u32 = mybir.dt.float32, mybir.dt.bfloat16, mybir.dt.int32, mybir.dt.uint32
    ALU, ACT, AX = mybir.AluOpType, mybir.ActivationFunctionType, mybir.AxisListType
    ds = bass.ds

    ctx = ExitStack()
    with ctx:
        def sb(name, shape, dt=f32):
            return ctx.enter_context(nc.sbuf_tensor(name, shape, dt))

        def sem(name):
            return ctx.enter_context(nc.semaphore(name))

        slot_x = nc.dram_tensor("slot_x", [E * CAP, D], f32, kind="Internal").ap()
        slot_y = nc.dram_tensor("slot_y", [E * CAP, D], f32, kind="Internal").ap()

        X = sb("X", [P, NT, D])
        Z = sb("Z", [P, NT, D])
        QKV = sb("QKV", [P, B, TPB * KV, 4 * DK])
        XL = sb("XL", [P, NT, D])
        CST = sb("CST", [P, consts.shape[1]])
        SQ = sb("SQ", [P, 10, D])
        GATE = sb("GATE", [P, E])
        RT = sb("RT", [P, E])
        UPW = sb("UPW", [P, E + 1, P])
        DNW = sb("DNW", [P, E, D])
        QKVT = sb("QKVT", [P, 2 * D])
        COLS = sb("COLS", [P, cols.shape[1]])
        BO = sb("BO", [P, D])
        DB = sb("DB", [E + 1, D])
        TG = sb("TG", [P, 4])
        CTX = sb("CTX", [P, B, KEYS])
        CREP = sb("CREP", [P, NCH * P])
        KT = sb("KT", [P, 2, KEYS])
        KEXP = sb("KEXP", [P, 2 * B, HK])
        VX = sb("VX", [P, 2 * B, NCH * 3, DK + 1])
        MKB = sb("MKB", [P, NT, KEYS], i32)
        MK1 = sb("MK1", [P, TPB, KEYS], i32)
        MZB = sb("MZB", [P, TPB, KEYS], i32)
        MZ1 = sb("MZ1", [P, TPB, KEYS], i32)
        NEG = sb("NEG", [P, 2])
        HALF = sb("HALF", [P, TPB])
        IDB = sb("IDB", [P, P], bf16)
        BEFB = sb("BEFB", [P, P], bf16)
        ONEB = sb("ONEB", [P, P], bf16)
        SELB = sb("SELB", [P, E, P], bf16)
        ST = sb("ST", [P, TPB, 6])
        MV = sb("MV", [P, TPB, 2])
        VE = sb("VE", [P, TPB])
        RS = sb("RS", [P, TPB])
        XN = sb("XN", [P, TPB, D])
        FX = sb("FX", [P, S])
        QT = sb("QT", [P, S])
        MX = sb("MX", [P, H])
        PR = sb("PR", [P, 2, HK])
        PT = sb("PT", [P, 2, NCH * P])
        RD = sb("RD", [P, H])
        OT = sb("OT", [P, TPB, D])
        XR = sb("XR", [P, TPB, D])
        GBO = sb("GBO", [P, D])
        LG = sb("LG", [P, NT, E])
        M8 = sb("M8", [P, NT, E])
        I8 = sb("I8", [P, NT, E], u32)
        IF = sb("IF", [P, NT, 2])
        OH = sb("OH", [P, 2, NT, E])
        EX = sb("EX", [P, TPB, E])
        CM = sb("CM", [P, TPB, E + 1])
        DN = sb("DN", [P, TPB])
        RC = sb("RC", [P, TPB])
        C3 = sb("C3", [P, TPB, 3 * E], bf16)
        C3F = sb("C3F", [P, TPB, E])
        CMT = sb("CMT", [E + 1, S])
        C3T = sb("C3T", [3 * E, S], bf16)
        SL = sb("SL", [P, 2, S])
        HS = sb("HS", [P, 2, S])
        kexp_flat = KEXP[:, :, :].rearrange("p a k -> p (a k)")
        GA = kexp_flat[:, 0:NT * 2 * D].rearrange("p (t k d) -> p t k d", t=NT, k=2)
        GT = [kexp_flat[:, NT * 2 * D + i * FC * CAP:NT * 2 * D + (i + 1) * FC * CAP]
              .rearrange("p (f n) -> p f n", f=FC) for i in range(2)]
        AO = PT[:, :, :].rearrange("p a k -> p (a k)")[:, 0:NT * D].rearrange("p (t d) -> p t d", t=NT)
        PRD = PR[:, :, :].rearrange("p a k -> p (a k)")[:, 0:4 * S].rearrange("p (t n) -> p t n", t=4)
        XE = sb("XE", [P, 2, XT_TILES, D])
        XT = sb("XT", [P, 2, CAP])
        YS = sb("YS", [P, 2, XT_TILES, D])
        W1 = sb("W1", [P, 2, FC * P])
        W2 = sb("W2", [P, 2, FC, D])
        SC = sb("SC", [P, B, B, TPB * H])
        SM = sb("SM", [P, B, TPB * H])
        SR = sb("SR", [P, B, TPB * H])
        CB = sb("CB", [P, 2 * NT, E], bf16)
        RK = sb("RK", [P, NT, E])
        TK = sb("TK", [P, NT, E])
        SLT = sb("SLT", [P, 4, NT])
        WT = sb("WT", [P, 2, NT])
        SCI = sb("SCI", [P, NT, 2], u32)
        GAI = sb("GAI", [P, NT, 2], u32)
        SPARE = sb("SPARE", [P, 1])
        ZERO = sb("ZERO", [P, 2 * D])

        def const(name, rows=P):
            return CST[0:rows, at[name][0]:at[name][1]]

        ident = const("ident")
        col = {n: COLS[:, i:i + 1] for i, n in enumerate(
            ["bq0", "bk0", "bv0", "zero", "ln1w", "ln1b", "ln2w", "ln2b"] + [f"up{e}" for e in range(E + 1)])}

        banks = [ctx.enter_context(nc.psum_tensor(n, [P, BANK], f32))
                 for n in ("S0", "S1", "S2", "T0", "T1", "O", "FLIP", "PROD")]
        SB_, TB_, OB, FLIP, PROD = banks[0:3], banks[3:5], banks[5], banks[6], banks[7]

        x_loaded, att_loaded, ffn_loaded, moe_consts = sem("x_loaded"), sem("att_loaded"), sem("ffn_loaded"), sem("moe_consts")
        small_loaded, masks_loaded = sem("small_loaded"), sem("masks_loaded")
        slots_zeroed, zero_ready = sem("slots_zeroed"), sem("zero_ready")
        consts_ready, tanh_ready, gbo_ready = sem("consts_ready"), sem("tanh_ready"), sem("gbo_ready")
        rep_ready, kprod_ready, kt_ready, kexp_ready = sem("rep_ready"), sem("kprod_ready"), sem("kt_ready"), sem("kexp_ready")
        vprod_ready, vx_ready = sem("vprod_ready"), sem("vx_ready")
        maskz_ready, xr_ready = sem("maskz_ready"), sem("xr_ready")
        dve_done, pool_done = sem("dve_done"), sem("pool_done")
        var_ready, rstd_ready, xn_ready = sem("var_ready"), sem("rstd_ready"), sem("xn_ready")
        flip_ready, flip_taken = sem("flip_ready"), sem("flip_taken")
        prod_ready, prod_taken = sem("prod_ready"), sem("prod_taken")
        scores_ready, scores_taken, probs_ready = sem("scores_ready"), sem("scores_taken"), sem("probs_ready")
        ptrans_ready, pt_ready, pv_ready, o_taken = sem("ptrans_ready"), sem("pt_ready"), sem("pv_ready"), sem("o_taken")
        x_updated = sem("x_updated")
        exp_in, exp_out, comb_ready, comb3_ready = sem("exp_in"), sem("exp_out"), sem("comb_ready"), sem("comb3_ready")
        up_ready, silu_ready, cb_ready, hs_ready = sem("up_ready"), sem("silu_ready"), sem("cb_ready"), sem("hs_ready")
        down_done, y_ready = sem("down_done"), sem("y_ready")
        in_scores, in_exp, ao_ready, z_ready = sem("in_scores"), sem("in_exp"), sem("ao_ready"), sem("z_ready")
        top_in, top_exp, cb2_ready, rank_ready, slots_ready = sem("top_in"), sem("top_exp"), sem("cb2_ready"), sem("rank_ready"), sem("slots_ready")
        scattered = sem("scattered")
        xe_loaded, w_loaded, y_stored = [sem("xe_loaded0"), sem("xe_loaded1")], [sem("w_loaded0"), sem("w_loaded1")], [sem("y_stored0"), sem("y_stored1")]
        xe_flipped, xt_ready, eup_ready, gelu_ready = sem("xe_flipped"), sem("xt_ready"), sem("eup_ready"), sem("gelu_ready")
        edown_ready, ye_ready = sem("edown_ready"), sem("ye_ready")
        gathered = [sem(f"gathered{s}") for s in range(B)]
        final_ready, out_stored = sem("final_ready"), sem("out_stored")

        FL = {n: i for i, n in enumerate(["ln0", "o0", "ln1", "comb", "ln2", "o1", "ln4"])}
        PD = {n: i for i, n in enumerate(["q0", "out0", "logits", "comb3", "q1", "out1", "qkv0", "qkv1"])}
        NFL, NPD = len(FL), len(PD)
        LNS = 5
        TB3 = TPB * 3

        def headed(ap, n):
            return ap.rearrange("p (h k) -> p h k", h=n)

        block = ctx.enter_context(nc.Block())

        @block.sync
        def _(sp):
            sp.dma_start(CTX[:, :, :], ctx_t).then_inc(small_loaded, 16)
            sp.dma_start(CST[:, :], consts).then_inc(small_loaded, 16)
            sp.dma_start(COLS[:, :], cols).then_inc(small_loaded, 16)
            sp.dma_start(BO[:, :], bo_rows).then_inc(small_loaded, 16)
            sp.dma_start(TG[:, :], gates).then_inc(small_loaded, 16)
            sp.dma_start(SQ[:, :, :], sq).then_inc(att_loaded, 16)
            sp.dma_start(X[:, :, :], x.rearrange("(t p) d -> p t d", p=P)).then_inc(x_loaded, 16)
            sp.dma_start(MKB[:, :, :], mask_b.rearrange("(t p) k -> p t k", p=P)).then_inc(masks_loaded, 16)
            sp.dma_start(MK1[:, :, :], mask_1.rearrange("(t p) k -> p t k", p=P)).then_inc(masks_loaded, 16)
            sp.dma_start(GATE[:, :], gate).then_inc(ffn_loaded, 16)
            sp.dma_start(UPW[:, :, :], up_w).then_inc(ffn_loaded, 16)
            sp.dma_start(DNW[:, :, :], down_w).then_inc(ffn_loaded, 16)
            sp.dma_start(DB[:, :], down_rows).then_inc(ffn_loaded, 16)
            sp.dma_start(QKVT[:, :], qkv_t).then_inc(ffn_loaded, 16)
            sp.dma_start(RT[:, :], router).then_inc(ffn_loaded, 16)
            sp.wait_ge(zero_ready, 1)
            sp.dma_start(slot_x.rearrange("(p q) d -> p q d", p=P),
                         ZERO[:, 0:D].unsqueeze(1).broadcast_to([P, E * CAP // P, D])).then_inc(slots_zeroed, 16)
            for i in range(2):
                sp.dma_start(W1[:, i, :], moe_w1[:, i]).then_inc(w_loaded[i], 16)
                sp.dma_start(W2[:, i, :, :], moe_w2[:, i]).then_inc(w_loaded[i], 16)
            sp.wait_ge(scattered, 16 * 2 * NT)
            for i in range(2):
                sp.dma_start(XE[:, i, :, :], slot_x[i * CAP:(i + 1) * CAP, :].rearrange("(c p) d -> p c d", p=P)).then_inc(xe_loaded[i], 16)
            slots = slot_x.rearrange("(e c p) d -> p e c d", c=XT_TILES, p=P)
            rows = slot_y.rearrange("(e c p) d -> p e c d", c=XT_TILES, p=P)
            with sp.Fori(0, E // 2 - 1) as pair:
                for i in range(2):
                    nxt = ds(pair * 2 + (2 + i), 1)
                    sp.wait_ge(xe_flipped, pair * 2 + (i + 1))
                    sp.dma_start(XE[:, i:i + 1, :, :], slots[:, nxt]).then_inc(xe_loaded[i], 16)
                    sp.wait_ge(ye_ready, pair * 2 + (i + 1))
                    sp.dma_start(rows[:, ds(pair * 2 + i, 1)], YS[:, i:i + 1, :, :]).then_inc(y_stored[i], 16)
                    sp.dma_start(W1[:, i:i + 1, :], moe_w1[:, nxt]).then_inc(w_loaded[i], 16)
                    sp.dma_start(W2[:, i:i + 1, :, :], moe_w2[:, nxt]).then_inc(w_loaded[i], 16)
            for i in range(2):
                sp.wait_ge(ye_ready, E - 1 + i)
                sp.dma_start(rows[:, E - 2 + i], YS[:, i, :, :]).then_inc(y_stored[i], 16)
            for s in range(B):
                sp.wait_ge(final_ready, s + 1)
                sp.dma_start(out[s * S:(s + 1) * S, :].rearrange("(t p) d -> p t d", p=P),
                             X[:, s * TPB:(s + 1) * TPB, :]).then_inc(out_stored, 16)
            sp.wait_ge(out_stored, 16 * B)

        @block.gpsimd
        def _(pool):
            nc.gpsimd.memset(ZERO[:, :], 0.0).then_inc(zero_ready, 1)
            nc.gpsimd.memset(HALF[:, :], -0.5)
            nc.gpsimd.memset(NEG[:, 0:1], -60000.0)
            nc.gpsimd.memset(NEG[:, 1:2], -1e9)
            nc.gpsimd.memset(CM[:, :, E:E + 1], 1.0)
            nc.gpsimd.memset(CB[:, 0:NT, :], 0.0)
            nc.gpsimd.memset(CREP[:, HK:NCH * P], 0.0)
            nc.gpsimd.memset(SC[:, :, :, :], -1e9).then_inc(pool_done, 1)
            pool.wait_ge(small_loaded, 16 * 5)
            nc.gpsimd.tensor_copy(IDB[:, :], ident)
            nc.gpsimd.tensor_copy(BEFB[:, :], const("before"))
            nc.gpsimd.tensor_copy(ONEB[:, :], const("ones"))
            nc.gpsimd.tensor_copy(SELB[:, :, :], const("sel").rearrange("p (e n) -> p e n", e=E)).then_inc(consts_ready, 1)
            pool.wait_ge(masks_loaded, 32)
            nc.gpsimd.tensor_scalar(MKB[:, :, :], MKB[:, :, :], 0.0, None, ALU.is_equal).then_inc(pool_done, 1)
            nc.gpsimd.tensor_scalar(MZ1[:, :, :], MK1[:, :, :], 0.0, None, ALU.is_equal).then_inc(maskz_ready, 1)
            pool.wait_ge(tanh_ready, 1)
            nc.gpsimd.tensor_scalar(GBO[:, :], BO[:, :], TG[:, 0:1], None, ALU.mult).then_inc(gbo_ready, 1)
            with pool.Fori(0, B) as b:
                pool.wait_ge(vprod_ready, b * 2)
                nc.gpsimd.tensor_copy(headed(CREP[:, 0:HK], H), CTX[:, ds(b, 1), :].broadcast_to([P, H, KEYS])).then_inc(rep_ready, 1)
                for l in range(2):
                    pool.wait_ge(kt_ready, b * 2 + (l + 1))
                    nc.gpsimd.tensor_tensor(KEXP[:, ds(b * 2 + l, 1), :].rearrange("p o (h k) -> p (o h) k", h=H),
                                            KT[:, l, :].unsqueeze(1).broadcast_to([P, H, KEYS]),
                                            const("hmask").unsqueeze(2).broadcast_to([P, H, KEYS]), ALU.mult).then_inc(kexp_ready, 1)

            def rstd(ready):
                pool.wait_ge(var_ready, ready)
                nc.gpsimd.tensor_tensor(RS[:, :], VE[:, :], HALF[:, :], ALU.pow).then_inc(rstd_ready, 1)

            pool.wait_ge(gbo_ready, 1)
            pool.wait_ge(pool_done, 2)
            pool.wait_ge(x_loaded, 16)
            with pool.Fori(0, B) as b:
                pool.wait_ge(scores_taken, b * (2 * TB3))
                nc.gpsimd.tensor_copy(MZB[:, :, :], MKB[:, ds(b * TPB, TPB), :]).then_inc(maskz_ready, 1)
                rstd(b * LNS + 1)
                nc.gpsimd.tensor_tensor(XR[:, :, :], X[:, ds(b * TPB, TPB), :],
                                        GBO[:, :].unsqueeze(1).broadcast_to([P, TPB, D]), ALU.add).then_inc(xr_ready, 1)
                for n in range(1, LNS):
                    rstd(b * LNS + n + 1)
            for s in range(B):
                rstd(B * LNS + s + 1)
            pool.wait_ge(slots_zeroed, 16)
            pool.wait_ge(slots_ready, 1)
            for T in range(NT):
                for k in range(2):
                    nc.gpsimd.indirect_dma_start(
                        out=slot_x, out_offset=bass.IndirectOffsetOnAxis(ap=SCI[:, T, k:k + 1], axis=0),
                        in_=XL[:, T, :], in_offset=None, bounds_check=E * CAP - 1, oob_is_err=False).then_inc(scattered, 16)
            for i in range(2):
                pool.wait_ge(y_stored[i], 16 * (E // 2))
            for T in range(NT):
                for k in range(2):
                    nc.gpsimd.indirect_dma_start(
                        out=GA[:, T, k, :], out_offset=None, in_=slot_y,
                        in_offset=bass.IndirectOffsetOnAxis(ap=GAI[:, T, k:k + 1], axis=0)).then_inc(gathered[T // TPB], 16)

        @block.scalar
        def _(act):
            act.wait_ge(small_loaded, 16 * 5)
            nc.scalar.activation(TG[:, :], TG[:, :], ACT.Tanh).then_inc(tanh_ready, 1)
            with act.Fori(0, B) as b:
                for l in range(2):
                    act.wait_ge(kprod_ready, b * 2 + (l + 1))
                    act.wait_ge(kexp_ready, b * 2)
                    nc.scalar.activation(KT[:, l, :], SB_[l][:, 0:KEYS], ACT.Identity,
                                         bias=col["bk0" if l == 0 else "zero"]).then_inc(kt_ready, 1)

            def flip_out(dst, ready, bias=None, scale=1.0, rows=P, width=S):
                act.wait_ge(flip_ready, ready)
                src = FLIP[0:rows, 0:width]
                if bias is None:
                    nc.scalar.activation(dst, src, ACT.Copy).then_inc(flip_taken, 1)
                else:
                    nc.scalar.activation(dst, src, ACT.Identity, bias=bias, scale=scale).then_inc(flip_taken, 1)

            def attention(b, l):
                flip_out(FX[:, :], b * NFL + (FL[f"ln{2 * l}"] + 1))
                act.wait_ge(prod_ready, b * NPD + (PD[f"q{l}"] + 1))
                nc.scalar.activation(QT[:, :], PROD[:, :], ACT.Identity, bias=col["bq0" if l == 0 else "zero"]).then_inc(prod_taken, 1)
                for step in range(TPB + 1):
                    if step >= 1:
                        t = step - 1
                        u = l * TPB + t
                        act.wait_ge(pv_ready, b * (2 * TPB) + max(u - 1, 0))
                        for j in range(3):
                            act.wait_ge(ptrans_ready, b * (2 * TB3) + (3 * u + j + 1))
                            w = min(4, NCH - 4 * j) * P
                            rows = P
                            src = TB_[(3 * u + j) % 2]
                            if j < 2:
                                nc.scalar.activation(PT[:, t % 2, 4 * j * P:4 * j * P + w], src[:, 0:w], ACT.Copy).then_inc(pt_ready, 1)
                            else:
                                nc.scalar.activation(PT[:, t % 2, 8 * P:9 * P], src[:, 0:P], ACT.Copy)
                                nc.scalar.activation(PT[0:NB[9], t % 2, 9 * P:10 * P], src[0:NB[9], P:2 * P], ACT.Copy).then_inc(pt_ready, 1)
                    if step < TPB:
                        u = l * TPB + step
                        act.wait_ge(scores_taken, b * (2 * TB3) + 3 * (u + 1))
                        nc.scalar.activation(PR[:, step % 2, :], PR[:, step % 2, :], ACT.Exp).then_inc(probs_ready, 1)
                flip_out(FX[:, :], b * NFL + (FL[f"o{l}"] + 1), bias=col["bv0" if l == 0 else "zero"])

            def mixture(b):
                flip_out(FX[:, :], b * NFL + (FL["ln1"] + 1))
                act.wait_ge(exp_in, b + 1)
                nc.scalar.activation(EX[:, :, :], EX[:, :, :], ACT.Exp).then_inc(exp_out, 1)
                flip_out(CMT[:, :], b * NFL + (FL["comb"] + 1), rows=E + 1)
                act.wait_ge(prod_ready, b * NPD + (PD["comb3"] + 1))
                nc.scalar.activation(C3T[:, :], PROD[0:3 * E, :], ACT.Copy).then_inc(prod_taken, 1)
                for e in range(E + 1):
                    act.wait_ge(up_ready, b * (E + 1) + (e + 1))
                    act.wait_ge(hs_ready, b * E + max(e - 1, 0))
                    nc.scalar.activation(SL[:, e % 2, :], SB_[e % 2][:, :], ACT.Silu, bias=col[f"up{e}"]).then_inc(silu_ready, 1)

            with act.Fori(0, B) as b:
                attention(b, 0)
                mixture(b)
                attention(b, 1)
                flip_out(FX[:, :], b * NFL + (FL["ln4"] + 1), bias=col["ln1b"], scale=col["ln1w"])
                for j in range(2):
                    act.wait_ge(prod_ready, b * NPD + (PD[f"qkv{j}"] + 1))
                    nc.scalar.activation(QKV[:, ds(b, 1), j * 2 * KV:(j + 1) * 2 * KV, :].rearrange("p o n d -> p (o n d)"),
                                         PROD[:, :], ACT.Copy).then_inc(prod_taken, 1)
            act.wait_ge(in_scores, 1)
            nc.scalar.activation(SC[:, :, :, :], SC[:, :, :, :], ACT.Exp, scale=SCALE).then_inc(in_exp, 1)
            for s in range(B):
                flip_out(FX[:, :], B * NFL + 2 * s + 1)
                flip_out(QT[:, :], B * NFL + 2 * s + 2, bias=col["ln2b"], scale=col["ln2w"])
            act.wait_ge(top_in, 1)
            nc.scalar.activation(WT[:, 1, :], WT[:, 1, :], ACT.Exp).then_inc(top_exp, 1)
            eb = [TB_[0], TB_[1], FLIP, PROD]
            with act.Fori(0, E // 2) as pair:
                for i in range(2):
                    for q in range(2 * FC):
                        act.wait_ge(eup_ready, pair * (4 * FC) + (i * 2 * FC + q + 1))
                        half = CAP // 2
                        nc.scalar.activation(GT[i][:, q // 2, (q % 2) * half:(q % 2 + 1) * half],
                                             eb[q % 4][:, 0:half], ACT.Gelu).then_inc(gelu_ready, 1)

        @block.vector
        def _(dve):
            link_base, links = [0], [0]

            def link(ins):
                links[0] += 1
                ins.then_inc(dve_done, 1)
                dve.wait_ge(dve_done, link_base[0] + links[0])

            def apart():
                nc.vector.memset(SPARE[:, :], 0.0)

            dve.wait_ge(small_loaded, 16 * 5)
            vmask = const("vmask")
            for a in range(2 * B):
                nc.vector.tensor_copy(VX[:, a, :, DK], vmask)
            with dve.Fori(0, B) as b:
                for l in range(2):
                    dve.wait_ge(vprod_ready, b * 2 + (l + 1))
                    nc.vector.tensor_tensor(VX[:, ds(b * 2 + l, 1), :, 0:DK].rearrange("p o c d -> p (o c) d"),
                                            TB_[l][:, 0:NCH * 3 * DK].rearrange("p (c d) -> p c d", d=DK),
                                            vmask.unsqueeze(2).broadcast_to([P, NCH * 3, DK]), ALU.mult).then_inc(vx_ready, 1)

            def norm(src, n, dst, done, flipped=None):
                apart()
                for t in range(TPB):
                    ins = nc.vector.bn_stats(ST[:, t, :], src(t))
                link(ins)
                apart()
                for t in range(TPB):
                    ins = nc.vector.bn_aggr(MV[:, t, :], ST[:, t, :])
                link(ins)
                nc.vector.tensor_scalar(VE[:, :], MV[:, :, 1], 1e-5, None, ALU.add).then_inc(var_ready, 1)
                dve.wait_ge(rstd_ready, n)
                if flipped is not None:
                    dve.wait_ge(flip_ready, flipped)
                for t in range(TPB):
                    ins = nc.vector.tensor_scalar(dst(t), src(t), MV[:, t, 0:1], RS[:, t:t + 1], ALU.subtract, ALU.mult)
                ins.then_inc(done, 1)

            def x_tile(b):
                return lambda t: X[:, ds(b * TPB + t, 1), :].rearrange("p o d -> p (o d)")

            def attention(b, l):
                mz = MZB if l == 0 else MZ1
                norm(x_tile(b), b * LNS + (2 * l + 1), lambda t: XN[:, t, :], xn_ready, b * NFL + FL[f"ln{2 * l}"])
                dve.wait_ge(maskz_ready, b + 2)
                for step in range(TPB + 2):
                    if step < TPB:
                        u = l * TPB + step
                        for g, (h0, n) in enumerate(GROUPS):
                            v = 3 * u + g
                            sc = headed(SB_[g][:, 0:n * KEYS], n)
                            dve.wait_ge(scores_ready, b * (2 * TB3) + (v + 1))
                            apart()
                            link(nc.vector.copy_predicated(sc, mz[:, step, :].unsqueeze(1).broadcast_to([P, n, KEYS]),
                                                           NEG[:, l:l + 1].unsqueeze(2).broadcast_to([P, n, KEYS])))
                            link(nc.vector.reduce_max(MX[:, h0:h0 + n], sc, AX.X))
                            if g == 0:
                                dve.wait_ge(ptrans_ready, b * (2 * TB3) + max(3 * (u - 1), 0))
                            nc.vector.tensor_tensor(headed(PR[:, step % 2, h0 * KEYS:(h0 + n) * KEYS], n), sc,
                                                    MX[:, h0:h0 + n].unsqueeze(2).broadcast_to([P, n, KEYS]),
                                                    ALU.subtract).then_inc(scores_taken, 1)
                    if step >= 2:
                        t = step - 2
                        u = l * TPB + t
                        dve.wait_ge(pv_ready, b * (2 * TPB) + (u + 1))
                        o9 = OB[:, 0:H * (DK + 1)].rearrange("p (h j) -> p h j", h=H)
                        link(nc.vector.reciprocal(RD[:, :], o9[:, :, DK]))
                        nc.vector.tensor_tensor(OT[:, t, :].rearrange("p (h d) -> p h d", h=H), o9[:, :, 0:DK],
                                                RD[:, :].unsqueeze(2).broadcast_to([P, H, DK]), ALU.mult).then_inc(o_taken, 1)
                dve.wait_ge(prod_ready, b * NPD + (PD[f"out{l}"] + 1))
                if l == 0:
                    dve.wait_ge(xr_ready, b + 1)
                xb = X[:, ds(b * TPB, TPB), :].rearrange("p t d -> p (t d)")
                rest = XR[:, :, :].rearrange("p t d -> p (t d)") if l == 0 else xb
                ins = nc.vector.scalar_tensor_tensor(out=xb, in0=PROD[:, :], scalar=TG[:, 2 * l:2 * l + 1], in1=rest,
                                                     op0=ALU.mult, op1=ALU.add)
                ins.then_inc(prod_taken, 1)
                dve.wait_ge(prod_taken, b * NPD + (PD[f"out{l}"] + 1))

            def top2(T0, n):
                apart()
                for T in range(T0, T0 + n):
                    ins = nc.vector.max(M8[:, T, :], LG[:, T, :])
                link(ins)
                apart()
                for T in range(T0, T0 + n):
                    ins = nc.vector.max_index(I8[:, T, :], M8[:, T, :], LG[:, T, :])
                link(ins)
                link(nc.vector.tensor_copy(IF[:, T0:T0 + n, :], I8[:, T0:T0 + n, 0:2]))
                for k in range(2):
                    ins = nc.vector.tensor_tensor(OH[:, k, T0:T0 + n, :], const("iota").unsqueeze(1).broadcast_to([P, n, E]),
                                                  IF[:, T0:T0 + n, k:k + 1].broadcast_to([P, n, E]), ALU.is_equal)
                link(ins)

            def mixture(b):
                norm(x_tile(b), b * LNS + 2, lambda t: XN[:, t, :], xn_ready, b * NFL + FL["ln1"])
                dve.wait_ge(prod_ready, b * NPD + (PD["logits"] + 1))
                ins = nc.vector.tensor_copy(LG[:, 0:TPB, :].rearrange("p t e -> p (t e)"), PROD[:, 0:TPB * E])
                ins.then_inc(prod_taken, 1)
                dve.wait_ge(prod_taken, b * NPD + (PD["logits"] + 1))
                top2(0, TPB)
                nc.vector.tensor_tensor(EX[:, :, :], LG[:, 0:TPB, :], M8[:, 0:TPB, 0:1].broadcast_to([P, TPB, E]),
                                        ALU.subtract).then_inc(exp_in, 1)
                link(nc.vector.tensor_tensor(OH[:, 0, 0:TPB, :], OH[:, 0, 0:TPB, :], OH[:, 1, 0:TPB, :], ALU.add))
                dve.wait_ge(exp_out, b + 1)
                cm = CM[:, :, 0:E]
                link(nc.vector.tensor_tensor(C3F[:, :, :], EX[:, :, :], OH[:, 0, 0:TPB, :], ALU.mult))
                link(nc.vector.reduce_sum(DN[:, :], C3F[:, :, :], AX.X))
                link(nc.vector.tensor_scalar(DN[:, :], DN[:, :], 1e-20, None, ALU.add))
                link(nc.vector.reciprocal(RC[:, :], DN[:, :]))
                ins = nc.vector.tensor_tensor(cm, C3F[:, :, :], RC[:, :].unsqueeze(2).broadcast_to([P, TPB, E]), ALU.mult)
                ins.then_inc(comb_ready, 1)
                dve.wait_ge(comb_ready, b + 1)
                link(nc.vector.tensor_copy(C3[:, :, 0:E], cm))
                link(nc.vector.tensor_tensor(C3F[:, :, :], cm, C3[:, :, 0:E], ALU.subtract))
                link(nc.vector.tensor_copy(C3[:, :, E:2 * E], C3F[:, :, :]))
                nc.vector.tensor_tensor(C3[:, :, 2 * E:3 * E], C3F[:, :, :], C3[:, :, E:2 * E], ALU.subtract).then_inc(comb3_ready, 1)
                for e in range(E):
                    dve.wait_ge(silu_ready, b * (E + 1) + (e + 1))
                    dve.wait_ge(cb_ready, b * E + (e + 1))
                    dve.wait_ge(down_done, b * (E + 1) + max(e - 1, 0))
                    nc.vector.tensor_tensor(HS[:, e % 2, :], SL[:, e % 2, :], TB_[e % 2][:, :], ALU.mult).then_inc(hs_ready, 1)
                dve.wait_ge(y_ready, b + 1)
                xb = X[:, ds(b * TPB, TPB), :].rearrange("p t d -> p (t d)")
                nc.vector.scalar_tensor_tensor(out=xb, in0=OB[:, :], scalar=TG[:, 1:2], in1=xb,
                                               op0=ALU.mult, op1=ALU.add).then_inc(x_updated, 1)
                dve.wait_ge(x_updated, b + 1)

            def batch(b):
                attention(b, 0)
                mixture(b)
                attention(b, 1)
                norm(x_tile(b), b * LNS + 4, lambda t: Z[:, ds(b * TPB + t, 1), :].rearrange("p o d -> p (o d)"), z_ready)
                dve.wait_ge(z_ready, b + 1)
                norm(lambda t: Z[:, ds(b * TPB + t, 1), :].rearrange("p o d -> p (o d)"), b * LNS + 5, lambda t: XN[:, t, :], xn_ready, b * NFL + FL["ln4"])

            PER = 2 * LNS + 2 * (2 * TB3 + TPB) + 4 + 5 + 3
            dve.wait_ge(x_loaded, 16)
            with dve.Fori(0, B) as b:
                links[0] = 0
                link_base[0] = b * PER
                batch(b)
                assert links[0] == PER, links[0]
            link_base[0], links[0] = B * PER, 0

            dve.wait_ge(prod_taken, B * NPD)
            dve.wait_ge(pool_done, 1)

            def q_of(s):
                return QKV[:, s, :, 0:2 * DK].rearrange("p n (j d) -> p n j d", j=2)

            def kv_of(t, k):
                return QKV[:, t, :, (2 + k) * DK:(3 + k) * DK].unsqueeze(2).broadcast_to([P, TPB * KV, 2, DK])

            def by_head(ap):
                return ap.rearrange("p (n j d) -> p n j d", j=2, d=DK)

            for s in range(B):
                for t in range(s + 1):
                    ins = nc.vector.tensor_tensor(by_head(PRD[:, t, :]), q_of(s), kv_of(t, 0), ALU.mult)
                link(ins)
                for t in range(s + 1):
                    ins = nc.vector.reduce_sum(SC[:, s, t, :], PRD[:, t, :].rearrange("p (n d) -> p n d", d=DK), AX.X)
                link(ins)
            link(nc.vector.reduce_max(SM[:, :, :], SC[:, :, :, :].rearrange("p s t n -> p s n t"), AX.X))
            for s in range(B):
                ins = nc.vector.tensor_tensor(SC[:, s, :, :], SC[:, s, :, :], SM[:, s, :].unsqueeze(1).broadcast_to([P, B, TPB * H]), ALU.subtract)
            ins.then_inc(in_scores, 1)
            dve.wait_ge(in_exp, 1)
            link(nc.vector.reduce_sum(SM[:, :, :], SC[:, :, :, :].rearrange("p s t n -> p s n t"), AX.X))
            link(nc.vector.reciprocal(SR[:, :, :], SM[:, :, :]))
            for s in range(B):
                ins = nc.vector.tensor_tensor(SC[:, s, :, :], SC[:, s, :, :], SR[:, s, :].unsqueeze(1).broadcast_to([P, B, TPB * H]), ALU.mult)
            link(ins)

            def inner_values(s):
                ao = AO[:, s * TPB:(s + 1) * TPB, :].rearrange("p t d -> p (t d)")
                for t in range(s + 1):
                    dst = ao if t == 0 else PRD[:, t, :]
                    w = SC[:, s, t, :].rearrange("p (n j) -> p n j", j=2).unsqueeze(3).broadcast_to([P, TPB * KV, 2, DK])
                    ins = nc.vector.tensor_tensor(by_head(dst), w, kv_of(t, 1), ALU.mult)
                for t in range(1, s + 1):
                    link(ins)
                    ins = nc.vector.tensor_tensor(ao, ao, PRD[:, t, :], ALU.add)
                ins.then_inc(ao_ready, 1)
                dve.wait_ge(ao_ready, s + 1)

            inner_values(0)
            for s in range(B):
                if s + 1 < B:
                    inner_values(s + 1)
                zs = Z[:, s * TPB:(s + 1) * TPB, :].rearrange("p t d -> p (t d)")
                dve.wait_ge(prod_ready, B * NPD + 2 * s + 1)
                ins = nc.vector.tensor_tensor(zs, PROD[:, :], zs, ALU.add)
                ins.then_inc(prod_taken, 1)
                dve.wait_ge(prod_taken, B * NPD + 2 * s + 1)
                norm(lambda t: Z[:, s * TPB + t, :], B * LNS + s + 1, lambda t: XL[:, s * TPB + t, :], xn_ready)
                dve.wait_ge(prod_ready, B * NPD + 2 * s + 2)
                ins = nc.vector.tensor_copy(LG[:, s * TPB:(s + 1) * TPB, :].rearrange("p t e -> p (t e)"), PROD[:, 0:TPB * E])
                ins.then_inc(prod_taken, 1)
            dve.wait_ge(prod_taken, B * NPD + 2 * B)
            top2(0, NT)
            nc.vector.tensor_tensor(CB[:, NT:2 * NT, :], OH[:, 0, :, :], OH[:, 1, :, :], ALU.add).then_inc(cb2_ready, 1)
            nc.vector.tensor_tensor(WT[:, 1, :], M8[:, :, 1], M8[:, :, 0], ALU.subtract).then_inc(top_in, 1)
            dve.wait_ge(top_exp, 1)
            link(nc.vector.tensor_scalar(SLT[:, 3, :], WT[:, 1, :], 1.0, None, ALU.add))
            link(nc.vector.reciprocal(WT[:, 0, :], SLT[:, 3, :]))
            link(nc.vector.tensor_tensor(WT[:, 1, :], WT[:, 1, :], WT[:, 0, :], ALU.mult))
            dve.wait_ge(rank_ready, 1)
            link(nc.vector.tensor_copy(RK[:, :, :].rearrange("p t e -> p (t e)"), PROD[:, 0:NT * E]))
            for k in range(2):
                rank, keep, slot, far = (SLT[:, i, :] for i in range(4))
                link(nc.vector.tensor_tensor(TK[:, :, :], RK[:, :, :], OH[:, k, :, :], ALU.mult))
                link(nc.vector.reduce_sum(rank, TK[:, :, :], AX.X))
                link(nc.vector.tensor_scalar(keep, rank, float(CAP), None, ALU.is_lt))
                link(nc.vector.scalar_tensor_tensor(out=slot, in0=IF[:, :, k], scalar=float(CAP), in1=rank, op0=ALU.mult, op1=ALU.add))
                link(nc.vector.tensor_scalar(far, keep, float(-2 * E * CAP), float(2 * E * CAP), ALU.mult, ALU.add))
                nc.vector.tensor_tensor(SCI[:, :, k], far, slot, ALU.add)
                nc.vector.tensor_tensor(GAI[:, :, k], slot, keep, ALU.mult)
                link(nc.vector.tensor_tensor(WT[:, k, :], WT[:, k, :], keep, ALU.mult))
            nc.vector.tensor_copy(SLT[:, 0, 0:1], SLT[:, 1, 0:1]).then_inc(slots_ready, 1)

            with dve.Fori(0, E // 2) as pair:
                for i in range(2):
                    dve.wait_ge(xe_flipped, pair * 2 + (i + 1))
                    nc.vector.tensor_scalar(XT[:, i, 0:BANK], SB_[0][:, :], col["ln2w"], col["ln2b"], ALU.mult, ALU.add)
                    nc.vector.tensor_scalar(XT[:, i, BANK:CAP], SB_[1][:, 0:CAP - BANK], col["ln2w"], col["ln2b"],
                                            ALU.mult, ALU.add).then_inc(xt_ready, 1)
                    dve.wait_ge(edown_ready, pair * 2 + (i + 1))
                    dve.wait_ge(y_stored[i], pair * 16)
                    ys = YS[:, i, :, :].rearrange("p c d -> p (c d)")
                    nc.vector.tensor_copy(ys[:, 0:BANK], OB[:, :])
                    nc.vector.tensor_copy(ys[:, BANK:CAP], SB_[2][:, 0:CAP - BANK]).then_inc(ye_ready, 1)
            for s in range(B):
                dve.wait_ge(gathered[s], 16 * 2 * TPB)
                for k in range(2):
                    for T in range(s * TPB, (s + 1) * TPB):
                        ins = nc.vector.scalar_tensor_tensor(out=Z[:, T, :], in0=GA[:, T, k, :], scalar=WT[:, k, T:T + 1], in1=Z[:, T, :],
                                                             op0=ALU.mult, op1=ALU.add)
                    link(ins)
                xs = X[:, s * TPB:(s + 1) * TPB, :].rearrange("p t d -> p (t d)")
                zs = Z[:, s * TPB:(s + 1) * TPB, :].rearrange("p t d -> p (t d)")
                nc.vector.scalar_tensor_tensor(out=xs, in0=zs, scalar=TG[:, 3:4], in1=xs, op0=ALU.mult, op1=ALU.add).then_inc(final_ready, 1)

        @block.tensor
        def _(pe):
            mm = nc.tensor.matmul
            pe.wait_ge(att_loaded, 16)
            pe.wait_ge(small_loaded, 16 * 5)
            with pe.Fori(0, B) as b:
                pe.wait_ge(rep_ready, b + 1)
                for l in range(2):
                    pe.wait_ge(kt_ready, b * 2)
                    mm(SB_[l][:, 0:KEYS], SQ[:, 4 * l + 1, :], CREP[:, 0:KEYS], start=True, stop=True).then_inc(kprod_ready, 1)
                for l in range(2):
                    pe.wait_ge(vx_ready, b * 2)
                    for c in range(NCH):
                        ins = mm(TB_[l][:, c * 3 * DK:(c + 1) * 3 * DK], CREP[:, c * P:(c + 1) * P],
                                 SQ[:, 4 * l + 2, CH0[c] * DK:(CH0[c] + 3) * DK], start=True, stop=True)
                    ins.then_inc(vprod_ready, 1)
            pe.wait_ge(kexp_ready, 2 * B)
            pe.wait_ge(vx_ready, 2 * B)
            pe.wait_ge(consts_ready, 1)
            pe.wait_ge(ffn_loaded, 16 * 6)

            def flip_tiles(src, taken):
                pe.wait_ge(flip_taken, taken)
                for t in range(TPB):
                    ins = nc.tensor.transpose(FLIP[:, t * P:(t + 1) * P], src(t), ident)
                ins.then_inc(flip_ready, 1)

            def attention(b, l):
                pe.wait_ge(xn_ready, b * 4 + (2 * l + 1))
                flip_tiles(lambda t: XN[:, t, :], b * NFL + FL[f"ln{2 * l}"])
                pe.wait_ge(flip_taken, b * NFL + (FL[f"ln{2 * l}"] + 1))
                pe.wait_ge(prod_taken, b * NPD + PD[f"q{l}"])
                mm(PROD[:, :], SQ[:, 4 * l, :], FX[:, :], start=True, stop=True).then_inc(prod_ready, 1)
                pe.wait_ge(prod_taken, b * NPD + (PD[f"q{l}"] + 1))
                for step in range(TPB + 2):
                    if step < TPB:
                        u = l * TPB + step
                        for g, (h0, n) in enumerate(GROUPS):
                            pe.wait_ge(scores_taken, b * (2 * TB3) + max(3 * u + g - 2, 0))
                            mm(SB_[g][:, 0:n * KEYS], QT[:, step * P:(step + 1) * P],
                               KEXP[:, ds(b * 2 + l, 1), h0 * KEYS:(h0 + n) * KEYS].rearrange("p o k -> p (o k)"),
                               start=True, stop=True).then_inc(scores_ready, 1)
                    if 1 <= step <= TPB:
                        u = l * TPB + step - 1
                        pe.wait_ge(probs_ready, b * (2 * TPB) + (u + 1))
                        for j in range(3):
                            pe.wait_ge(pt_ready, b * (2 * TB3) + max(3 * u + j - 1, 0))
                            for c in range(4 * j, min(4 * j + 4, NCH)):
                                ins = nc.tensor.transpose(TB_[(3 * u + j) % 2][0:NB[c], (c % 4) * P:(c % 4 + 1) * P],
                                                          PR[:, (step - 1) % 2, c * P:c * P + NB[c]], ident)
                            ins.then_inc(ptrans_ready, 1)
                    if step >= 2:
                        t = step - 2
                        u = l * TPB + t
                        pe.wait_ge(pt_ready, b * (2 * TB3) + 3 * (u + 1))
                        pe.wait_ge(o_taken, b * (2 * TPB) + u)
                        for c in range(NCH):
                            at_col = CH0[c] * (DK + 1)
                            ins = mm(OB[:, at_col:at_col + 3 * (DK + 1)], PT[0:NB[c], t % 2, c * P:(c + 1) * P],
                                     VX[0:NB[c], ds(b * 2 + l, 1), 3 * c:3 * c + 3, :].rearrange("p o c j -> p (o c j)"),
                                     start=(c == 0), stop=(c == NCH - 1), skip_group_check=True)
                        ins.then_inc(pv_ready, 1)
                pe.wait_ge(o_taken, b * (2 * TPB) + (l + 1) * TPB)
                flip_tiles(lambda t: OT[:, t, :], b * NFL + FL[f"o{l}"])
                pe.wait_ge(flip_taken, b * NFL + (FL[f"o{l}"] + 1))
                pe.wait_ge(prod_taken, b * NPD + PD[f"out{l}"])
                project(SQ[:, 4 * l + 3, :])

            def project(w, src=FX, width=D, tiles=range(TPB)):
                for i, t in enumerate(tiles):
                    ins = mm(PROD[:, i * width:(i + 1) * width], src[:, t * P:(t + 1) * P], w, start=True, stop=True)
                ins.then_inc(prod_ready, 1)

            def mixture(b):
                pe.wait_ge(xn_ready, b * 4 + 2)
                flip_tiles(lambda t: XN[:, t, :], b * NFL + FL["ln1"])
                pe.wait_ge(flip_taken, b * NFL + (FL["ln1"] + 1))
                pe.wait_ge(prod_taken, b * NPD + PD["logits"])
                project(GATE[:, :], width=E)

                def up(e):
                    pe.wait_ge(silu_ready, b * (E + 1) + max(e - 1, 0))
                    mm(SB_[e % 2][:, :], UPW[:, e, :], FX[:, :], start=True, stop=True).then_inc(up_ready, 1)

                up(0)
                up(1)
                pe.wait_ge(comb_ready, b + 1)
                for t in range(TPB):
                    ins = nc.tensor.transpose(FLIP[0:E + 1, t * P:(t + 1) * P], CM[:, t, :], ident)
                ins.then_inc(flip_ready, 1)
                pe.wait_ge(comb3_ready, b + 1)
                pe.wait_ge(prod_taken, b * NPD + PD["comb3"])
                for t in range(TPB):
                    ins = mm(PROD[0:3 * E, t * P:(t + 1) * P], C3[:, t, :], IDB[:, :], start=True, stop=True)
                ins.then_inc(prod_ready, 1)
                pe.wait_ge(prod_taken, b * NPD + (PD["comb3"] + 1))

                def spread(e):
                    pe.wait_ge(hs_ready, b * E + max(e - 1, 0))
                    mm(TB_[e % 2][:, :], SELB[0:3 * E, e, :], C3T[:, :], start=True, stop=True).then_inc(cb_ready, 1)

                spread(0)
                for e in range(E + 1):
                    if 2 <= e + 1 <= E:
                        up(e + 1)
                    if e + 1 < E:
                        spread(e + 1)
                    if e < E:
                        pe.wait_ge(hs_ready, b * E + (e + 1))
                        h, w = HS[:, e % 2, :], DNW[:, e, :]
                    else:
                        pe.wait_ge(silu_ready, (b + 1) * (E + 1))
                        h, w = SL[:, e % 2, :], SQ[:, 9, :]
                    for t in range(TPB):
                        ins = mm(OB[:, t * P:(t + 1) * P], h[:, t * P:(t + 1) * P], w,
                                 start=(e == 0 and t == 0), stop=False, skip_group_check=True)
                    ins.then_inc(down_done, 1)
                for t in range(TPB):
                    ins = mm(OB[:, t * P:(t + 1) * P], CMT[:, t * P:(t + 1) * P], DB[:, :], start=False, stop=True, skip_group_check=True)
                ins.then_inc(y_ready, 1)

            with pe.Fori(0, B) as b:
                attention(b, 0)
                mixture(b)
                attention(b, 1)
                pe.wait_ge(xn_ready, b * 4 + 4)
                flip_tiles(lambda t: XN[:, t, :], b * NFL + FL["ln4"])
                pe.wait_ge(flip_taken, b * NFL + (FL["ln4"] + 1))
                for j in range(2):
                    pe.wait_ge(prod_taken, b * NPD + PD[f"qkv{j}"])
                    project(QKVT[:, :], width=2 * D, tiles=range(2 * j, 2 * j + 2))

            for s in range(B):
                pe.wait_ge(ao_ready, s + 1)
                flip_tiles(lambda t: AO[:, s * TPB + t, :], B * NFL + 2 * s)
                pe.wait_ge(flip_taken, B * NFL + 2 * s + 1)
                pe.wait_ge(prod_taken, B * NPD + 2 * s)
                project(SQ[:, 8, :])
                pe.wait_ge(xn_ready, 4 * B + s + 1)
                flip_tiles(lambda t: XL[:, s * TPB + t, :], B * NFL + 2 * s + 1)
                pe.wait_ge(flip_taken, B * NFL + 2 * s + 2)
                pe.wait_ge(prod_taken, B * NPD + 2 * s + 1)
                project(RT[:, :], src=QT, width=E)
            pe.wait_ge(cb2_ready, 1)
            pe.wait_ge(prod_taken, B * NPD + 2 * B)
            cb = CB[:, :, :].rearrange("p t e -> p (t e)")
            mm(PROD[:, 0:NT * E], BEFB[:, :], cb[:, NT * E:2 * NT * E], start=True, stop=False)
            for j in range(1, NT):
                ins = mm(PROD[:, 0:NT * E], ONEB[:, :], cb[:, (NT - j) * E:(2 * NT - j) * E], start=False, stop=(j == NT - 1))
            ins.then_inc(rank_ready, 1)

            eb = [TB_[0], TB_[1], FLIP, PROD]
            half = CAP // 2
            pe.wait_ge(slots_ready, 1)
            with pe.Fori(0, E // 2) as pair:
                for i in range(2):
                    pe.wait_ge(xe_loaded[i], pair * 16 + 16)
                    pe.wait_ge(xt_ready, pair * 2 + i)
                    for c in range(XT_TILES):
                        ins = nc.tensor.transpose(SB_[c // 4][:, (c % 4) * P:(c % 4 + 1) * P], XE[:, i, c, :], ident)
                    ins.then_inc(xe_flipped, 1)
                    pe.wait_ge(w_loaded[i], pair * 32 + 32)
                    pe.wait_ge(xt_ready, pair * 2 + (i + 1))
                    for q in range(2 * FC):
                        pe.wait_ge(gelu_ready, pair * (4 * FC) + max(2 * FC * i + q - 3, 0))
                        mm(eb[q % 4][:, 0:half], W1[:, i, (q // 2) * P:(q // 2 + 1) * P],
                           XT[:, i, (q % 2) * half:(q % 2 + 1) * half], start=True, stop=True).then_inc(eup_ready, 1)
                    pe.wait_ge(gelu_ready, pair * (4 * FC) + 2 * FC * (i + 1))
                    pe.wait_ge(ye_ready, pair * 2 + i)
                    for c in range(XT_TILES):
                        dst = OB[:, c * P:(c + 1) * P] if c < 4 else SB_[2][:, 0:P]
                        for f in range(FC):
                            ins = mm(dst, GT[i][:, f, c * P:(c + 1) * P], W2[:, i, f, :], start=(f == 0), stop=(f == FC - 1))
                    ins.then_inc(edown_ready, 1)


def kernel(**inputs):
    import numpy as np
    import concourse.bacc as bacc
    from concourse.bass_utils import run_bass_kernel_spmd

    a = {k: np.asarray(v) for k, v in inputs.items()}
    t = np.ascontiguousarray

    def square(w):
        return w.T
    zero = np.zeros(D, np.float32)
    consts, at = shape_constants()
    sq = [a["L0_xattn_Wq"].T, a["L0_xattn_Wk"].T, a["L0_xattn_Wv"].T, a["L0_xattn_Wo"].T,
          a["L1_xattn_w_q"].T, a["L1_xattn_w_k"].T, a["L1_xattn_w_v"].T, a["L1_xattn_w_o"].T,
          a["L1_ffn_proj_weight"].T, a["L0_ffn_sh_down_w"]]
    cols = [a["L0_xattn_bq"], a["L0_xattn_bk"], a["L0_xattn_bv"], zero, a["L1_ffn_ln1_weight"], a["L1_ffn_ln1_bias"],
            a["L1_ffn_ln2_weight"], a["L1_ffn_ln2_bias"], *a["L0_ffn_up_b"], a["L0_ffn_sh_up_b"]]
    g = [a["g_xattn"][0], a["g_ffn"][0], a["g_xattn"][1], a["g_ffn"][1]]
    arrays = {
        "x": a["x"].reshape(B * S, D),
        "ctx_t": a["ctx_1024"].transpose(2, 0, 1),
        "mask_b": a["mask_Bx1xSxS2_if1"].reshape(B * S, KEYS),
        "mask_1": a["mask_1x1xSxS2_if1"].reshape(S, KEYS),
        "consts": consts,
        "sq": np.stack(sq, 1),
        "gate": a["L0_ffn_gate_w"].T,
        "up_w": np.concatenate([a["L0_ffn_up_w"], a["L0_ffn_sh_up_w"][None]]).transpose(1, 0, 2),
        "down_w": a["L0_ffn_down_w"].transpose(1, 0, 2),
        "cols": np.stack(cols, 1),
        "bo_rows": np.broadcast_to(a["L0_xattn_bo"], (P, D)),
        "down_rows": np.concatenate([a["L0_ffn_down_b"], a["L0_ffn_sh_down_b"][None]]),
        "gates": np.broadcast_to(np.stack(g), (P, 4)),
        "qkv_t": a["L1_ffn_qkv_weight"].T,
        "router": a["L1_ffn_router_weight"],
        "moe_w1": a["L1_ffn_moe_w1"].transpose(1, 0, 2),
        "moe_w2": a["L1_ffn_moe_w2"].reshape(E, FC, P, D).transpose(2, 0, 1, 3),
    }
    nc = bacc.Bacc("TRN2", target_bir_lowering=False, num_devices=1)
    arrays = {n: t(v) for n, v in arrays.items()}
    args = {n: nc.dram_tensor(n, v.shape, mybir.dt.from_np(v.dtype), kind="ExternalInput").ap() for n, v in arrays.items()}
    out = nc.dram_tensor("out", (B * S, D), mybir.dt.float32, kind="ExternalOutput").ap()
    gated_layers_kernel(nc, at=at, out=out, **args)
    r = run_bass_kernel_spmd(nc, [arrays], core_ids=[0])
    return r.results[0]["out"].reshape(B, S, D)
```

```python
import concourse.bass as bass
from concourse import mybir
from contextlib import ExitStack

B, S, D, P = 4, 512, 128, 128
TPB = S // P
NT = B * TPB
H, DK, KEYS = 16, 8, 77
HK = H * KEYS
HG = 4
NKC = 3
CR = -(-4 * KEYS // NKC)
CSTART = [0, CR, 4 * KEYS - CR]
NCH = HG * NKC
GROUPS = [(0, 6), (6, 6), (12, 4)]
NA = 2 * B
E = 8
CAP = -(-(B * S * 2 * 5) // (E * 4))
XT_TILES = CAP // P
FC = 4
KV = 8
BANK = 512
SCALE = float(DK) ** -0.5


def shape_constants():
    import numpy as np
    p = np.arange(P)
    d = np.arange(D)
    vmask = np.zeros((P, NKC, D))
    for i, c0 in enumerate(CSTART):
        new = p + c0 >= (CSTART[i - 1] + CR if i else 0)
        vmask[:, i, :] = ((p[:, None] + c0) // KEYS == d // DK % 4) & new[:, None] & (p < CR)[:, None]
    parts = {
        "ident": np.eye(P),
        "hmask": (p[:, None] // DK == np.arange(H)) * SCALE,
        "vmask": vmask.reshape(P, NKC * D),
        "iota": np.broadcast_to(np.arange(E), (P, E)),
        "before": p[:, None] < p,
        "ones": np.ones((P, P)),
    }
    at, start = {}, 0
    for k, a in parts.items():
        at[k] = (start, start + a.shape[1])
        start += a.shape[1]
    return np.ascontiguousarray(np.concatenate(list(parts.values()), 1).astype(np.float32)), at


def gated_layers_kernel(nc, x, ctx_t, mask_b, mask_1, consts, at, sq, gate, up_w, down_w, cols, rows_b,
                        down_rows, gates, qkv_t, router, moe_w1, moe_w2, out):
    f32, bf16, i32, u32 = mybir.dt.float32, mybir.dt.bfloat16, mybir.dt.int32, mybir.dt.uint32
    ALU, ACT, AX = mybir.AluOpType, mybir.ActivationFunctionType, mybir.AxisListType
    ds = bass.ds

    SLOTS = range(B + 7)
    NU = E + 1
    UNITS = {1: (0, 1, 2), 2: (3, 4, 5), 3: (6, 7, 8)}

    def mix(k):
        return k - 2 if 0 <= k - 2 < B else None

    def inner(k):
        return k - 6 if 0 <= k - 6 < B else None

    def tail(k):
        return k - 7 if 0 <= k - 7 < B else None

    uses = ["prep0", "flipP0", "q0"]
    for k in SLOTS:
        if tail(k) is not None:
            uses += [f"flipA{tail(k)}", f"proj{tail(k)}"]
        if mix(k) is not None:
            uses += [f"flipM{mix(k)}", f"gate{mix(k)}"]
        if k + 1 < NA:
            uses += [f"prep{k + 1}"]
        if mix(k) is not None:
            uses += [f"flipC{mix(k)}"]
        if inner(k) is not None:
            uses += [f"flipQ{inner(k)}", f"qkva{inner(k)}", f"qkvb{inner(k)}"]
        if tail(k) is not None:
            uses += [f"flipX{tail(k)}"]
        if k + 1 < NA:
            uses += [f"flipP{k + 1}"]
        if tail(k) is not None:
            uses += [f"router{tail(k)}"]
        if 1 <= k <= NA:
            uses += [f"out{k - 1}"]
        if k + 1 < NA:
            uses += [f"q{k + 1}"]
    M = {n: i for i, n in enumerate(uses)}

    ctx = ExitStack()
    with ctx:
        def sb(name, shape, dt=f32):
            return ctx.enter_context(nc.sbuf_tensor(name, shape, dt))

        def sem(name):
            return ctx.enter_context(nc.semaphore(name))

        slot_x = nc.dram_tensor("slot_x", [E * CAP, D], f32, kind="Internal").ap()
        slot_y = nc.dram_tensor("slot_y", [E * CAP, D], f32, kind="Internal").ap()

        X = sb("X", [P, NT, D])
        Z = sb("Z", [P, NT, D])
        QKV = sb("QKV", [P, B, TPB * KV, 4 * DK])
        XL = sb("XL", [P, NT, D])
        CST = sb("CST", [P, consts.shape[1]])
        SQ = sb("SQ", [P, 10, D])
        GATE = sb("GATE", [P, E])
        RT = sb("RT", [P, E])
        UPW = sb("UPW", [P, NU, P])
        DNW = sb("DNW", [P, E, D])
        QKVT = sb("QKVT", [P, 2 * D])
        COLS = sb("COLS", [P, cols.shape[1]])
        ROWS = sb("ROWS", [P, 2, D])
        DB = sb("DB", [E + 1, D])
        TG = sb("TG", [P, 4])
        CTX = sb("CTX", [P, B, KEYS])
        CTX4 = sb("CTX4", [P, B, 4, KEYS])
        KT = sb("KT", [P, KEYS])
        KEXP = sb("KEXP", [P, 2, HK])
        BVM = sb("BVM", [P, NKC, D])
        VX = sb("VX", [P, 3, NKC, D])
        MZB = sb("MZB", [P, NT, KEYS], i32)
        MZ1 = sb("MZ1", [P, TPB, KEYS], i32)
        ANY = sb("ANY", [P, 2])
        ANYI = sb("ANYI", [1, 2], i32)
        NEG = sb("NEG", [P, 2])
        HALF = sb("HALF", [P, TPB])
        BEFB = sb("BEFB", [P, P], bf16)
        ONEB = sb("ONEB", [P, P], bf16)
        ST = sb("ST", [P, 2, TPB, 6])
        MV = sb("MV", [P, 2, TPB, 2])
        VE = sb("VE", [P, 2, TPB])
        RS = sb("RS", [P, 2, TPB])
        XP = sb("XP", [P, TPB, D])
        XM = sb("XM", [P, TPB, D])
        XQ = sb("XQ", [P, TPB, D])
        FP = sb("FP", [P, S])
        FM = sb("FM", [P, S])
        FQ = sb("FQ", [P, S])
        FA = sb("FA", [P, S])
        FR = sb("FR", [P, S])
        OF = sb("OF", [P, S])
        QT = sb("QT", [P, 2, S])
        MX = sb("MX", [P, H])
        PR = sb("PR", [P, 2, HK])
        PT = sb("PT", [P, NCH, S])
        RD = sb("RD", [P, S])
        XR = sb("XR", [P, TPB, D])
        GBO = sb("GBO", [P, D])
        LG = sb("LG", [P, NT, E])
        M8 = sb("M8", [P, NT, E])
        I8 = sb("I8", [P, NT, E], u32)
        IF = sb("IF", [P, NT, 2])
        OH = sb("OH", [P, 2, NT, E])
        LM = sb("LM", [P, TPB, E])
        EX = sb("EX", [P, TPB, E])
        CM = sb("CM", [P, TPB, E + 1])
        CW = sb("CW", [P, TPB, E])
        DN = sb("DN", [P, TPB])
        RC = sb("RC", [P, TPB])
        CMT = sb("CMT", [E + 1, S])
        SL = sb("SL", [P, 2, S])
        YA = sb("YA", [P, TPB, D])
        AO = sb("AO", [P, TPB, D])
        PRD = sb("PRD", [P, B, S])
        XE = sb("XE", [P, 2, XT_TILES, D])
        XT = sb("XT", [P, 2, CAP])
        YS = sb("YS", [P, 2, XT_TILES, D])
        W1 = sb("W1", [P, 2, FC * P])
        W2 = sb("W2", [P, 2, FC, D])
        SC = sb("SC", [P, B, TPB * H])
        SM = sb("SM", [P, TPB * H])
        SR = sb("SR", [P, TPB * H])
        CB = sb("CB", [P, 2 * NT, E], bf16)
        RK = sb("RK", [P, NT, E])
        TK = sb("TK", [P, NT, E])
        SLT = sb("SLT", [P, 4, NT])
        WT = sb("WT", [P, 2, NT])
        SCI = sb("SCI", [P, NT, 2], u32)
        GAI = sb("GAI", [P, NT, 2], u32)
        ZERO = sb("ZERO", [P, D])
        pt_flat = PT[:, :, :].rearrange("p a k -> p (a k)")
        GT = [pt_flat[:, i * FC * CAP:(i + 1) * FC * CAP].rearrange("p (f n) -> p f n", f=FC) for i in range(2)]
        GA = QKV[:, :, :, :].rearrange("p s n d -> p (s n d)").rearrange("p (t k d) -> p t k d", t=NT, k=2)

        def const(name, rows=P):
            return CST[0:rows, at[name][0]:at[name][1]]

        ident = const("ident")
        vmask = const("vmask").rearrange("p (i d) -> p i d", i=NKC)
        col = {n: COLS[:, i:i + 1] for i, n in enumerate(
            ["bq0", "bk0", "zero", "ln1w", "ln1b", "ln2w", "ln2b"] + [f"up{e}" for e in range(NU)])}

        S0, S1, T_, NUM, DEN, U_, Y_, M_ = [ctx.enter_context(nc.psum_tensor(n, [P, BANK], f32))
                                            for n in ("S0", "S1", "T", "NUM", "DEN", "U", "Y", "M")]
        SBK = [S0, S1]

        names = """small_loaded masks_loaded att_loaded x_loaded rest_loaded ffn_loaded zero_ready slots_zeroed
            consts_ready ctx4_ready pool_ready tanh_ready gbo_ready maskz_ready any_ready anysum_ready anyint_ready hidden0 hidden1
            kt_ready kexp_ready vx_ready xr_ready dve_done var_ready rstd_ready
            xp_ready xm_ready xq_ready xl_ready m_ready m_taken scores_ready scores_taken probs_ready
            ptrans_ready pt_ready pv_ready o_ready x_updated z_ready
            exp_in exp_out comb_ready up_ready silu_ready down_ready y_taken
            in_scores in_exp ao_ready top_in top_exp cb_ready rank_ready slots_ready scattered
            xe_loaded0 xe_loaded1 w_loaded0 w_loaded1 y_stored0 y_stored1 xe_flipped xt_ready eup_ready gelu_ready
            edown_ready ye_ready gathered0 gathered1 gathered2 gathered3 final_ready out_stored""".split()
        sm = {n: sem(n) for n in names}
        (small_loaded, masks_loaded, att_loaded, x_loaded, rest_loaded, ffn_loaded, zero_ready, slots_zeroed,
         consts_ready, ctx4_ready, pool_ready, tanh_ready, gbo_ready, maskz_ready, any_ready, anysum_ready, anyint_ready, hidden0, hidden1,
         kt_ready, kexp_ready, vx_ready, xr_ready, dve_done, var_ready, rstd_ready,
         xp_ready, xm_ready, xq_ready, xl_ready, m_ready, m_taken, scores_ready, scores_taken, probs_ready,
         ptrans_ready, pt_ready, pv_ready, o_ready, x_updated, z_ready,
         exp_in, exp_out, comb_ready, up_ready, silu_ready, down_ready, y_taken,
         in_scores, in_exp, ao_ready, top_in, top_exp, cb_ready, rank_ready, slots_ready, scattered) = list(sm.values())[:57]
        xe_loaded, w_loaded, y_stored = ([sm[f"{n}{i}"] for i in range(2)] for n in ("xe_loaded", "w_loaded", "y_stored"))
        xe_flipped, xt_ready, eup_ready, gelu_ready, edown_ready, ye_ready = (
            sm[n] for n in ("xe_flipped", "xt_ready", "eup_ready", "gelu_ready", "edown_ready", "ye_ready"))
        gathered = [sm[f"gathered{s}"] for s in range(B)]
        final_ready, out_stored = sm["final_ready"], sm["out_stored"]

        def headed(ap, n):
            return ap.rearrange("p (h k) -> p h k", h=n)

        def xs(b):
            return X[:, b * TPB:(b + 1) * TPB, :].rearrange("p t d -> p (t d)")

        def wait(eng, semaphore, value):
            if value > 0:
                eng.wait_ge(semaphore, value)

        block = ctx.enter_context(nc.Block())

        @block.sync
        def _(sp):
            sp.dma_start(X[:, 0:TPB, :], x[0:S, :].rearrange("(t p) d -> p t d", p=P)).then_inc(x_loaded, 16)
            sp.dma_start(CST[:, :], consts).then_inc(small_loaded, 16)
            sp.dma_start(CTX[:, :, :], ctx_t).then_inc(small_loaded, 16)
            sp.dma_start(COLS[:, :], cols).then_inc(small_loaded, 16)
            sp.dma_start(ROWS[:, :, :], rows_b).then_inc(small_loaded, 16)
            sp.dma_start(TG[:, :], gates).then_inc(small_loaded, 16)
            sp.dma_start(SQ[:, :, :], sq).then_inc(att_loaded, 16)
            sp.dma_start(MZB[:, :, :], mask_b.rearrange("(t p) k -> p t k", p=P)).then_inc(masks_loaded, 16)
            sp.dma_start(MZ1[:, :, :], mask_1.rearrange("(t p) k -> p t k", p=P)).then_inc(masks_loaded, 16)
            sp.dma_start(X[:, TPB:NT, :], x[S:B * S, :].rearrange("(t p) d -> p t d", p=P)).then_inc(rest_loaded, 16)
            sp.dma_start(GATE[:, :], gate).then_inc(ffn_loaded, 16)
            sp.dma_start(UPW[:, :, :], up_w).then_inc(ffn_loaded, 16)
            sp.dma_start(DNW[:, :, :], down_w).then_inc(ffn_loaded, 16)
            sp.dma_start(DB[:, :], down_rows).then_inc(ffn_loaded, 16)
            sp.dma_start(QKVT[:, :], qkv_t).then_inc(ffn_loaded, 16)
            sp.dma_start(RT[:, :], router).then_inc(ffn_loaded, 16)
            sp.wait_ge(zero_ready, 1)
            sp.dma_start(slot_x.rearrange("(p q) d -> p q d", p=P),
                         ZERO[:, :].unsqueeze(1).broadcast_to([P, E * CAP // P, D])).then_inc(slots_zeroed, 16)
            for i in range(2):
                sp.dma_start(W1[:, i, :], moe_w1[:, i]).then_inc(w_loaded[i], 16)
                sp.dma_start(W2[:, i, :, :], moe_w2[:, i]).then_inc(w_loaded[i], 16)
            sp.wait_ge(scattered, 16 * 2 * NT)
            slots = slot_x.rearrange("(e c p) d -> p e c d", c=XT_TILES, p=P)
            rows = slot_y.rearrange("(e c p) d -> p e c d", c=XT_TILES, p=P)
            for i in range(2):
                sp.dma_start(XE[:, i, :, :], slots[:, i]).then_inc(xe_loaded[i], 16)
            with sp.Fori(0, E // 2 - 1) as pair:
                for i in range(2):
                    nxt = ds(pair * 2 + (2 + i), 1)
                    sp.wait_ge(xe_flipped, pair * 2 + (i + 1))
                    sp.dma_start(XE[:, i:i + 1, :, :], slots[:, nxt]).then_inc(xe_loaded[i], 16)
                    sp.wait_ge(ye_ready, pair * 2 + (i + 1))
                    sp.dma_start(rows[:, ds(pair * 2 + i, 1)], YS[:, i:i + 1, :, :]).then_inc(y_stored[i], 16)
                    sp.dma_start(W1[:, i:i + 1, :], moe_w1[:, nxt]).then_inc(w_loaded[i], 16)
                    sp.dma_start(W2[:, i:i + 1, :, :], moe_w2[:, nxt]).then_inc(w_loaded[i], 16)
            for i in range(2):
                sp.wait_ge(ye_ready, E - 1 + i)
                sp.dma_start(rows[:, E - 2 + i], YS[:, i, :, :]).then_inc(y_stored[i], 16)
            for s in range(B):
                sp.wait_ge(final_ready, s + 1)
                sp.dma_start(out[s * S:(s + 1) * S, :].rearrange("(t p) d -> p t d", p=P),
                             X[:, s * TPB:(s + 1) * TPB, :]).then_inc(out_stored, 16)
            sp.wait_ge(out_stored, 16 * B)

        @block.gpsimd
        def _(pool):
            nc.gpsimd.memset(HALF[:, :], -0.5)
            nc.gpsimd.memset(NEG[:, 0:1], -60000.0)
            nc.gpsimd.memset(NEG[:, 1:2], -1e9)
            nc.gpsimd.memset(CM[:, :, E:E + 1], 1.0)
            nc.gpsimd.memset(CB[:, 0:NT, :], 0.0)
            nc.gpsimd.memset(ZERO[:, :], 0.0).then_inc(zero_ready, 1)

            norms = [0]

            def rstd():
                n = norms[0]
                norms[0] += 1
                pool.wait_ge(var_ready, n + 1)
                nc.gpsimd.tensor_tensor(RS[:, n % 2, :], VE[:, n % 2, :], HALF[:, :], ALU.pow).then_inc(rstd_ready, 1)

            def keys(k):
                pool.wait_ge(kt_ready, k + 1)
                wait(pool, scores_ready, 3 * TPB * (k - 1))
                nc.gpsimd.tensor_tensor(headed(KEXP[:, k % 2, :], H), KT[:, :].unsqueeze(1).broadcast_to([P, H, KEYS]),
                                        const("hmask").unsqueeze(2).broadcast_to([P, H, KEYS]), ALU.mult).then_inc(kexp_ready, 1)

            pool.wait_ge(zero_ready, 1)
            rstd()
            pool.wait_ge(small_loaded, 16 * 5)
            nc.gpsimd.tensor_copy(CTX4[:, :, :, :], CTX[:, :, :].unsqueeze(2).broadcast_to([P, B, 4, KEYS])).then_inc(ctx4_ready, 1)
            for i in range(NKC):
                ins = nc.gpsimd.tensor_tensor(BVM[:, i, :], vmask[:, i, :], ROWS[:, 1, :], ALU.mult)
            ins.then_inc(consts_ready, 1)
            keys(0)
            pool.wait_ge(masks_loaded, 32)
            nc.gpsimd.tensor_scalar(MZB[:, :, :], MZB[:, :, :], 0.0, None, ALU.is_equal)
            nc.gpsimd.tensor_scalar(MZ1[:, :, :], MZ1[:, :, :], 0.0, None, ALU.is_equal).then_inc(maskz_ready, 1)
            pool.wait_ge(tanh_ready, 1)
            nc.gpsimd.tensor_scalar(GBO[:, :], ROWS[:, 0, :], TG[:, 0:1], None, ALU.mult).then_inc(gbo_ready, 1)
            nc.gpsimd.tensor_copy(BEFB[:, :], const("before"))
            nc.gpsimd.tensor_copy(ONEB[:, :], const("ones")).then_inc(pool_ready, 1)
            pool.wait_ge(gbo_ready, 1)
            pool.wait_ge(x_loaded, 16)
            pool.wait_ge(rest_loaded, 16)
            for k in SLOTS:
                if inner(k) is not None:
                    rstd()
                if tail(k) is not None:
                    rstd()
                if k + 1 < NA:
                    keys(k + 1)
                    rstd()
                if 1 <= k <= B:
                    b = k - 1
                    wait(pool, m_taken, M[f"out{b - 1}"] + 1 if b else 0)
                    nc.gpsimd.tensor_tensor(XR[:, :, :], X[:, b * TPB:(b + 1) * TPB, :],
                                            GBO[:, :].unsqueeze(1).broadcast_to([P, TPB, D]), ALU.add).then_inc(xr_ready, 1)
                if 1 <= k <= NA:
                    rstd()
            pool.wait_ge(slots_zeroed, 16)
            pool.wait_ge(slots_ready, 1)
            for T in range(NT):
                for j in range(2):
                    nc.gpsimd.indirect_dma_start(
                        out=slot_x, out_offset=bass.IndirectOffsetOnAxis(ap=SCI[:, T, j:j + 1], axis=0),
                        in_=XL[:, T, :], in_offset=None, bounds_check=E * CAP - 1, oob_is_err=False).then_inc(scattered, 16)
            for i in range(2):
                pool.wait_ge(y_stored[i], 16 * (E // 2))
            for T in range(NT):
                for j in range(2):
                    nc.gpsimd.indirect_dma_start(
                        out=GA[:, T, j, :], out_offset=None, in_=slot_y,
                        in_offset=bass.IndirectOffsetOnAxis(ap=GAI[:, T, j:j + 1], axis=0)).then_inc(gathered[T // TPB], 16)

        @block.scalar
        def _(act):
            act.wait_ge(small_loaded, 16 * 5)
            nc.scalar.activation(TG[:, :], TG[:, :], ACT.Tanh).then_inc(tanh_ready, 1)

            def m_out(use, dst, bias=None, scale=1.0, rows=P):
                act.wait_ge(m_ready, M[use] + 1)
                if bias is None:
                    nc.scalar.activation(dst, M_[0:rows, :], ACT.Copy).then_inc(m_taken, 1)
                else:
                    nc.scalar.activation(dst, M_[0:rows, :], ACT.Identity, bias=bias, scale=scale).then_inc(m_taken, 1)

            def queries(k):
                wait(act, scores_ready, 3 * TPB * (k - 1))
                m_out(f"q{k}", QT[:, k % 2, :], bias=col["bq0" if k < B else "zero"])

            def chunks(tau):
                k, t = tau // TPB, tau % TPB
                wait(act, pv_ready, k)
                for j in range(3):
                    act.wait_ge(ptrans_ready, 3 * tau + j + 1)
                    nc.scalar.activation(PT[0:CR, 4 * j:4 * j + 4, t * P:(t + 1) * P],
                                         T_[0:CR, :].rearrange("p (c n) -> p c n", c=4), ACT.Copy).then_inc(pt_ready, 1)

            def silu(b, e):
                n = NU * b + e
                act.wait_ge(up_ready, n + 1)
                wait(act, down_ready, n - 1)
                nc.scalar.activation(SL[:, n % 2, :], U_[:, :], ACT.Silu, bias=col[f"up{(e - 1) % NU}"]).then_inc(silu_ready, 1)

            m_out("flipP0", FP[:, :])
            queries(0)
            for k in SLOTS:
                mb, ib, tb = mix(k), inner(k), tail(k)
                for step in range(TPB):
                    tau = TPB * k + step
                    if 1 <= tau <= TPB * NA:
                        chunks(tau - 1)
                    if tau < TPB * NA:
                        act.wait_ge(scores_taken, 3 * (tau + 1))
                        nc.scalar.activation(PR[:, tau % 2, :], PR[:, tau % 2, :], ACT.Exp).then_inc(probs_ready, 1)
                    if step == 0:
                        if tb is not None:
                            m_out(f"flipA{tb}", FA[:, :])
                        if mb is not None:
                            m_out(f"flipM{mb}", FM[:, :])
                            act.wait_ge(exp_in, mb + 1)
                            nc.scalar.activation(EX[:, :, :], EX[:, :, :], ACT.Exp).then_inc(exp_out, 1)
                            silu(mb, 0)
                    if step == 1:
                        if mb is not None:
                            m_out(f"flipC{mb}", CMT[:, :], rows=E + 1)
                        if ib is not None:
                            m_out(f"flipQ{ib}", FQ[:, :], bias=col["ln1b"], scale=col["ln1w"])
                            m_out(f"qkva{ib}", QKV[:, ib, 0:2 * KV, :].rearrange("p n d -> p (n d)"))
                            m_out(f"qkvb{ib}", QKV[:, ib, 2 * KV:4 * KV, :].rearrange("p n d -> p (n d)"))
                        if tb is not None:
                            m_out(f"flipX{tb}", FR[:, :], bias=col["ln2b"], scale=col["ln2w"])
                    if step == 2:
                        if k + 1 < NA:
                            m_out(f"flipP{k + 1}", FP[:, :])
                        if ib is not None:
                            act.wait_ge(in_scores, ib + 1)
                            nc.scalar.activation(SC[:, 0:ib + 1, :], SC[:, 0:ib + 1, :], ACT.Exp, scale=SCALE).then_inc(in_exp, 1)
                    if step == 3 and k + 1 < NA:
                        queries(k + 1)
                    if mb is not None:
                        for e in UNITS.get(step, ()):
                            if e + 1 < NU:
                                silu(mb, e + 1)
            act.wait_ge(top_in, 1)
            nc.scalar.activation(WT[:, 1, :], WT[:, 1, :], ACT.Exp).then_inc(top_exp, 1)
            half = CAP // 2
            with act.Fori(0, E // 2) as pair:
                for i in range(2):
                    for q in range(2 * FC):
                        act.wait_ge(eup_ready, pair * (4 * FC) + (i * 2 * FC + q + 1))
                        nc.scalar.activation(GT[i][:, q // 2, (q % 2) * half:(q % 2 + 1) * half],
                                             [T_, DEN, U_, M_][q % 4][:, 0:half], ACT.Gelu).then_inc(gelu_ready, 1)

        @block.vector
        def _(dve):
            links = [0]

            def link(ins):
                links[0] += 1
                ins.then_inc(dve_done, 1)
                dve.wait_ge(dve_done, links[0])

            norms = [0]

            def stats(src):
                n = norms[0] % 2
                for t in range(TPB):
                    ins = nc.vector.bn_stats(ST[:, n, t, :], src(t))
                link(ins)
                for t in range(TPB):
                    ins = nc.vector.bn_aggr(MV[:, n, t, :], ST[:, n, t, :])
                link(ins)
                nc.vector.tensor_scalar(VE[:, n, :], MV[:, n, :, 1], 1e-5, None, ALU.add).then_inc(var_ready, 1)

            def apply(src, dst, done):
                n = norms[0] % 2
                norms[0] += 1
                dve.wait_ge(rstd_ready, norms[0])
                for t in range(TPB):
                    ins = nc.vector.tensor_scalar(dst(t), src(t), MV[:, n, t, 0:1], RS[:, n, t:t + 1], ALU.subtract, ALU.mult)
                ins.then_inc(done, 1)

            def tile_of(buf, b):
                return lambda t: buf[:, b * TPB + t, :]

            def prep(k):
                dve.wait_ge(m_ready, M[f"prep{k}"] + 1)
                wait(dve, kexp_ready, k)
                nc.vector.tensor_scalar(KT[:, :], M_[:, 0:KEYS], col["bk0" if k < B else "zero"], None, ALU.add).then_inc(kt_ready, 1)
                v = VX[0:CR, k % 3, :, :].rearrange("p i d -> p (i d)")
                wait(dve, pv_ready, k - 2)
                ins = nc.vector.tensor_tensor(v, M_[0:CR, P:P + NKC * D], const("vmask", CR), ALU.mult)
                ins.then_inc(m_taken, 1)
                if k < B:
                    dve.wait_ge(m_taken, M[f"prep{k}"] + 1)
                    nc.vector.tensor_tensor(v, v, BVM[0:CR, :, :].rearrange("p i d -> p (i d)"), ALU.add).then_inc(vx_ready, 1)

            def groups(tau, hidden):
                l, mz = (0, MZB[:, tau, :]) if tau < NT else (1, MZ1[:, tau % TPB, :])
                for g, (h0, n) in enumerate(GROUPS):
                    v = 3 * tau + g
                    sc = headed(SBK[v % 2][:, 0:n * KEYS], n)
                    dve.wait_ge(scores_ready, v + 1)
                    with dve.If_ne(hidden, 0):
                        nc.vector.copy_predicated(sc, mz.unsqueeze(1).broadcast_to([P, n, KEYS]),
                                                  NEG[:, l:l + 1].unsqueeze(2).broadcast_to([P, n, KEYS])).then_inc([hidden0, hidden1][l], 1)
                        dve.wait_ge([hidden0, hidden1][l], v % (3 * NT) + 1)
                    link(nc.vector.reduce_max(MX[:, h0:h0 + n], sc, AX.X))
                    if g == 0:
                        wait(dve, ptrans_ready, 3 * (tau - 1))
                    nc.vector.tensor_tensor(headed(PR[:, tau % 2, h0 * KEYS:(h0 + n) * KEYS], n), sc,
                                            MX[:, h0:h0 + n].unsqueeze(2).broadcast_to([P, n, KEYS]),
                                            ALU.subtract).then_inc(scores_taken, 1)

            def attended(k):
                dve.wait_ge(pv_ready, k + 1)
                link(nc.vector.reciprocal(RD[:, :], DEN[:, :]))
                wait(dve, m_ready, M[f"out{k - 1}"] + 1 if k else 0)
                nc.vector.tensor_tensor(OF[:, :], NUM[:, :], RD[:, :], ALU.mult).then_inc(o_ready, 1)

            def residual(k):
                l, b = k // B, k % B
                dve.wait_ge(m_ready, M[f"out{k}"] + 1)
                if l == 0:
                    dve.wait_ge(xr_ready, b + 1)
                rest = XR[:, :, :].rearrange("p t d -> p (t d)") if l == 0 else xs(b)
                nc.vector.scalar_tensor_tensor(out=xs(b), in0=M_[:, :], scalar=TG[:, 2 * l:2 * l + 1], in1=rest,
                                               op0=ALU.mult, op1=ALU.add).then_inc(m_taken, 1)
                dve.wait_ge(m_taken, M[f"out{k}"] + 1)

            def top2(LGv, T0, n):
                for T in range(n):
                    ins = nc.vector.max(M8[:, T0 + T, :], LGv[:, T, :])
                link(ins)
                for T in range(n):
                    ins = nc.vector.max_index(I8[:, T0 + T, :], M8[:, T0 + T, :], LGv[:, T, :])
                link(ins)
                link(nc.vector.tensor_copy(IF[:, T0:T0 + n, :], I8[:, T0:T0 + n, 0:2]))
                for j in range(2):
                    ins = nc.vector.tensor_tensor(OH[:, j, T0:T0 + n, :], const("iota").unsqueeze(1).broadcast_to([P, n, E]),
                                                  IF[:, T0:T0 + n, j:j + 1].broadcast_to([P, n, E]), ALU.is_equal)
                link(ins)

            def gating(b):
                dve.wait_ge(m_ready, M[f"gate{b}"] + 1)
                nc.vector.tensor_copy(LM[:, :, :].rearrange("p t e -> p (t e)"), M_[:, 0:TPB * E]).then_inc(m_taken, 1)
                dve.wait_ge(m_taken, M[f"gate{b}"] + 1)
                for t in range(TPB):
                    ins = nc.vector.max(M8[:, t, :], LM[:, t, :])
                link(ins)
                nc.vector.tensor_tensor(EX[:, :, :], LM[:, :, :], M8[:, 0:TPB, 0:1].broadcast_to([P, TPB, E]),
                                        ALU.subtract).then_inc(exp_in, 1)
                for t in range(TPB):
                    ins = nc.vector.max_index(I8[:, t, :], M8[:, t, :], LM[:, t, :])
                link(ins)
                link(nc.vector.tensor_copy(IF[:, 0:TPB, :], I8[:, 0:TPB, 0:2]))
                for j in range(2):
                    ins = nc.vector.tensor_tensor(OH[:, j, 0:TPB, :], const("iota").unsqueeze(1).broadcast_to([P, TPB, E]),
                                                  IF[:, 0:TPB, j:j + 1].broadcast_to([P, TPB, E]), ALU.is_equal)
                link(ins)
                link(nc.vector.tensor_tensor(OH[:, 0, 0:TPB, :], OH[:, 0, 0:TPB, :], OH[:, 1, 0:TPB, :], ALU.add))
                dve.wait_ge(exp_out, b + 1)
                link(nc.vector.tensor_tensor(CW[:, :, :], EX[:, :, :], OH[:, 0, 0:TPB, :], ALU.mult))
                link(nc.vector.reduce_sum(DN[:, :], CW[:, :, :], AX.X))
                link(nc.vector.tensor_scalar(DN[:, :], DN[:, :], 1e-20, None, ALU.add))
                link(nc.vector.reciprocal(RC[:, :], DN[:, :]))
                nc.vector.tensor_tensor(CM[:, :, 0:E], CW[:, :, :], RC[:, :].unsqueeze(2).broadcast_to([P, TPB, E]), ALU.mult).then_inc(comb_ready, 1)
                dve.wait_ge(comb_ready, b + 1)

            def unit(b, e):
                n = NU * b + e
                dve.wait_ge(down_ready, n + 1)
                wait(dve, y_taken, n)
                if e == 0:
                    ins = nc.vector.tensor_copy(YA[:, :, :].rearrange("p t d -> p (t d)"), Y_[:, :])
                else:
                    for t in range(TPB):
                        ins = nc.vector.scalar_tensor_tensor(out=YA[:, t, :], in0=Y_[:, t * P:(t + 1) * P], scalar=CM[:, t, e - 1:e],
                                                             in1=YA[:, t, :], op0=ALU.mult, op1=ALU.add)
                ins.then_inc(y_taken, 1)

            def mixed(b):
                dve.wait_ge(y_taken, NU * (b + 1))
                nc.vector.scalar_tensor_tensor(out=xs(b), in0=YA[:, :, :].rearrange("p t d -> p (t d)"), scalar=TG[:, 1:2],
                                               in1=xs(b), op0=ALU.mult, op1=ALU.add).then_inc(x_updated, 1)
                dve.wait_ge(x_updated, b + 1)

            def by_head(ap):
                return ap.rearrange("p (n j d) -> p n j d", j=2, d=DK)

            def kv_of(t, which):
                return QKV[:, t, :, (2 + which) * DK:(3 + which) * DK].unsqueeze(2).broadcast_to([P, TPB * KV, 2, DK])

            def inner_scores(s):
                dve.wait_ge(m_taken, M[f"qkvb{s}"] + 1)
                q = QKV[:, s, :, 0:2 * DK].rearrange("p n (j d) -> p n j d", j=2)
                for t in range(s + 1):
                    ins = nc.vector.tensor_tensor(by_head(PRD[:, t, :]), q, kv_of(t, 0), ALU.mult)
                link(ins)
                link(nc.vector.reduce_sum(SC[:, 0:s + 1, :], PRD[:, 0:s + 1, :].rearrange("p t (n d) -> p t n d", d=DK), AX.X))
                link(nc.vector.reduce_max(SM[:, :], SC[:, 0:s + 1, :].rearrange("p t n -> p n t"), AX.X))
                nc.vector.tensor_tensor(SC[:, 0:s + 1, :], SC[:, 0:s + 1, :], SM[:, :].unsqueeze(1).broadcast_to([P, s + 1, TPB * H]),
                                        ALU.subtract).then_inc(in_scores, 1)

            def inner_values(s):
                dve.wait_ge(in_exp, s + 1)
                link(nc.vector.reduce_sum(SM[:, :], SC[:, 0:s + 1, :].rearrange("p t n -> p n t"), AX.X))
                link(nc.vector.reciprocal(SR[:, :], SM[:, :]))
                link(nc.vector.tensor_tensor(SC[:, 0:s + 1, :], SC[:, 0:s + 1, :], SR[:, :].unsqueeze(1).broadcast_to([P, s + 1, TPB * H]), ALU.mult))
                ao = AO[:, :, :].rearrange("p t d -> p (t d)")
                if s:
                    dve.wait_ge(m_ready, M[f"flipA{s - 1}"] + 1)
                for t in range(s + 1):
                    dst = ao if t == 0 else PRD[:, t, :]
                    w = SC[:, t, :].rearrange("p (n j) -> p n j", j=2).unsqueeze(3).broadcast_to([P, TPB * KV, 2, DK])
                    ins = nc.vector.tensor_tensor(by_head(dst), w, kv_of(t, 1), ALU.mult)
                for t in range(1, s + 1):
                    link(ins)
                    ins = nc.vector.tensor_tensor(ao, ao, PRD[:, t, :], ALU.add)
                ins.then_inc(ao_ready, 1)
                dve.wait_ge(ao_ready, s + 1)

            def flipped(use):
                if use in M:
                    dve.wait_ge(m_ready, M[use] + 1)

            dve.wait_ge(x_loaded, 16)
            stats(tile_of(X, 0))
            dve.wait_ge(small_loaded, 16 * 5)
            dve.wait_ge(consts_ready, 1)
            apply(tile_of(X, 0), lambda t: XP[:, t, :], xp_ready)
            prep(0)
            dve.wait_ge(maskz_ready, 1)
            nc.vector.reduce_sum(ANY[:, 0:1], MZB[:, :, :].rearrange("p t k -> p (t k)"), AX.X)
            nc.vector.reduce_sum(ANY[:, 1:2], MZ1[:, :, :].rearrange("p t k -> p (t k)"), AX.X).then_inc(any_ready, 1)
            dve.wait_ge(anysum_ready, 1)
            nc.vector.tensor_copy(ANYI[:, :], Y_[0:1, 0:2]).then_inc(anyint_ready, 1)
            dve.wait_ge(anyint_ready, 1)
            hidden = [dve.alloc_register(f"hidden{l}") for l in range(2)]
            for l in range(2):
                dve.reg_load(hidden[l], ANYI[0:1, l:l + 1])
            dve.wait_ge(rest_loaded, 16)
            for k in SLOTS:
                mb, ib, tb = mix(k), inner(k), tail(k)
                for step in range(TPB):
                    tau = TPB * k + step
                    if step == 0 and ib is not None:
                        stats(tile_of(Z, ib))
                    if step == 1 and k + 1 < NA:
                        stats(tile_of(X, (k + 1) % B))
                    if k < NA:
                        groups(tau, hidden[k // B])
                    if step == 0:
                        if ib is not None:
                            flipped(f"flipQ{ib - 1}")
                            apply(tile_of(Z, ib), lambda t: XQ[:, t, :], xq_ready)
                        if tb is not None:
                            zs = Z[:, tb * TPB:(tb + 1) * TPB, :].rearrange("p t d -> p (t d)")
                            dve.wait_ge(m_ready, M[f"proj{tb}"] + 1)
                            nc.vector.tensor_tensor(zs, M_[:, :], zs, ALU.add).then_inc(m_taken, 1)
                            dve.wait_ge(m_taken, M[f"proj{tb}"] + 1)
                            stats(tile_of(Z, tb))
                            apply(tile_of(Z, tb), tile_of(XL, tb), xl_ready)
                        if mb is not None:
                            gating(mb)
                        if k + 1 < NA:
                            prep(k + 1)
                    if step == 1 and k + 1 < NA:
                        flipped(f"flipP{k}")
                        apply(tile_of(X, (k + 1) % B), lambda t: XP[:, t, :], xp_ready)
                    if step == 2:
                        if 1 <= k <= NA:
                            attended(k - 1)
                        if ib is not None:
                            inner_scores(ib)
                        if tb is not None:
                            dve.wait_ge(m_ready, M[f"router{tb}"] + 1)
                            nc.vector.tensor_copy(LG[:, tb * TPB:(tb + 1) * TPB, :].rearrange("p t e -> p (t e)"),
                                                  M_[:, 0:TPB * E]).then_inc(m_taken, 1)
                    if step == 3 and 1 <= k <= NA:
                        residual(k - 1)
                        stats(tile_of(X, (k - 1) % B))
                    if step == 3 and ib is not None:
                        inner_values(ib)
                    if mb is not None:
                        for e in UNITS.get(step, ()):
                            unit(mb, e)
                    if step == 3 and mb is not None:
                        mixed(mb)
                    if step == 3 and 1 <= k <= NA:
                        b = (k - 1) % B
                        if k - 1 < B:
                            flipped(f"flipM{b - 1}")
                            apply(tile_of(X, b), lambda t: XM[:, t, :], xm_ready)
                        else:
                            apply(tile_of(X, b), tile_of(Z, b), z_ready)
                            dve.wait_ge(z_ready, b + 1)
            dve.wait_ge(m_taken, M[f"router{B - 1}"] + 1)
            top2(LG, 0, NT)
            nc.vector.tensor_tensor(CB[:, NT:2 * NT, :], OH[:, 0, :, :], OH[:, 1, :, :], ALU.add).then_inc(cb_ready, 1)
            nc.vector.tensor_tensor(WT[:, 1, :], M8[:, :, 1], M8[:, :, 0], ALU.subtract).then_inc(top_in, 1)
            dve.wait_ge(top_exp, 1)
            link(nc.vector.tensor_scalar(SLT[:, 3, :], WT[:, 1, :], 1.0, None, ALU.add))
            link(nc.vector.reciprocal(WT[:, 0, :], SLT[:, 3, :]))
            link(nc.vector.tensor_tensor(WT[:, 1, :], WT[:, 1, :], WT[:, 0, :], ALU.mult))
            dve.wait_ge(rank_ready, 1)
            link(nc.vector.tensor_copy(RK[:, :, :].rearrange("p t e -> p (t e)"), M_[:, 0:NT * E]))
            for j in range(2):
                rank, keep, slot, far = (SLT[:, i, :] for i in range(4))
                link(nc.vector.tensor_tensor(TK[:, :, :], RK[:, :, :], OH[:, j, :, :], ALU.mult))
                link(nc.vector.reduce_sum(rank, TK[:, :, :], AX.X))
                link(nc.vector.tensor_scalar(keep, rank, float(CAP), None, ALU.is_lt))
                link(nc.vector.scalar_tensor_tensor(out=slot, in0=IF[:, :, j], scalar=float(CAP), in1=rank, op0=ALU.mult, op1=ALU.add))
                link(nc.vector.tensor_scalar(far, keep, float(-2 * E * CAP), float(2 * E * CAP), ALU.mult, ALU.add))
                nc.vector.tensor_tensor(SCI[:, :, j], far, slot, ALU.add)
                nc.vector.tensor_tensor(GAI[:, :, j], slot, keep, ALU.mult)
                ins = nc.vector.tensor_tensor(WT[:, j, :], WT[:, j, :], keep, ALU.mult)
                if j == 0:
                    link(ins)
            ins.then_inc(slots_ready, 1)

            with dve.Fori(0, E // 2) as pair:
                for i in range(2):
                    dve.wait_ge(xe_flipped, pair * 2 + (i + 1))
                    nc.vector.tensor_scalar(XT[:, i, 0:BANK], S0[:, :], col["ln2w"], col["ln2b"], ALU.mult, ALU.add)
                    nc.vector.tensor_scalar(XT[:, i, BANK:CAP], S1[:, 0:CAP - BANK], col["ln2w"], col["ln2b"],
                                            ALU.mult, ALU.add).then_inc(xt_ready, 1)
                    dve.wait_ge(edown_ready, pair * 2 + (i + 1))
                    dve.wait_ge(y_stored[i], pair * 16)
                    ys = YS[:, i, :, :].rearrange("p c d -> p (c d)")
                    nc.vector.tensor_copy(ys[:, 0:BANK], Y_[:, :])
                    nc.vector.tensor_copy(ys[:, BANK:CAP], NUM[:, 0:CAP - BANK]).then_inc(ye_ready, 1)
            for s in range(B):
                dve.wait_ge(gathered[s], 16 * 2 * TPB)
                for j in range(2):
                    for T in range(s * TPB, (s + 1) * TPB):
                        ins = nc.vector.scalar_tensor_tensor(out=Z[:, T, :], in0=GA[:, T, j, :], scalar=WT[:, j, T:T + 1], in1=Z[:, T, :],
                                                             op0=ALU.mult, op1=ALU.add)
                    link(ins)
                zs = Z[:, s * TPB:(s + 1) * TPB, :].rearrange("p t d -> p (t d)")
                nc.vector.scalar_tensor_tensor(out=xs(s), in0=zs, scalar=TG[:, 3:4], in1=xs(s), op0=ALU.mult, op1=ALU.add).then_inc(final_ready, 1)

        @block.tensor
        def _(pe):
            mm = nc.tensor.matmul

            def free(use):
                wait(pe, m_taken, M[use])

            def flip(use, src, src_ready, value):
                pe.wait_ge(src_ready, value)
                free(use)
                for t in range(TPB):
                    tile = src(t)
                    ins = nc.tensor.transpose(M_[0:tile.shape[1], t * P:(t + 1) * P], tile, ident)
                ins.then_inc(m_ready, 1)

            def project(use, src, w, width=D, tiles=range(TPB)):
                free(use)
                for i, t in enumerate(tiles):
                    ins = mm(M_[:, i * width:(i + 1) * width], src[:, t * P:(t + 1) * P], w, start=True, stop=True)
                ins.then_inc(m_ready, 1)

            def prep(k):
                l, b = k // B, k % B
                free(f"prep{k}")
                mm(M_[:, 0:KEYS], SQ[:, 4 * l + 1, :], CTX[:, b, :], start=True, stop=True)
                if k == 0:
                    pe.wait_ge(ctx4_ready, 1)
                ctx4 = CTX4[:, b, :, :].rearrange("p h k -> p (h k)")
                for i, c0 in enumerate(CSTART):
                    ins = mm(M_[0:CR, P + i * D:P + (i + 1) * D], ctx4[:, c0:c0 + CR],
                             SQ[:, 4 * l + 2, :], start=True, stop=True)
                ins.then_inc(m_ready, 1)

            def queries(k):
                pe.wait_ge(m_taken, M[f"flipP{k}"] + 1)
                free(f"q{k}")
                mm(M_[:, :], SQ[:, 4 * (k // B), :], FP[:, :], start=True, stop=True).then_inc(m_ready, 1)

            def scores(tau, g):
                k, t = tau // TPB, tau % TPB
                h0, n = GROUPS[g]
                v = 3 * tau + g
                if t == 0 and g == 0:
                    pe.wait_ge(kexp_ready, k + 1)
                    pe.wait_ge(m_taken, M[f"q{k}"] + 1)
                wait(pe, scores_taken, v - 1)
                mm(SBK[v % 2][:, 0:n * KEYS], QT[:, k % 2, t * P:(t + 1) * P], KEXP[:, k % 2, h0 * KEYS:(h0 + n) * KEYS],
                   start=True, stop=True).then_inc(scores_ready, 1)

            def chunks(tau, j):
                w = 3 * tau + j
                if j == 0:
                    pe.wait_ge(probs_ready, tau + 1)
                wait(pe, pt_ready, w)
                for c in range(4 * j, 4 * j + 4):
                    c0 = c // NKC * 4 * KEYS + CSTART[c % NKC]
                    ins = nc.tensor.transpose(T_[0:CR, (c % 4) * P:(c % 4 + 1) * P],
                                              PR[:, tau % 2, c0:c0 + CR], ident)
                ins.then_inc(ptrans_ready, 1)

            def values(k):
                pe.wait_ge(pt_ready, 3 * TPB * (k + 1))
                if k < B:
                    pe.wait_ge(vx_ready, k + 1)
                else:
                    pe.wait_ge(m_taken, M[f"prep{k}"] + 1)
                wait(pe, o_ready, k)
                for bank in (NUM, DEN):
                    for i in range(NKC):
                        for hg in range(HG):
                            w = VX[0:CR, k % 3, i, 32 * hg:32 * hg + 32] if bank is NUM else vmask[0:CR, i, 0:32]
                            ins = mm(bank[32 * hg:32 * hg + 32, :], w, PT[0:CR, hg * NKC + i, :],
                                     start=(i == 0), stop=(i == NKC - 1), tile_position=(0, 32 * hg))
                ins.then_inc(pv_ready, 1)

            def up(b, e):
                n = NU * b + e
                wait(pe, silu_ready, n)
                mm(U_[:, :], UPW[:, (e - 1) % NU, :], FM[:, :], start=True, stop=True).then_inc(up_ready, 1)

            def down(b, e):
                n = NU * b + e
                pe.wait_ge(silu_ready, n + 1)
                wait(pe, y_taken, n)
                h, w = SL[:, n % 2, :], (SQ[:, 9, :] if e == 0 else DNW[:, e - 1, :])
                for t in range(TPB):
                    ins = mm(Y_[:, t * P:(t + 1) * P], h[:, t * P:(t + 1) * P], w, start=True, stop=(e > 0))
                    if e == 0:
                        ins = mm(Y_[:, t * P:(t + 1) * P], CMT[:, t * P:(t + 1) * P], DB[:, :], start=False, stop=True)
                ins.then_inc(down_ready, 1)

            pe.wait_ge(small_loaded, 16 * 5)
            pe.wait_ge(att_loaded, 16)
            prep(0)
            flip("flipP0", lambda t: XP[:, t, :], xp_ready, 1)
            queries(0)
            pe.wait_ge(any_ready, 1)
            mm(Y_[0:1, 0:2], const("ones")[:, 0:1], ANY[:, :], start=True, stop=True).then_inc(anysum_ready, 1)
            pe.wait_ge(ffn_loaded, 16 * 6)
            for k in SLOTS:
                mb, ib, tb = mix(k), inner(k), tail(k)
                for step in range(TPB):
                    tau = TPB * k + step
                    for g in range(3):
                        if tau < TPB * NA:
                            scores(tau, g)
                        if step == 1 and g == 1 and 1 <= k <= NA:
                            values(k - 1)
                        if 1 <= tau <= TPB * NA:
                            chunks(tau - 1, g)
                    if step == 0:
                        if tb is not None:
                            flip(f"flipA{tb}", lambda t: AO[:, t, :], ao_ready, tb + 1)
                            pe.wait_ge(m_taken, M[f"flipA{tb}"] + 1)
                            project(f"proj{tb}", FA, SQ[:, 8, :])
                        if mb is not None:
                            flip(f"flipM{mb}", lambda t: XM[:, t, :], xm_ready, mb + 1)
                            pe.wait_ge(m_taken, M[f"flipM{mb}"] + 1)
                            up(mb, 0)
                            project(f"gate{mb}", FM, GATE[:, :], width=E)
                        if k + 1 < NA:
                            prep(k + 1)
                    if step == 1:
                        if mb is not None:
                            flip(f"flipC{mb}", lambda t: CM[:, t, :], comb_ready, mb + 1)
                            pe.wait_ge(m_taken, M[f"flipC{mb}"] + 1)
                        if ib is not None:
                            flip(f"flipQ{ib}", lambda t: XQ[:, t, :], xq_ready, ib + 1)
                            pe.wait_ge(m_taken, M[f"flipQ{ib}"] + 1)
                            for i, n in enumerate("ab"):
                                project(f"qkv{n}{ib}", FQ, QKVT[:, :], width=2 * D, tiles=(2 * i, 2 * i + 1))
                        if tb is not None:
                            flip(f"flipX{tb}", lambda t: XL[:, tb * TPB + t, :], xl_ready, tb + 1)
                    if step == 2:
                        if k + 1 < NA:
                            flip(f"flipP{k + 1}", lambda t: XP[:, t, :], xp_ready, k + 2)
                        if tb is not None:
                            pe.wait_ge(m_taken, M[f"flipX{tb}"] + 1)
                            project(f"router{tb}", FR, RT[:, :], width=E)
                    if step == 3:
                        if 1 <= k <= NA:
                            pe.wait_ge(o_ready, k)
                            project(f"out{k - 1}", OF, SQ[:, 4 * ((k - 1) // B) + 3, :])
                        if k + 1 < NA:
                            queries(k + 1)
                    if mb is not None:
                        for e in UNITS.get(step, ()):
                            if e + 1 < NU:
                                up(mb, e + 1)
                            down(mb, e)
            pe.wait_ge(cb_ready, 1)
            pe.wait_ge(pool_ready, 1)
            cb = CB[:, :, :].rearrange("p t e -> p (t e)")
            mm(M_[:, 0:NT * E], BEFB[:, :], cb[:, NT * E:2 * NT * E], start=True, stop=False)
            for j in range(1, NT):
                ins = mm(M_[:, 0:NT * E], ONEB[:, :], cb[:, (NT - j) * E:(2 * NT - j) * E], start=False, stop=(j == NT - 1))
            ins.then_inc(rank_ready, 1)

            half = CAP // 2
            pe.wait_ge(slots_ready, 1)
            with pe.Fori(0, E // 2) as pair:
                for i in range(2):
                    pe.wait_ge(xe_loaded[i], pair * 16 + 16)
                    pe.wait_ge(xt_ready, pair * 2 + i)
                    for c in range(XT_TILES):
                        ins = nc.tensor.transpose(SBK[c // 4][:, (c % 4) * P:(c % 4 + 1) * P], XE[:, i, c, :], ident)
                    ins.then_inc(xe_flipped, 1)
                    pe.wait_ge(w_loaded[i], pair * 32 + 32)
                    pe.wait_ge(xt_ready, pair * 2 + (i + 1))
                    for q in range(2 * FC):
                        pe.wait_ge(gelu_ready, pair * (4 * FC) + max(2 * FC * i + q - 3, 0))
                        mm([T_, DEN, U_, M_][q % 4][:, 0:half], W1[:, i, (q // 2) * P:(q // 2 + 1) * P],
                           XT[:, i, (q % 2) * half:(q % 2 + 1) * half], start=True, stop=True).then_inc(eup_ready, 1)
                    pe.wait_ge(gelu_ready, pair * (4 * FC) + 2 * FC * (i + 1))
                    pe.wait_ge(ye_ready, pair * 2 + i)
                    for c in range(XT_TILES):
                        dst = Y_[:, c * P:(c + 1) * P] if c < 4 else NUM[:, 0:P]
                        for f in range(FC):
                            ins = mm(dst, GT[i][:, f, c * P:(c + 1) * P], W2[:, i, f, :], start=(f == 0), stop=(f == FC - 1))
                    ins.then_inc(edown_ready, 1)


def kernel(**inputs):
    import numpy as np
    import concourse.bacc as bacc
    from concourse.bass_utils import run_bass_kernel_spmd

    a = {k: np.asarray(v) for k, v in inputs.items()}
    t = np.ascontiguousarray

    zero = np.zeros(D, np.float32)
    consts, at = shape_constants()
    sq = [a["L0_xattn_Wq"].T, a["L0_xattn_Wk"].T, a["L0_xattn_Wv"].T, a["L0_xattn_Wo"].T,
          a["L1_xattn_w_q"].T, a["L1_xattn_w_k"].T, a["L1_xattn_w_v"].T, a["L1_xattn_w_o"].T,
          a["L1_ffn_proj_weight"].T, a["L0_ffn_sh_down_w"]]
    cols = [a["L0_xattn_bq"], a["L0_xattn_bk"], zero, a["L1_ffn_ln1_weight"], a["L1_ffn_ln1_bias"],
            a["L1_ffn_ln2_weight"], a["L1_ffn_ln2_bias"], *a["L0_ffn_up_b"], a["L0_ffn_sh_up_b"]]
    g = [a["g_xattn"][0], a["g_ffn"][0], a["g_xattn"][1], a["g_ffn"][1]]
    arrays = {
        "x": a["x"].reshape(B * S, D),
        "ctx_t": a["ctx_1024"].transpose(2, 0, 1),
        "mask_b": a["mask_Bx1xSxS2_if1"].reshape(B * S, KEYS),
        "mask_1": a["mask_1x1xSxS2_if1"].reshape(S, KEYS),
        "consts": consts,
        "sq": np.stack(sq, 1),
        "gate": a["L0_ffn_gate_w"].T,
        "up_w": np.concatenate([a["L0_ffn_up_w"], a["L0_ffn_sh_up_w"][None]]).transpose(1, 0, 2),
        "down_w": a["L0_ffn_down_w"].transpose(1, 0, 2),
        "cols": np.stack(cols, 1),
        "rows_b": np.broadcast_to(np.stack([a["L0_xattn_bo"], a["L0_xattn_bv"]]), (P, 2, D)),
        "down_rows": np.concatenate([a["L0_ffn_down_b"], a["L0_ffn_sh_down_b"][None]]),
        "gates": np.broadcast_to(np.stack(g), (P, 4)),
        "qkv_t": a["L1_ffn_qkv_weight"].T,
        "router": a["L1_ffn_router_weight"],
        "moe_w1": a["L1_ffn_moe_w1"].transpose(1, 0, 2),
        "moe_w2": a["L1_ffn_moe_w2"].reshape(E, FC, P, D).transpose(2, 0, 1, 3),
    }
    nc = bacc.Bacc("TRN2", target_bir_lowering=False, num_devices=1)
    arrays = {n: t(v) for n, v in arrays.items()}
    args = {n: nc.dram_tensor(n, v.shape, mybir.dt.from_np(v.dtype), kind="ExternalInput").ap() for n, v in arrays.items()}
    out = nc.dram_tensor("out", (B * S, D), mybir.dt.float32, kind="ExternalOutput").ap()
    gated_layers_kernel(nc, at=at, out=out, **args)
    r = run_bass_kernel_spmd(nc, [arrays], core_ids=[0])
    return r.results[0]["out"].reshape(B, S, D)
```

```python
import concourse.bass as bass
from concourse import mybir
from contextlib import ExitStack

B, S, D, P = 4, 512, 128, 128
TPB = S // P
NT = B * TPB
H, DK, KEYS = 16, 8, 77
HK = H * KEYS
HG = 4
NKC = 3
CR = -(-4 * KEYS // NKC)
CSTART = [0, CR, 4 * KEYS - CR]
NCH = HG * NKC
GROUPS = [(0, 6), (6, 6), (12, 4)]
NA = 2 * B
E = 8
CAP = -(-(B * S * 2 * 5) // (E * 4))
XT_TILES = CAP // P
FC = 4
KV = 8
BANK = 512
SCALE = float(DK) ** -0.5
FAR = float(4 * E * CAP)


def shape_constants():
    import numpy as np
    p = np.arange(P)
    d = np.arange(D)
    vmask = np.zeros((P, NKC, D))
    for i, c0 in enumerate(CSTART):
        new = p + c0 >= (CSTART[i - 1] + CR if i else 0)
        vmask[:, i, :] = ((p[:, None] + c0) // KEYS == d // DK % 4) & new[:, None] & (p < CR)[:, None]
    parts = {
        "ident": np.eye(P),
        "hmask": (p[:, None] // DK == np.arange(H)) * SCALE,
        "vmask": vmask.reshape(P, NKC * D),
        "dest": 2 * (P * np.arange(NT)[None, :, None] + p[:, None, None]) + np.arange(2),
        "iota": np.broadcast_to(np.arange(E), (P, E)),
        "before": p[:, None] < p,
        "ones": np.ones((P, P)),
    }
    at, start = {}, 0
    parts["dest"] = parts["dest"].reshape(P, 2 * NT)
    for k, a in parts.items():
        at[k] = (start, start + a.shape[1])
        start += a.shape[1]
    return np.ascontiguousarray(np.concatenate(list(parts.values()), 1).astype(np.float32)), at


def gated_layers_kernel(nc, x, ctx_t, mask_b, mask_1, consts, at, sq, gate, up_w, down_w, cols, rows_b,
                        down_rows, gates, qkv_t, router, moe_w1, moe_w2, out):
    f32, bf16, i32, u32 = mybir.dt.float32, mybir.dt.bfloat16, mybir.dt.int32, mybir.dt.uint32
    ALU, ACT, AX = mybir.AluOpType, mybir.ActivationFunctionType, mybir.AxisListType
    ds = bass.ds

    SLOTS = range(B + 7)
    NU = E + 1
    def chunks_of(k, p):
        if k == NA:
            return [(TPB * NA - 2, 2)] + [(TPB * NA - 1, j) for j in range(3)] if p == 0 else []
        tau, j = divmod(3 * TPB * k + p - 4, 3)
        if tau < 0 or tau >= TPB * NA or p in (4, 5):
            return []
        return [(tau, i) for i in ((0, 1, 2) if p == 6 else (j,))]

    U0 = 3

    def mix(k):
        return k - 2 if 0 <= k - 2 < B else None

    def inner(k):
        return k - 6 if 0 <= k - 6 < B else None

    def tail(k):
        return k - 7 if 0 <= k - 7 < B else None

    def done(k):
        return k - 1 if 1 <= k <= NA else None

    def coming(k):
        return k + 1 if k + 1 < NA else None

    TAKER = dict(flipA="A", flipM="A", proj="V", gate="V", flipQ="A", prep="V", qkva="A", qkvb="A", flipX="A",
                 flipC="A", router="V", flipP="A", rank="V", out="V", q="A")

    def places(k):
        at = dict(flipA=0, flipM=0, proj=1, gate=1, flipQ=2, prep=3, qkva=3, qkvb=4, flipX=4, flipC=7, router=5,
                  flipP=6, rank=6, out=8, q=9,
                  num=4, den=5, zstats=0, xq=1, hidden=1, xl=2, xstats=2, xp=3, attended=6, iscores=6, iexp=7, rin=5,
                  rout=7, resid=8, ivals=9, norm=10)
        if k == 0:
            at.update(prep=5, flipP=5, q=7)
        if k == 1:
            at.update(xp=5, q=7)
        if mix(k) is not None:
            at.update(prep=0, q=10)
        if k == NA - 2:
            at.update(prep=1, iscores=5)
        if k == NA - 1:
            at.update(xl=3, iscores=4, resid=11, norm=11)
        if k == NA:
            at.update(num=1, den=2, attended=3, flipQ=3, qkvb=3, out=5, iscores=5, resid=6, iexp=7, flipX=6,
                      norm=8, router=7, rank=8, rin=8, ivals=7, rout=9)
        if k == NA + 1:
            at.update(flipX=5, router=6, rank=7, iscores=5, iexp=5, rin=6, ivals=7, rout=8)
        return at

    uses = ["prep0", "flipP0", "q0"]
    slot_of = dict.fromkeys(uses, 0)
    for k in SLOTS:
        batch = dict(flipA=tail(k), flipM=mix(k), prep=coming(k), proj=tail(k), gate=mix(k), flipQ=inner(k), qkva=inner(k),
                     qkvb=inner(k), flipX=tail(k), flipC=mix(k), router=tail(k), flipP=coming(k), rank=tail(k), out=done(k),
                     q=coming(k))
        for n in sorted((n for n in batch if batch[n] is not None), key=lambda n: places(k)[n]):
            uses.append(f"{n}{batch[n]}")
            slot_of[uses[-1]] = k
    M, BANK_OF, TAKEN, BEFORE = {}, {}, {}, {}
    taken, last = {"A": 0, "V": 0}, {}
    for i, use in enumerate(uses):
        name = use.rstrip("0123456789")
        ring = 2 if slot_of[use] < 2 else 3
        bank, taker = i % ring, TAKER[name]
        if mix(slot_of[use]) is not None:
            bank = 1 if name == "prep" else 0
        taken[taker] += 1
        M[use], BANK_OF[use], TAKEN[use], BEFORE[use] = i, bank, (taker, taken[taker]), last.get(bank)
        last[bank] = use
    FIRST_Y = [u for u in uses if BANK_OF[u] == 2][0]
    U_BEFORE = [[u for u in uses if BANK_OF[u] == 1 and mix(slot_of[u]) in (None, b) and slot_of[u] <= b + 2][-1] for b in range(B)]
    UNITS_BEFORE = {u: NU * (max(slot_of[u] - 2, 0) if slot_of[u] < 6 else B) for u in uses if BANK_OF[u] == 1}

    ctx = ExitStack()
    with ctx:
        def sb(name, shape, dt=f32):
            return ctx.enter_context(nc.sbuf_tensor(name, shape, dt))

        def sem(name):
            return ctx.enter_context(nc.semaphore(name))

        slot_x = nc.dram_tensor("slot_x", [E * CAP, D + 1], f32, kind="Internal").ap()
        token_y = nc.dram_tensor("token_y", [2 * NT * P, D], f32, kind="Internal").ap()

        X = sb("X", [P, NT, D])
        Z = sb("Z", [P, NT, D])
        QKV = sb("QKV", [P, B, TPB * KV, 4 * DK])
        XL = sb("XL", [P, 2, NT, D + 1])
        CST = sb("CST", [P, consts.shape[1]])
        SQ = sb("SQ", [P, 10, D])
        GATE = sb("GATE", [P, E])
        RT = sb("RT", [P, E])
        UPW = sb("UPW", [P, NU, P])
        DNW = sb("DNW", [P, E, D])
        QKVT = sb("QKVT", [P, 2 * D])
        COLS = sb("COLS", [P, cols.shape[1]])
        ROWS = sb("ROWS", [P, 2, D])
        DB = sb("DB", [E + 1, D])
        TG = sb("TG", [P, 4])
        CTX = sb("CTX", [P, B, KEYS])
        CTX4 = sb("CTX4", [P, B, 4, KEYS])
        KT = sb("KT", [P, KEYS])
        KEXP = sb("KEXP", [P, 2, HK])
        BVM = sb("BVM", [P, NKC, D])
        VX = sb("VX", [P, 3, NKC, D])
        MZB = sb("MZB", [P, NT, KEYS], i32)
        MZ1 = sb("MZ1", [P, TPB, KEYS], i32)
        ANY = sb("ANY", [P, 2])
        ANYI = sb("ANYI", [1, 2], i32)
        NEG = sb("NEG", [P, 2])
        HALF = sb("HALF", [P, TPB])
        BEFB = sb("BEFB", [P, P], bf16)
        ONEB = sb("ONEB", [P, P], bf16)
        ST = sb("ST", [P, 2, TPB, 6])
        MV = sb("MV", [P, 2, TPB, 2])
        VE = sb("VE", [P, 2, TPB])
        RS = sb("RS", [P, 2, TPB])
        XP = sb("XP", [P, TPB, D])
        XM = sb("XM", [P, TPB, D])
        XQ = sb("XQ", [P, TPB, D])
        FP = sb("FP", [P, S])
        FM = sb("FM", [P, S])
        FQ = sb("FQ", [P, S])
        FA = sb("FA", [P, S])
        FR = sb("FR", [P, S])
        OF = sb("OF", [P, S])
        QT = sb("QT", [P, 2, S])
        MX = sb("MX", [P, H])
        PR = sb("PR", [P, 3, HK])
        PT = sb("PT", [P, NCH, S])
        RD = sb("RD", [P, S])
        XR = sb("XR", [P, TPB, D])
        GBO = sb("GBO", [P, D])
        LG = sb("LG", [P, NT, E])
        M8 = sb("M8", [P, NT, E])
        I8 = sb("I8", [P, NT, E], u32)
        IF = sb("IF", [P, NT, 2])
        OH = sb("OH", [P, 2, NT, E])
        LM = sb("LM", [P, TPB, E])
        EX = sb("EX", [P, TPB, E])
        CM = sb("CM", [P, TPB, E + 1])
        CW = sb("CW", [P, TPB, E])
        DN = sb("DN", [P, TPB])
        RC = sb("RC", [P, TPB])
        CMT = sb("CMT", [E + 1, S])
        SL = sb("SL", [P, 2, S])
        YA = sb("YA", [P, TPB, D])
        AO = sb("AO", [P, TPB, D])
        PRD = sb("PRD", [P, B, S])
        XE = sb("XE", [P, 2, XT_TILES, D + 1])
        DEST = sb("DEST", [P, 2, XT_TILES], u32)
        W1 = sb("W1", [P, 2, FC * P])
        W2 = sb("W2", [P, 2, FC, D])
        SC = sb("SC", [P, B, TPB * H])
        SM = sb("SM", [P, TPB * H])
        SR = sb("SR", [P, TPB * H])
        CB = sb("CB", [P, 2 * NT, E], bf16)
        RK = sb("RK", [P, NT, E])
        TK = sb("TK", [P, 2, TPB, E])
        SLT = sb("SLT", [P, 3, 2, TPB])
        KEEP = sb("KEEP", [P, 2, NT])
        DNW1 = sb("DNW1", [P, NT])
        WT = sb("WT", [P, 2, NT])
        SCI = sb("SCI", [P, NT, 2], u32)
        SPARE = sb("SPARE", [P, 4])
        ZERO = sb("ZERO", [P, D + 1])
        pt_flat = PT[:, :, :].rearrange("p a k -> p (a k)")
        GT = [pt_flat[:, i * FC * CAP:(i + 1) * FC * CAP].rearrange("p (f n) -> p f n", f=FC) for i in range(2)]
        XT = KEXP[:, :, :].rearrange("p a k -> p (a k)")[:, 0:2 * CAP].rearrange("p (i n) -> p i n", i=2)
        YS = PRD[:, :, :].rearrange("p t k -> p (t k)")[:, 0:2 * CAP].rearrange("p (i c d) -> p i c d", i=2, d=D)
        GA = QKV[:, :, :, :].rearrange("p s n d -> p (s n d)").rearrange("p (t k d) -> p t k d", t=NT, k=2)

        def const(name, rows=P):
            return CST[0:rows, at[name][0]:at[name][1]]

        ident = const("ident")
        vmask = const("vmask").rearrange("p (i d) -> p i d", i=NKC)
        col = {n: COLS[:, i:i + 1] for i, n in enumerate(
            ["bq0", "bk0", "zero", "ln1w", "ln1b", "ln2w", "ln2b"] + [f"up{e}" for e in range(NU)])}

        S0, S1, T_, NUM, DEN, U_, Y_, M_ = [ctx.enter_context(nc.psum_tensor(n, [P, BANK], f32))
                                            for n in ("S0", "S1", "T", "NUM", "DEN", "U", "Y", "M")]
        SBK = [S0, S1]

        def sems(text):
            return [sem(n) for n in text.split()]

        small_loaded, masks_loaded, att_loaded, x_loaded, rest_loaded, ffn_loaded, w_loaded0, w_loaded1 = sems(
            "small_loaded masks_loaded att_loaded x_loaded rest_loaded ffn_loaded w_loaded0 w_loaded1")
        zero_ready, slots_blank, consts_ready, ctx4_ready, pool_ready, tanh_ready, gbo_ready, dest_ready = sems(
            "zero_ready slots_blank consts_ready ctx4_ready pool_ready tanh_ready gbo_ready dest_ready")
        maskz_ready, any_ready, anysum_ready, anyint_ready, hidden0, hidden1 = sems(
            "maskz_ready any_ready anysum_ready anyint_ready hidden0 hidden1")
        kt_ready, kexp_ready, vx_ready, xr_ready, dve_done, var_ready, rstd_ready = sems(
            "kt_ready kexp_ready vx_ready xr_ready dve_done var_ready rstd_ready")
        xp_ready, xm_ready, xq_ready, xl_ready, xl2_ready, m_ready, act_took, dve_took = sems("xp_ready xm_ready xq_ready xl_ready xl2_ready m_ready act_took dve_took")
        scores_ready, scores_taken, probs_ready, ptrans_ready, pt_ready, pv_ready, o_ready = sems(
            "scores_ready scores_taken probs_ready ptrans_ready pt_ready pv_ready o_ready")
        x_updated, z_ready, exp_in, exp_out, comb_ready, up_ready, silu_ready, down_ready, y_taken = sems(
            "x_updated z_ready exp_in exp_out comb_ready up_ready silu_ready down_ready y_taken")
        in_scores, in_exp, ao_ready, top_in, top_exp, cb_ready, slots_ready, scattered = sems(
            "in_scores in_exp ao_ready top_in top_exp cb_ready slots_ready scattered")
        xe_loaded0, xe_loaded1, xe_flipped, xt_ready, eup_ready, gelu_ready, edown_ready, ye_ready, dests_ready = sems(
            "xe_loaded0 xe_loaded1 xe_flipped xt_ready eup_ready gelu_ready edown_ready ye_ready dests_ready")
        y_out = sems("y_out0 y_out1")
        y_blank, ys_free = sems("y_blank ys_free")
        gathered = sems("gathered0 gathered1 gathered2 gathered3")
        final_ready, out_stored = sems("final_ready out_stored")
        xe_loaded, w_loaded = [xe_loaded0, xe_loaded1], [w_loaded0, w_loaded1]
        def headed(ap, n):
            return ap.rearrange("p (h k) -> p h k", h=n)

        def xs(b):
            return X[:, b * TPB:(b + 1) * TPB, :].rearrange("p t d -> p (t d)")

        def bank(use):
            return [M_, U_, Y_][BANK_OF[use]]

        def took(eng, use):
            taker, n = TAKEN[use]
            eng.wait_ge(act_took if taker == "A" else dve_took, n)

        def wait(eng, semaphore, value):
            if value > 0:
                eng.wait_ge(semaphore, value)

        block = ctx.enter_context(nc.Block())

        @block.sync
        def _(sp):
            sp.dma_start(X[:, 0:TPB, :], x[0:S, :].rearrange("(t p) d -> p t d", p=P)).then_inc(x_loaded, 16)
            sp.dma_start(CST[:, :], consts).then_inc(small_loaded, 16)
            sp.dma_start(CTX[:, :, :], ctx_t).then_inc(small_loaded, 16)
            sp.dma_start(COLS[:, :], cols).then_inc(small_loaded, 16)
            sp.dma_start(ROWS[:, :, :], rows_b).then_inc(small_loaded, 16)
            sp.dma_start(TG[:, :], gates).then_inc(small_loaded, 16)
            sp.dma_start(SQ[:, :, :], sq).then_inc(att_loaded, 16)
            sp.dma_start(MZB[:, :, :], mask_b.rearrange("(t p) k -> p t k", p=P)).then_inc(masks_loaded, 16)
            sp.dma_start(MZ1[:, :, :], mask_1.rearrange("(t p) k -> p t k", p=P)).then_inc(masks_loaded, 16)
            sp.dma_start(X[:, TPB:NT, :], x[S:B * S, :].rearrange("(t p) d -> p t d", p=P)).then_inc(rest_loaded, 16)
            sp.dma_start(GATE[:, :], gate).then_inc(ffn_loaded, 16)
            sp.dma_start(UPW[:, :, :], up_w).then_inc(ffn_loaded, 16)
            sp.dma_start(DNW[:, :, :], down_w).then_inc(ffn_loaded, 16)
            sp.dma_start(DB[:, :], down_rows).then_inc(ffn_loaded, 16)
            sp.dma_start(QKVT[:, :], qkv_t).then_inc(ffn_loaded, 16)
            sp.dma_start(RT[:, :], router).then_inc(ffn_loaded, 16)
            sp.wait_ge(zero_ready, 1)
            sp.dma_start(slot_x.rearrange("(p q) d -> p q d", p=P),
                         ZERO[:, :].unsqueeze(1).broadcast_to([P, E * CAP // P, D + 1])).then_inc(slots_blank, 16)
            half_y = token_y.rearrange("(i p q) d -> i p q d", i=2, p=P)
            for i in range(2):
                sp.dma_start(half_y[i], ZERO[:, 0:D].unsqueeze(1).broadcast_to([P, NT, D])).then_inc(y_blank, 16)
            for i in range(2):
                sp.dma_start(W1[:, i, :], moe_w1[:, i]).then_inc(w_loaded[i], 16)
                sp.dma_start(W2[:, i, :, :], moe_w2[:, i]).then_inc(w_loaded[i], 16)
            sp.wait_ge(scattered, 16 * 2 * NT)
            slots = slot_x.rearrange("(e c p) d -> p e c d", c=XT_TILES, p=P)
            for i in range(2):
                sp.dma_start(XE[:, i, :, :], slots[:, i]).then_inc(xe_loaded[i], 16)
            with sp.Fori(0, E // 2 - 1) as pair:
                for i in range(2):
                    nxt = ds(pair * 2 + (2 + i), 1)
                    sp.wait_ge(xe_flipped, pair * 2 + (i + 1))
                    sp.wait_ge(dests_ready, pair * 2 + (i + 1))
                    sp.dma_start(XE[:, i:i + 1, :, :], slots[:, nxt]).then_inc(xe_loaded[i], 16)
                    sp.wait_ge(edown_ready, pair * 2 + (i + 1))
                    sp.dma_start(W1[:, i:i + 1, :], moe_w1[:, nxt]).then_inc(w_loaded[i], 16)
                    sp.dma_start(W2[:, i:i + 1, :, :], moe_w2[:, nxt]).then_inc(w_loaded[i], 16)
            for i in range(2):
                sp.wait_ge(y_out[i], 16 * XT_TILES * (E // 2))
            for s in range(B):
                sp.dma_start(GA[:, s * TPB:(s + 1) * TPB, :, :],
                             token_y[2 * s * S:2 * (s + 1) * S, :].rearrange("(t p j) d -> p t j d", p=P, j=2)).then_inc(gathered[s], 16)
            for s in range(B):
                sp.wait_ge(final_ready, s + 1)
                sp.dma_start(out[s * S:(s + 1) * S, :].rearrange("(t p) d -> p t d", p=P),
                             X[:, s * TPB:(s + 1) * TPB, :]).then_inc(out_stored, 16)
            sp.wait_ge(out_stored, 16 * B)

        @block.gpsimd
        def _(pool):
            nc.gpsimd.memset(HALF[:, :], -0.5)
            nc.gpsimd.memset(NEG[:, 0:1], -60000.0)
            nc.gpsimd.memset(NEG[:, 1:2], -1e9)
            nc.gpsimd.memset(CM[:, :, E:E + 1], 1.0)
            nc.gpsimd.memset(CB[:, 0:NT, :], 0.0)
            nc.gpsimd.memset(ZERO[:, D:D + 1], FAR)
            nc.gpsimd.memset(ZERO[:, 0:D], 0.0).then_inc(zero_ready, 1)

            norms = [0]

            def rstd():
                n = norms[0]
                norms[0] += 1
                pool.wait_ge(var_ready, n + 1)
                nc.gpsimd.tensor_tensor(RS[:, n % 2, :], VE[:, n % 2, :], HALF[:, :], ALU.pow).then_inc(rstd_ready, 1)

            def keys(k):
                pool.wait_ge(kt_ready, k + 1)
                wait(pool, scores_ready, 3 * TPB * (k - 1))
                nc.gpsimd.tensor_tensor(headed(KEXP[:, k % 2, :], H), KT[:, :].unsqueeze(1).broadcast_to([P, H, KEYS]),
                                        const("hmask").unsqueeze(2).broadcast_to([P, H, KEYS]), ALU.mult).then_inc(kexp_ready, 1)

            def scatter(b, j):
                pool.wait_ge(slots_ready, b + 1)
                if j == 0:
                    pool.wait_ge(xl_ready, b + 1)
                if j == 1:
                    pool.wait_ge(xl2_ready, b + 1)
                for T in range(b * TPB, (b + 1) * TPB):
                    nc.gpsimd.indirect_dma_start(
                        out=slot_x, out_offset=bass.IndirectOffsetOnAxis(ap=SCI[:, T, j:j + 1], axis=0),
                        in_=XL[:, j, T, :], in_offset=None, bounds_check=E * CAP - 1, oob_is_err=False).then_inc(scattered, 16)

            pool.wait_ge(zero_ready, 1)
            rstd()
            pool.wait_ge(small_loaded, 16 * 5)
            for i in range(NKC):
                ins = nc.gpsimd.tensor_tensor(BVM[:, i, :], vmask[:, i, :], ROWS[:, 1, :], ALU.mult)
            ins.then_inc(consts_ready, 1)
            keys(0)
            pool.wait_ge(tanh_ready, 1)
            nc.gpsimd.tensor_scalar(GBO[:, :], ROWS[:, 0, :], TG[:, 0:1], None, ALU.mult).then_inc(gbo_ready, 1)
            nc.gpsimd.tensor_copy(BEFB[:, :], const("before"))
            nc.gpsimd.tensor_copy(ONEB[:, :], const("ones")).then_inc(pool_ready, 1)
            for j in range(2):
                ins = nc.gpsimd.tensor_copy(XL[:, j, :, D], const("dest").rearrange("p (t j) -> p t j", j=2)[:, :, j])
            ins.then_inc(dest_ready, 1)
            pool.wait_ge(dest_ready, 1)
            pool.wait_ge(slots_blank, 16)
            pool.wait_ge(gbo_ready, 1)
            pool.wait_ge(x_loaded, 16)
            pool.wait_ge(rest_loaded, 16)
            for k in SLOTS:
                if inner(k) is not None:
                    rstd()
                if tail(k) == B - 1:
                    scatter(B - 2, 0)
                if tail(k) is not None:
                    rstd()
                    if tail(k):
                        if tail(k) < B - 1:
                            scatter(tail(k) - 1, 0)
                        scatter(tail(k) - 1, 1)
                if coming(k) is not None:
                    rstd()
                    keys(k + 1)
                if 1 <= k <= B:
                    b = k - 1
                    if b:
                        took(pool, f"out{b - 1}")
                    nc.gpsimd.tensor_tensor(XR[:, :, :], X[:, b * TPB:(b + 1) * TPB, :],
                                            GBO[:, :].unsqueeze(1).broadcast_to([P, TPB, D]), ALU.add).then_inc(xr_ready, 1)
                if done(k) is not None:
                    rstd()
            for j in range(2):
                scatter(B - 1, j)
            def passed(c):
                return nc.gpsimd.tensor_tensor(SPARE[:, c:c + 1], HALF[:, 0:1], HALF[:, 0:1], ALU.mult)

            pool.wait_ge(y_blank, 32)
            nc.gpsimd.memset(SPARE[:, :], 0.0).then_inc(ys_free, 2)
            pool.wait_ge(ys_free, 2)
            with pool.Fori(0, E // 2) as pair:
                for i in range(2):
                    pool.wait_ge(xe_loaded[i], pair * 16 + 16)
                    passed(0)
                    nc.gpsimd.tensor_copy(DEST[:, i, :], XE[:, i, :, D]).then_inc(dests_ready, 1)
                    pool.wait_ge(dests_ready, pair * 2 + (i + 1))
                    passed(1)
                    pool.wait_ge(ye_ready, pair * 2 + (i + 2))
                    passed(2)
                    for c in range(XT_TILES):
                        nc.gpsimd.indirect_dma_start(
                            out=token_y, out_offset=bass.IndirectOffsetOnAxis(ap=DEST[:, i, c:c + 1], axis=0),
                            in_=YS[:, i, c, :], in_offset=None, bounds_check=2 * NT * P - 1, oob_is_err=False).then_inc(y_out[i], 16)
                    pool.wait_ge(y_out[i], pair * (16 * XT_TILES) + 16 * XT_TILES)
                    passed(3).then_inc(ys_free, 1)

        @block.scalar
        def _(act):
            act.wait_ge(small_loaded, 16 * 5)
            nc.scalar.activation(TG[:, :], TG[:, :], ACT.Tanh).then_inc(tanh_ready, 1)

            def m_out(use, dst, bias=None, scale=1.0, rows=P):
                act.wait_ge(m_ready, M[use] + 1)
                if bias is None:
                    nc.scalar.activation(dst, bank(use)[0:rows, :], ACT.Copy).then_inc(act_took, 1)
                else:
                    nc.scalar.activation(dst, bank(use)[0:rows, :], ACT.Identity, bias=bias, scale=scale).then_inc(act_took, 1)

            def queries(k):
                wait(act, scores_ready, 3 * TPB * (k - 1))
                m_out(f"q{k}", QT[:, k % 2, :], bias=col["bq0" if k < B else "zero"])

            def chunk(tau, j):
                k, t = tau // TPB, tau % TPB
                wait(act, pv_ready, k)
                act.wait_ge(ptrans_ready, 3 * tau + j + 1)
                nc.scalar.activation(PT[0:CR, 4 * j:4 * j + 4, t * P:(t + 1) * P],
                                     T_[0:CR, :].rearrange("p (c n) -> p c n", c=4), ACT.Copy).then_inc(pt_ready, 1)

            def silu(b, e):
                n = NU * b + e
                act.wait_ge(up_ready, n + 1)
                wait(act, down_ready, n - 1)
                nc.scalar.activation(SL[:, n % 2, :], U_[:, :], ACT.Silu, bias=col[f"up{e}"]).then_inc(silu_ready, 1)

            m_out("flipP0", FP[:, :])
            queries(0)
            for k in SLOTS:
                mb, ib, tb, nb = mix(k), inner(k), tail(k), coming(k)
                at = places(k)
                for p in range(3 * TPB):
                    tau = TPB * k + p // 3
                    if p == at["flipA"] and tb is not None:
                        m_out(f"flipA{tb}", FA[:, :])
                    if p == at["flipM"] and mb is not None:
                        m_out(f"flipM{mb}", FM[:, :])
                    if p == at["flipQ"] and ib is not None:
                        m_out(f"flipQ{ib}", FQ[:, :], bias=col["ln1b"], scale=col["ln1w"])
                    if p == at["qkva"] and ib is not None:
                        m_out(f"qkva{ib}", QKV[:, ib, 0:2 * KV, :].rearrange("p n d -> p (n d)"))
                    if p == at["qkvb"] and ib is not None:
                        m_out(f"qkvb{ib}", QKV[:, ib, 2 * KV:4 * KV, :].rearrange("p n d -> p (n d)"))
                    if p == at["flipX"] and tb is not None:
                        m_out(f"flipX{tb}", FR[:, :], bias=col["ln2b"], scale=col["ln2w"])
                        T = slice(tb * TPB, (tb + 1) * TPB)
                        act.wait_ge(xl_ready, tb + 1)
                        nc.scalar.activation(XL[:, 1, T, 0:D], XL[:, 0, T, 0:D], ACT.Copy).then_inc(xl2_ready, 1)
                    if p == at["flipC"] and mb is not None:
                        m_out(f"flipC{mb}", CMT[:, :], rows=E + 1)
                    if p == at["flipP"] and nb is not None:
                        m_out(f"flipP{nb}", FP[:, :])
                    if p == at["q"] and nb is not None:
                        queries(nb)
                    third = chunks_of(k, p)[:1] if p == 6 else []
                    for c in third:
                        chunk(*c)
                    if mb is not None and p >= U0 - 1 and p + 1 - U0 < NU:
                        silu(mb, p + 1 - U0)
                    for c in chunks_of(k, p)[len(third):]:
                        chunk(*c)
                    if p == at["gate"] and mb is not None:
                        act.wait_ge(exp_in, mb + 1)
                        nc.scalar.activation(EX[:, :, :], EX[:, :, :], ACT.Exp).then_inc(exp_out, 1)
                    if p == at["iexp"] and ib is not None:
                        act.wait_ge(in_scores, ib + 1)
                        nc.scalar.activation(SC[:, 0:ib + 1, :], SC[:, 0:ib + 1, :], ACT.Exp, scale=SCALE).then_inc(in_exp, 1)
                    if p % 3 == 2 and tau < TPB * NA:
                        act.wait_ge(scores_taken, 3 * (tau + 1))
                        nc.scalar.activation(PR[:, tau % 3, :], PR[:, tau % 3, :], ACT.Exp).then_inc(probs_ready, 1)
            act.wait_ge(top_in, 1)
            nc.scalar.activation(WT[:, 1, :], WT[:, 1, :], ACT.Exp).then_inc(top_exp, 1)
            half = CAP // 2
            with act.Fori(0, E // 2) as pair:
                for i in range(2):
                    for q in range(2 * FC):
                        act.wait_ge(eup_ready, pair * (4 * FC) + (i * 2 * FC + q + 1))
                        nc.scalar.activation(GT[i][:, q // 2, (q % 2) * half:(q % 2 + 1) * half],
                                             [T_, DEN, U_, M_][q % 4][:, 0:half], ACT.Gelu).then_inc(gelu_ready, 1)

        @block.vector
        def _(dve):
            links = [0]

            def link(ins):
                links[0] += 1
                ins.then_inc(dve_done, 1)
                dve.wait_ge(dve_done, links[0])

            norms = [0]

            def stats(src):
                n = norms[0] % 2
                for t in range(TPB):
                    ins = nc.vector.bn_stats(ST[:, n, t, :], src(t))
                link(ins)
                for t in range(TPB):
                    ins = nc.vector.bn_aggr(MV[:, n, t, :], ST[:, n, t, :])
                link(ins)
                nc.vector.tensor_scalar(VE[:, n, :], MV[:, n, :, 1], 1e-5, None, ALU.add).then_inc(var_ready, 1)

            def apply(src, dst, done):
                n = norms[0] % 2
                norms[0] += 1
                dve.wait_ge(rstd_ready, norms[0])
                for t in range(TPB):
                    ins = nc.vector.tensor_scalar(dst(t), src(t), MV[:, n, t, 0:1], RS[:, n, t:t + 1], ALU.subtract, ALU.mult)
                ins.then_inc(done, 1)

            def tile_of(buf, b):
                return lambda t: buf[:, b * TPB + t, :]

            def prep(k):
                dve.wait_ge(m_ready, M[f"prep{k}"] + 1)
                wait(dve, kexp_ready, k)
                nc.vector.tensor_scalar(KT[:, :], bank(f"prep{k}")[:, 0:KEYS], col["bk0" if k < B else "zero"], None, ALU.add).then_inc(kt_ready, 1)
                v = VX[0:CR, k % 3, :, :].rearrange("p i d -> p (i d)")
                wait(dve, pv_ready, k - 2)
                ins = nc.vector.tensor_tensor(v, bank(f"prep{k}")[0:CR, P:P + NKC * D], const("vmask", CR), ALU.mult)
                ins.then_inc(dve_took, 1)
                if k < B:
                    took(dve, f"prep{k}")
                    nc.vector.tensor_tensor(v, v, BVM[0:CR, :, :].rearrange("p i d -> p (i d)"), ALU.add).then_inc(vx_ready, 1)

            def groups(tau, g, hidden):
                l, mz = (0, MZB[:, tau, :]) if tau < NT else (1, MZ1[:, tau % TPB, :])
                h0, n = GROUPS[g]
                v = 3 * tau + g
                sc = headed(SBK[v % 2][:, 0:n * KEYS], n)
                dve.wait_ge(scores_ready, v + 1)
                with dve.If_ne(hidden, 0):
                    nc.vector.copy_predicated(sc, mz.unsqueeze(1).broadcast_to([P, n, KEYS]),
                                              NEG[:, l:l + 1].unsqueeze(2).broadcast_to([P, n, KEYS])).then_inc([hidden0, hidden1][l], 1)
                    dve.wait_ge([hidden0, hidden1][l], v % (3 * NT) + 1)
                link(nc.vector.reduce_max(MX[:, h0:h0 + n], sc, AX.X))
                if g == 0:
                    wait(dve, ptrans_ready, 3 * (tau - 2))
                nc.vector.tensor_tensor(headed(PR[:, tau % 3, h0 * KEYS:(h0 + n) * KEYS], n), sc,
                                        MX[:, h0:h0 + n].unsqueeze(2).broadcast_to([P, n, KEYS]),
                                        ALU.subtract).then_inc(scores_taken, 1)

            def attended(k):
                dve.wait_ge(pv_ready, k + 1)
                link(nc.vector.reciprocal(RD[:, :], DEN[:, :]))
                wait(dve, m_ready, M[f"out{k - 1}"] + 1 if k else 0)
                nc.vector.tensor_tensor(OF[:, :], NUM[:, :], RD[:, :], ALU.mult).then_inc(o_ready, 1)

            def residual(k):
                l, b = k // B, k % B
                dve.wait_ge(m_ready, M[f"out{k}"] + 1)
                if l == 0:
                    dve.wait_ge(xr_ready, b + 1)
                rest = XR[:, :, :].rearrange("p t d -> p (t d)") if l == 0 else xs(b)
                nc.vector.scalar_tensor_tensor(out=xs(b), in0=bank(f"out{k}")[:, :], scalar=TG[:, 2 * l:2 * l + 1], in1=rest,
                                               op0=ALU.mult, op1=ALU.add).then_inc(dve_took, 1)
                took(dve, f"out{k}")

            def top2(lg, T0, n):
                for T in range(n):
                    ins = nc.vector.max_index(I8[:, T0 + T, :], M8[:, T0 + T, :], lg[:, T, :])
                link(ins)
                link(nc.vector.tensor_copy(IF[:, T0:T0 + n, :], I8[:, T0:T0 + n, 0:2]))
                for j in range(2):
                    ins = nc.vector.tensor_tensor(OH[:, j, T0:T0 + n, :], const("iota").unsqueeze(1).broadcast_to([P, n, E]),
                                                  IF[:, T0:T0 + n, j:j + 1].broadcast_to([P, n, E]), ALU.is_equal)
                link(ins)

            def gating_in(b):
                dve.wait_ge(m_ready, M[f"gate{b}"] + 1)
                nc.vector.tensor_copy(LM[:, :, :].rearrange("p t e -> p (t e)"), bank(f"gate{b}")[:, 0:TPB * E]).then_inc(dve_took, 1)
                took(dve, f"gate{b}")
                for t in range(TPB):
                    ins = nc.vector.max(M8[:, t, :], LM[:, t, :])
                link(ins)
                nc.vector.tensor_tensor(EX[:, :, :], LM[:, :, :], M8[:, 0:TPB, 0:1].broadcast_to([P, TPB, E]),
                                        ALU.subtract).then_inc(exp_in, 1)

            def gating_out(b):
                dve.wait_ge(exp_out, b + 1)
                link(nc.vector.tensor_tensor(CW[:, :, :], EX[:, :, :], OH[:, 0, 0:TPB, :], ALU.mult))
                link(nc.vector.reduce_sum(DN[:, :], CW[:, :, :], AX.X))
                link(nc.vector.tensor_scalar(DN[:, :], DN[:, :], 1e-20, None, ALU.add))
                link(nc.vector.reciprocal(RC[:, :], DN[:, :]))
                nc.vector.tensor_tensor(CM[:, :, 0:E], CW[:, :, :], RC[:, :].unsqueeze(2).broadcast_to([P, TPB, E]), ALU.mult).then_inc(comb_ready, 1)
                dve.wait_ge(comb_ready, b + 1)

            def unit(b, e):
                n = NU * b + e
                dve.wait_ge(down_ready, n + 1)
                wait(dve, y_taken, n)
                ya = YA[:, :, :].rearrange("p t d -> p (t d)")
                if e == E:
                    ins = nc.vector.tensor_tensor(ya, Y_[:, :], ya, ALU.add)
                for t in range(TPB if e < E else 0):
                    y, w = Y_[:, t * P:(t + 1) * P], CM[:, t, e:e + 1]
                    if e == 0:
                        ins = nc.vector.tensor_scalar(YA[:, t, :], y, w, None, ALU.mult)
                    else:
                        ins = nc.vector.scalar_tensor_tensor(out=YA[:, t, :], in0=y, scalar=w, in1=YA[:, t, :], op0=ALU.mult, op1=ALU.add)
                ins.then_inc(y_taken, 1)

            def mixed(b):
                dve.wait_ge(y_taken, NU * (b + 1))
                nc.vector.scalar_tensor_tensor(out=xs(b), in0=YA[:, :, :].rearrange("p t d -> p (t d)"), scalar=TG[:, 1:2],
                                               in1=xs(b), op0=ALU.mult, op1=ALU.add).then_inc(x_updated, 1)
                dve.wait_ge(x_updated, b + 1)

            def by_head(ap):
                return ap.rearrange("p (n j d) -> p n j d", j=2, d=DK)

            def kv_of(t, which):
                return QKV[:, t, :, (2 + which) * DK:(3 + which) * DK].unsqueeze(2).broadcast_to([P, TPB * KV, 2, DK])

            def inner_scores(s):
                took(dve, f"qkvb{s}")
                q = QKV[:, s, :, 0:2 * DK].rearrange("p n (j d) -> p n j d", j=2)
                for t in range(s + 1):
                    ins = nc.vector.tensor_tensor(by_head(PRD[:, t, :]), q, kv_of(t, 0), ALU.mult)
                link(ins)
                link(nc.vector.reduce_sum(SC[:, 0:s + 1, :], PRD[:, 0:s + 1, :].rearrange("p t (n d) -> p t n d", d=DK), AX.X))
                link(nc.vector.reduce_max(SM[:, :], SC[:, 0:s + 1, :].rearrange("p t n -> p n t"), AX.X))
                nc.vector.tensor_tensor(SC[:, 0:s + 1, :], SC[:, 0:s + 1, :], SM[:, :].unsqueeze(1).broadcast_to([P, s + 1, TPB * H]),
                                        ALU.subtract).then_inc(in_scores, 1)

            def inner_values(s):
                dve.wait_ge(in_exp, s + 1)
                link(nc.vector.reduce_sum(SM[:, :], SC[:, 0:s + 1, :].rearrange("p t n -> p n t"), AX.X))
                link(nc.vector.reciprocal(SR[:, :], SM[:, :]))
                link(nc.vector.tensor_tensor(SC[:, 0:s + 1, :], SC[:, 0:s + 1, :], SR[:, :].unsqueeze(1).broadcast_to([P, s + 1, TPB * H]), ALU.mult))
                ao = AO[:, :, :].rearrange("p t d -> p (t d)")
                if s:
                    dve.wait_ge(m_ready, M[f"flipA{s - 1}"] + 1)
                for t in range(s + 1):
                    dst = ao if t == 0 else PRD[:, t, :]
                    w = SC[:, t, :].rearrange("p (n j) -> p n j", j=2).unsqueeze(3).broadcast_to([P, TPB * KV, 2, DK])
                    ins = nc.vector.tensor_tensor(by_head(dst), w, kv_of(t, 1), ALU.mult)
                for t in range(1, s + 1):
                    link(ins)
                    ins = nc.vector.tensor_tensor(ao, ao, PRD[:, t, :], ALU.add)
                ins.then_inc(ao_ready, 1)
                dve.wait_ge(ao_ready, s + 1)

            def routing_in(b):
                T0 = b * TPB
                dve.wait_ge(m_ready, M[f"router{b}"] + 1)
                nc.vector.tensor_copy(LG[:, T0:T0 + TPB, :].rearrange("p t e -> p (t e)"), bank(f"router{b}")[:, 0:TPB * E]).then_inc(dve_took, 1)
                took(dve, f"router{b}")
                for T in range(T0, T0 + TPB):
                    ins = nc.vector.max(M8[:, T, :], LG[:, T, :])
                link(ins)
                top2(LG[:, T0:T0 + TPB, :], T0, TPB)
                nc.vector.tensor_tensor(CB[:, NT + T0:NT + T0 + TPB, :], OH[:, 0, T0:T0 + TPB, :], OH[:, 1, T0:T0 + TPB, :],
                                        ALU.add).then_inc(cb_ready, 1)

            def routing_out(b):
                T = slice(b * TPB, (b + 1) * TPB)
                rank, slot, far = (SLT[:, i, :, :] for i in range(3))
                dve.wait_ge(m_ready, M[f"rank{b}"] + 1)
                nc.vector.tensor_copy(RK[:, T, :].rearrange("p t e -> p (t e)"), bank(f"rank{b}")[:, 0:TPB * E]).then_inc(dve_took, 1)
                took(dve, f"rank{b}")
                link(nc.vector.tensor_tensor(TK[:, :, :, :], RK[:, T, :].unsqueeze(1).broadcast_to([P, 2, TPB, E]), OH[:, :, T, :], ALU.mult))
                link(nc.vector.reduce_sum(rank, TK[:, :, :, :], AX.X))
                link(nc.vector.tensor_scalar(KEEP[:, :, T], rank, float(CAP), None, ALU.is_lt))
                nc.vector.scalar_tensor_tensor(out=slot, in0=IF[:, T, :].rearrange("p t j -> p j t"), scalar=float(CAP), in1=rank,
                                               op0=ALU.mult, op1=ALU.add)
                link(nc.vector.tensor_scalar(far, KEEP[:, :, T], -FAR, FAR, ALU.mult, ALU.add))
                nc.vector.tensor_tensor(SCI[:, T, :].rearrange("p t j -> p j t"), far, slot, ALU.add).then_inc(slots_ready, 1)

            def flipped(use):
                if use in M:
                    dve.wait_ge(m_ready, M[use] + 1)

            dve.wait_ge(x_loaded, 16)
            stats(tile_of(X, 0))
            dve.wait_ge(small_loaded, 16 * 5)
            nc.vector.tensor_copy(CTX4[:, :, :, :], CTX[:, :, :].unsqueeze(2).broadcast_to([P, B, 4, KEYS])).then_inc(ctx4_ready, 1)
            apply(tile_of(X, 0), lambda t: XP[:, t, :], xp_ready)
            dve.wait_ge(consts_ready, 1)
            prep(0)
            dve.wait_ge(masks_loaded, 32)
            nc.vector.tensor_scalar(MZB[:, :, :], MZB[:, :, :], 0.0, None, ALU.is_equal)
            nc.vector.tensor_scalar(MZ1[:, :, :], MZ1[:, :, :], 0.0, None, ALU.is_equal).then_inc(maskz_ready, 1)
            dve.wait_ge(maskz_ready, 1)
            nc.vector.reduce_sum(ANY[:, 0:1], MZB[:, :, :].rearrange("p t k -> p (t k)"), AX.X)
            nc.vector.reduce_sum(ANY[:, 1:2], MZ1[:, :, :].rearrange("p t k -> p (t k)"), AX.X).then_inc(any_ready, 1)
            dve.wait_ge(anysum_ready, 1)
            nc.vector.tensor_copy(ANYI[:, :], Y_[0:1, 0:2]).then_inc(anyint_ready, 1)
            dve.wait_ge(anyint_ready, 1)
            hidden = [dve.alloc_register(f"hidden{l}") for l in range(2)]
            for l in range(2):
                dve.reg_load(hidden[l], ANYI[0:1, l:l + 1])
            dve.wait_ge(rest_loaded, 16)
            for k in SLOTS:
                mb, ib, tb, ab, nb = mix(k), inner(k), tail(k), done(k), coming(k)
                at = places(k)
                for p in range(3 * TPB):
                    if mb is not None and p > U0:
                        unit(mb, p - 1 - U0)
                    if k < NA:
                        groups(TPB * k + p // 3, p % 3, hidden[k // B])
                    if p == at["zstats"] and ib is not None:
                        stats(tile_of(Z, ib))
                    if p == at["xq"] and ib is not None:
                        flipped(f"flipQ{ib - 1}")
                        apply(tile_of(Z, ib), lambda t: XQ[:, t, :], xq_ready)
                    if p == at["hidden"] and tb is not None:
                        zs = Z[:, tb * TPB:(tb + 1) * TPB, :].rearrange("p t d -> p (t d)")
                        dve.wait_ge(m_ready, M[f"proj{tb}"] + 1)
                        nc.vector.tensor_tensor(zs, bank(f"proj{tb}")[:, :], zs, ALU.add).then_inc(dve_took, 1)
                        took(dve, f"proj{tb}")
                        stats(tile_of(Z, tb))
                    if p == at["gate"] and mb is not None:
                        gating_in(mb)
                    if p == at["gate"] + 1 and mb is not None:
                        top2(LM, 0, TPB)
                        link(nc.vector.tensor_tensor(OH[:, 0, 0:TPB, :], OH[:, 0, 0:TPB, :], OH[:, 1, 0:TPB, :], ALU.add))
                    if p == at["xl"] and tb is not None:
                        if tb == 0:
                            dve.wait_ge(dest_ready, 1)
                        apply(tile_of(Z, tb), lambda t: XL[:, 0, tb * TPB + t, 0:D], xl_ready)
                    if p == at["xstats"] and nb is not None:
                        stats(tile_of(X, nb % B))
                    if p == at["gate"] + 2 and mb is not None:
                        gating_out(mb)
                    if p == at["prep"] and nb is not None:
                        prep(nb)
                    if p == at["xp"] and nb is not None:
                        flipped(f"flipP{k}")
                        apply(tile_of(X, nb % B), lambda t: XP[:, t, :], xp_ready)
                    if p == at["rin"] and tb is not None:
                        routing_in(tb)
                    if p == at["attended"] and ab is not None:
                        attended(ab)
                    if p == at["iscores"] and ib is not None:
                        inner_scores(ib)
                    if p == at["rout"] and tb is not None:
                        routing_out(tb)
                    if p == at["resid"] and ab is not None:
                        residual(ab)
                        stats(tile_of(X, ab % B))
                    if p == at["ivals"] and ib is not None:
                        inner_values(ib)
                    if p == at["norm"] and ab is not None:
                        b = ab % B
                        if ab < B:
                            flipped(f"flipM{b - 1}")
                            apply(tile_of(X, b), lambda t: XM[:, t, :], xm_ready)
                        else:
                            apply(tile_of(X, b), tile_of(Z, b), z_ready)
                            dve.wait_ge(z_ready, b + 1)
                if mb is not None:
                    unit(mb, NU - 1)
                    mixed(mb)

            nc.vector.tensor_tensor(WT[:, 1, :], M8[:, :, 1], M8[:, :, 0], ALU.subtract).then_inc(top_in, 1)
            dve.wait_ge(top_exp, 1)
            link(nc.vector.tensor_scalar(DNW1[:, :], WT[:, 1, :], 1.0, None, ALU.add))
            link(nc.vector.reciprocal(WT[:, 0, :], DNW1[:, :]))
            link(nc.vector.tensor_tensor(WT[:, 1, :], WT[:, 1, :], WT[:, 0, :], ALU.mult))
            link(nc.vector.scalar_tensor_tensor(out=WT[:, :, :], in0=KEEP[:, :, :], scalar=TG[:, 3:4], in1=WT[:, :, :],
                                                op0=ALU.mult, op1=ALU.mult))
            for s in range(B):
                zs = Z[:, s * TPB:(s + 1) * TPB, :].rearrange("p t d -> p (t d)")
                ins = nc.vector.scalar_tensor_tensor(out=xs(s), in0=zs, scalar=TG[:, 3:4], in1=xs(s), op0=ALU.mult, op1=ALU.add)
            ins.then_inc(ye_ready, 1)
            dve.wait_ge(ye_ready, 1)

            def inputs(i, flips):
                dve.wait_ge(xe_flipped, flips)
                nc.vector.tensor_scalar(XT[:, i, 0:BANK], S0[:, :], col["ln2w"], col["ln2b"], ALU.mult, ALU.add)
                nc.vector.tensor_scalar(XT[:, i, BANK:CAP], S1[:, 0:CAP - BANK], col["ln2w"], col["ln2b"],
                                        ALU.mult, ALU.add).then_inc(xt_ready, 1)

            def outputs(i, downs):
                dve.wait_ge(edown_ready, downs)
                dve.wait_ge(ys_free, downs)
                ys = YS[:, i, :, :].rearrange("p c d -> p (c d)")
                nc.vector.tensor_copy(ys[:, 0:BANK], Y_[:, :])
                nc.vector.tensor_copy(ys[:, BANK:CAP], NUM[:, 0:CAP - BANK]).then_inc(ye_ready, 1)

            inputs(0, 1)
            with dve.Fori(0, E // 2 - 1) as pair:
                for i in range(2):
                    inputs(1 - i, pair * 2 + (i + 2))
                    outputs(i, pair * 2 + (i + 1))
            inputs(1, E)
            for i in range(2):
                outputs(i, E - 1 + i)
            for s in range(B):
                dve.wait_ge(gathered[s], 16)
                for j in range(2):
                    for T in range(s * TPB, (s + 1) * TPB):
                        ins = nc.vector.scalar_tensor_tensor(out=X[:, T, :], in0=GA[:, T, j, :], scalar=WT[:, j, T:T + 1], in1=X[:, T, :],
                                                             op0=ALU.mult, op1=ALU.add)
                    if j == 0:
                        link(ins)
                ins.then_inc(final_ready, 1)

        @block.tensor
        def _(pe):
            mm = nc.tensor.matmul

            def free(use):
                if BEFORE[use] is not None:
                    took(pe, BEFORE[use])
                if use == FIRST_Y:
                    pe.wait_ge(y_taken, NU * B)
                wait(pe, silu_ready, UNITS_BEFORE.get(use, 0))

            def flip(use, src, src_ready, value):
                pe.wait_ge(src_ready, value)
                free(use)
                for t in range(TPB):
                    tile = src(t)
                    ins = nc.tensor.transpose(bank(use)[0:tile.shape[1], t * P:(t + 1) * P], tile, ident)
                ins.then_inc(m_ready, 1)

            def project(use, src, w, width=D, tiles=range(TPB)):
                free(use)
                for i, t in enumerate(tiles):
                    ins = mm(bank(use)[:, i * width:(i + 1) * width], src[:, t * P:(t + 1) * P], w, start=True, stop=True)
                ins.then_inc(m_ready, 1)

            def prep(k):
                l, b = k // B, k % B
                free(f"prep{k}")
                mm(bank(f"prep{k}")[:, 0:KEYS], SQ[:, 4 * l + 1, :], CTX[:, b, :], start=True, stop=True)
                if k == 0:
                    pe.wait_ge(ctx4_ready, 1)
                ctx4 = CTX4[:, b, :, :].rearrange("p h k -> p (h k)")
                for i, c0 in enumerate(CSTART):
                    ins = mm(bank(f"prep{k}")[0:CR, P + i * D:P + (i + 1) * D], ctx4[:, c0:c0 + CR],
                             SQ[:, 4 * l + 2, :], start=True, stop=True)
                ins.then_inc(m_ready, 1)

            def queries(k):
                took(pe, f"flipP{k}")
                free(f"q{k}")
                mm(bank(f"q{k}")[:, :], SQ[:, 4 * (k // B), :], FP[:, :], start=True, stop=True).then_inc(m_ready, 1)

            def scores(tau, g):
                k, t = tau // TPB, tau % TPB
                h0, n = GROUPS[g]
                v = 3 * tau + g
                if t == 0 and g == 0:
                    pe.wait_ge(kexp_ready, k + 1)
                    took(pe, f"q{k}")
                wait(pe, scores_taken, v - 1)
                mm(SBK[v % 2][:, 0:n * KEYS], QT[:, k % 2, t * P:(t + 1) * P], KEXP[:, k % 2, h0 * KEYS:(h0 + n) * KEYS],
                   start=True, stop=True).then_inc(scores_ready, 1)

            def chunks(tau, j):
                w = 3 * tau + j
                if j == 0:
                    pe.wait_ge(probs_ready, tau + 1)
                wait(pe, pt_ready, w)
                for c in range(4 * j, 4 * j + 4):
                    c0 = c // NKC * 4 * KEYS + CSTART[c % NKC]
                    ins = nc.tensor.transpose(T_[0:CR, (c % 4) * P:(c % 4 + 1) * P],
                                              PR[:, tau % 3, c0:c0 + CR], ident)
                ins.then_inc(ptrans_ready, 1)

            def values(k, bank):
                if bank is NUM:
                    pe.wait_ge(pt_ready, 3 * TPB * (k + 1))
                    if k < B:
                        pe.wait_ge(vx_ready, k + 1)
                    else:
                        took(pe, f"prep{k}")
                    wait(pe, o_ready, k)
                for i in range(NKC):
                    for hg in range(HG):
                        w = VX[0:CR, k % 3, i, 32 * hg:32 * hg + 32] if bank is NUM else vmask[0:CR, i, 0:32]
                        ins = mm(bank[32 * hg:32 * hg + 32, :], w, PT[0:CR, hg * NKC + i, :],
                                 start=(i == 0), stop=(i == NKC - 1), tile_position=(0, 32 * hg))
                if bank is DEN:
                    ins.then_inc(pv_ready, 1)

            def ranks(b):
                pe.wait_ge(cb_ready, b + 1)
                if b == 0:
                    pe.wait_ge(pool_ready, 1)
                free(f"rank{b}")
                cb = CB[:, :, :].rearrange("p t e -> p (t e)")
                c0, n = (NT + b * TPB) * E, TPB * E
                mm(bank(f"rank{b}")[:, 0:n], BEFB[:, :], cb[:, c0:c0 + n], start=True, stop=False)
                last = (b + 1) * TPB - 1
                for j in range(1, last + 1):
                    ins = mm(bank(f"rank{b}")[:, 0:n], ONEB[:, :], cb[:, c0 - j * E:c0 - j * E + n], start=False, stop=(j == last))
                ins.then_inc(m_ready, 1)

            def up(b, e):
                n = NU * b + e
                wait(pe, silu_ready, n)
                if e == 0:
                    took(pe, U_BEFORE[b])
                mm(U_[:, :], UPW[:, e, :], FM[:, :], start=True, stop=True).then_inc(up_ready, 1)

            def down(b, e):
                n = NU * b + e
                pe.wait_ge(silu_ready, n + 1)
                wait(pe, y_taken, n)
                h, w = SL[:, n % 2, :], (SQ[:, 9, :] if e == E else DNW[:, e, :])
                for t in range(TPB):
                    ins = mm(Y_[:, t * P:(t + 1) * P], h[:, t * P:(t + 1) * P], w, start=True, stop=(e < E))
                    if e == E:
                        ins = mm(Y_[:, t * P:(t + 1) * P], CMT[:, t * P:(t + 1) * P], DB[:, :], start=False, stop=True)
                ins.then_inc(down_ready, 1)

            pe.wait_ge(small_loaded, 16 * 5)
            pe.wait_ge(att_loaded, 16)
            prep(0)
            flip("flipP0", lambda t: XP[:, t, :], xp_ready, 1)
            queries(0)
            pe.wait_ge(any_ready, 1)
            mm(Y_[0:1, 0:2], const("ones")[:, 0:1], ANY[:, :], start=True, stop=True).then_inc(anysum_ready, 1)
            scores(0, 0)
            for k in SLOTS:
                mb, ib, tb, ab, nb = mix(k), inner(k), tail(k), done(k), coming(k)
                at = places(k)
                if mb == 0:
                    pe.wait_ge(ffn_loaded, 16 * 6)
                for p in range(3 * TPB):
                    v = 3 * TPB * k + p
                    if p == at["flipA"] and tb is not None:
                        flip(f"flipA{tb}", lambda t: AO[:, t, :], ao_ready, tb + 1)
                    if p == at["flipM"] and mb is not None:
                        flip(f"flipM{mb}", lambda t: XM[:, t, :], xm_ready, mb + 1)
                    if p == at["prep"] and nb is not None:
                        prep(nb)
                    if p == at["proj"] and tb is not None:
                        took(pe, f"flipA{tb}")
                        project(f"proj{tb}", FA, SQ[:, 8, :])
                    if p == at["gate"] and mb is not None:
                        took(pe, f"flipM{mb}")
                        project(f"gate{mb}", FM, GATE[:, :], width=E)
                    if p == at["flipQ"] and ib is not None:
                        flip(f"flipQ{ib}", lambda t: XQ[:, t, :], xq_ready, ib + 1)
                    if p == at["qkva"] and ib is not None:
                        took(pe, f"flipQ{ib}")
                        project(f"qkva{ib}", FQ, QKVT[:, :], width=2 * D, tiles=(0, 1))
                    if p == at["qkvb"] and ib is not None:
                        project(f"qkvb{ib}", FQ, QKVT[:, :], width=2 * D, tiles=(2, 3))
                    if p == at["flipX"] and tb is not None:
                        flip(f"flipX{tb}", lambda t: XL[:, 0, tb * TPB + t, 0:D], xl_ready, tb + 1)
                    if p == at["flipC"] and mb is not None:
                        flip(f"flipC{mb}", lambda t: CM[:, t, :], comb_ready, mb + 1)
                    if p == at["router"] and tb is not None:
                        took(pe, f"flipX{tb}")
                        project(f"router{tb}", FR, RT[:, :], width=E)
                    if p == at["flipP"] and nb is not None:
                        flip(f"flipP{nb}", lambda t: XP[:, t, :], xp_ready, nb + 1)
                    if p == at["rank"] and tb is not None:
                        ranks(tb)
                    if p == at["out"] and ab is not None:
                        pe.wait_ge(o_ready, ab + 1)
                        project(f"out{ab}", OF, SQ[:, 4 * (ab // B) + 3, :])
                    if p == at["q"] and nb is not None:
                        queries(nb)
                    third = chunks_of(k, p) if p == 6 else []
                    for c in third[:1]:
                        chunks(*c)
                    if v + 1 < 3 * TPB * NA:
                        scores((v + 1) // 3, (v + 1) % 3)
                    e = p - U0
                    if mb is not None and -1 <= e < NU - 1:
                        up(mb, e + 1)
                    for c in third[1:2]:
                        chunks(*c)
                    if mb is not None and 0 <= e < NU:
                        down(mb, e)
                    if p == at["num"] and ab is not None:
                        values(ab, NUM)
                    if p == at["den"] and ab is not None:
                        values(ab, DEN)
                    for c in third[2:] or chunks_of(k, p):
                        chunks(*c)

            half = CAP // 2

            def flips(i, loads, e):
                pe.wait_ge(xe_loaded[i], loads * 16)
                pe.wait_ge(xt_ready, e)
                for c in range(XT_TILES):
                    ins = nc.tensor.transpose(SBK[c // 4][:, (c % 4) * P:(c % 4 + 1) * P], XE[:, i, c, 0:D], ident)
                ins.then_inc(xe_flipped, 1)

            def hidden(i, loads, e, gelus):
                pe.wait_ge(w_loaded[i], loads * 32)
                pe.wait_ge(xt_ready, e + 1)
                for q in range(2 * FC):
                    if gelus is not None or q > 3:
                        pe.wait_ge(gelu_ready, (gelus if gelus is not None else 0) + (q - 3))
                    mm([T_, DEN, U_, M_][q % 4][:, 0:half], W1[:, i, (q // 2) * P:(q // 2 + 1) * P],
                       XT[:, i, (q % 2) * half:(q % 2 + 1) * half], start=True, stop=True).then_inc(eup_ready, 1)

            def output(i, e, gelus):
                pe.wait_ge(gelu_ready, gelus)
                pe.wait_ge(ye_ready, e + 1)
                for c in range(XT_TILES):
                    dst = Y_[:, c * P:(c + 1) * P] if c < 4 else NUM[:, 0:P]
                    for f in range(FC):
                        ins = mm(dst, GT[i][:, f, c * P:(c + 1) * P], W2[:, i, f, :], start=(f == 0), stop=(f == FC - 1))
                ins.then_inc(edown_ready, 1)

            pe.wait_ge(xe_loaded[0], 16)
            for c in range(XT_TILES):
                ins = nc.tensor.transpose(SBK[c // 4][:, (c % 4) * P:(c % 4 + 1) * P], XE[:, 0, c, 0:D], ident)
            ins.then_inc(xe_flipped, 1)
            hidden(0, 1, 0, None)
            with pe.Fori(0, E // 2 - 1) as pair:
                for i in range(2):
                    done_before = pair * (4 * FC) + 2 * FC * (i + 1)
                    flips(1 - i, pair + (1 + i), pair * 2 + (i + 1))
                    output(i, pair * 2 + i, done_before)
                    hidden(1 - i, pair + (1 + i), pair * 2 + (i + 1), done_before)
            flips(1, E // 2, E - 1)
            output(0, E - 2, 2 * FC * (E - 1))
            hidden(1, E // 2, E - 1, 2 * FC * (E - 1))
            output(1, E - 1, 2 * FC * E)


def kernel(**inputs):
    import numpy as np
    import concourse.bacc as bacc
    from concourse.bass_utils import run_bass_kernel_spmd

    a = {k: np.asarray(v) for k, v in inputs.items()}
    t = np.ascontiguousarray

    zero = np.zeros(D, np.float32)
    consts, at = shape_constants()
    sq = [a["L0_xattn_Wq"].T, a["L0_xattn_Wk"].T, a["L0_xattn_Wv"].T, a["L0_xattn_Wo"].T,
          a["L1_xattn_w_q"].T, a["L1_xattn_w_k"].T, a["L1_xattn_w_v"].T, a["L1_xattn_w_o"].T,
          a["L1_ffn_proj_weight"].T, a["L0_ffn_sh_down_w"]]
    cols = [a["L0_xattn_bq"], a["L0_xattn_bk"], zero, a["L1_ffn_ln1_weight"], a["L1_ffn_ln1_bias"],
            a["L1_ffn_ln2_weight"], a["L1_ffn_ln2_bias"], *a["L0_ffn_up_b"], a["L0_ffn_sh_up_b"]]
    g = [a["g_xattn"][0], a["g_ffn"][0], a["g_xattn"][1], a["g_ffn"][1]]
    arrays = {
        "x": a["x"].reshape(B * S, D),
        "ctx_t": a["ctx_1024"].transpose(2, 0, 1),
        "mask_b": a["mask_Bx1xSxS2_if1"].reshape(B * S, KEYS),
        "mask_1": a["mask_1x1xSxS2_if1"].reshape(S, KEYS),
        "consts": consts,
        "sq": np.stack(sq, 1),
        "gate": a["L0_ffn_gate_w"].T,
        "up_w": np.concatenate([a["L0_ffn_up_w"], a["L0_ffn_sh_up_w"][None]]).transpose(1, 0, 2),
        "down_w": a["L0_ffn_down_w"].transpose(1, 0, 2),
        "cols": np.stack(cols, 1),
        "rows_b": np.broadcast_to(np.stack([a["L0_xattn_bo"], a["L0_xattn_bv"]]), (P, 2, D)),
        "down_rows": np.concatenate([a["L0_ffn_down_b"], a["L0_ffn_sh_down_b"][None]]),
        "gates": np.broadcast_to(np.stack(g), (P, 4)),
        "qkv_t": a["L1_ffn_qkv_weight"].T,
        "router": a["L1_ffn_router_weight"],
        "moe_w1": a["L1_ffn_moe_w1"].transpose(1, 0, 2),
        "moe_w2": a["L1_ffn_moe_w2"].reshape(E, FC, P, D).transpose(2, 0, 1, 3),
    }
    nc = bacc.Bacc("TRN2", target_bir_lowering=False, num_devices=1)
    arrays = {n: t(v) for n, v in arrays.items()}
    args = {n: nc.dram_tensor(n, v.shape, mybir.dt.from_np(v.dtype), kind="ExternalInput").ap() for n, v in arrays.items()}
    out = nc.dram_tensor("out", (B * S, D), mybir.dt.float32, kind="ExternalOutput").ap()
    gated_layers_kernel(nc, at=at, out=out, **args)
    r = run_bass_kernel_spmd(nc, [arrays], core_ids=[0])
    return r.results[0]["out"].reshape(B, S, D)
```
